# Optimizing a Trainium2 kernel written in Bass

```python
import numpy as np
import jax
import jax.numpy as jnp

def _softmax(x, axis=-1):
    return jax.nn.softmax(x, axis=axis)

def _gelu(x):
    return jax.nn.gelu(x, approximate=True)

def _silu(x):
    return jax.nn.silu(x)

def _sigmoid(x):
    return jax.nn.sigmoid(x)

def _layernorm(x, axis=-1, eps=1e-05):
    m = jnp.mean(x, axis=axis, keepdims=True)
    v = jnp.var(x, axis=axis, keepdims=True)
    return (x - m) / jnp.sqrt(v + eps)

def _scatter_add(tgt, idx, src, axis=0):
    return tgt.at[idx].add(src)

def _segment_sum(src, seg, n):
    return jax.ops.segment_sum(src, seg, n)
kernel_name = 'mk_seq_preln_d4_jaxref_r8_4b73c6'

def setup_inputs(seed: int=0):
    np.random.seed(seed)
    _w = jnp.asarray

    def _L0_attn_setup():
        import jax, jax.numpy as jnp
        import numpy as np
        B, S, D, H, N = (8, 256, 128, 4, 8)
        TAU = 1.0
        SINKHORN_ITERS = 5
        LN_EPS = 1e-05

        def _sinkhorn(log_alpha):
            for _ in range(SINKHORN_ITERS):
                log_alpha = log_alpha - jax.nn.logsumexp(log_alpha, axis=-1, keepdims=True)
                log_alpha = log_alpha - jax.nn.logsumexp(log_alpha, axis=-2, keepdims=True)
            return jnp.exp(log_alpha)

        def _greedy_hard_one(soft):
            n = soft.shape[-1]
            order = jnp.argsort(-soft.max(axis=-1))

            def body(i, carry):
                avail, hard = carry
                r = order[i]
                scores = jnp.where(avail, soft[r], -jnp.inf)
                c = jnp.argmax(scores)
                return (avail.at[c].set(False), hard.at[r, c].set(1.0))
            avail0 = jnp.ones((n,), dtype=bool)
            hard0 = jnp.zeros_like(soft)
            _, hard = jax.lax.fori_loop(0, n, body, (avail0, hard0))
            return hard

        def _forward(x, ln_w, ln_b, sign_W, sign_b, perm_W, perm_b, gate_W, gate_b, in_W, in_b, out_W, out_b):
            b, s, d = x.shape
            residual = x
            mu = x.mean(axis=-1, keepdims=True)
            var = x.var(axis=-1, keepdims=True)
            xn = (x - mu) / jnp.sqrt(var + LN_EPS) * ln_w + ln_b
            signs = 2.0 * jax.nn.sigmoid((xn @ sign_W + sign_b).reshape(b, s, H, N)) - 1.0
            perm_logits = (xn @ perm_W + perm_b).reshape(b, s, H, N, N) / TAU
            gamma = jax.nn.sigmoid((xn @ gate_W + gate_b).reshape(b, s, H, N))
            b_in = (xn @ in_W + in_b).reshape(b, s, H, N)
            soft = _sinkhorn(perm_logits)
            soft_sg = jax.lax.stop_gradient(soft)
            hard = jax.vmap(_greedy_hard_one)(soft_sg.reshape(-1, N, N)).reshape(soft.shape)
            P = hard + soft - soft_sg
            xs = (jnp.moveaxis(P, 1, 0), jnp.moveaxis(signs, 1, 0), jnp.moveaxis(gamma, 1, 0), jnp.moveaxis(b_in, 1, 0))
            h0 = jnp.zeros((b, H, N), dtype=x.dtype)

            def step(h, inp):
                P_t, s_t, g_t, b_t = inp
                h_perm = jnp.einsum('bhij,bhj->bhi', P_t, h)
                h = g_t * (s_t * h_perm) + (1.0 - g_t) * b_t
                return (h, h)
            _, ys = jax.lax.scan(step, h0, xs)
            out = jnp.moveaxis(ys, 0, 1).reshape(b, s, H * N) @ out_W + out_b
            return residual + out
        key = jax.random.key(seed)
        ks = jax.random.split(key, 8)
        n_hn = H * N
        inp = {'x': jax.random.normal(ks[0], (B, S, D), dtype=jnp.float32), 'ln_w': jnp.ones((D,), jnp.float32), 'ln_b': jnp.zeros((D,), jnp.float32), 'sign_W': jax.random.normal(ks[1], (D, n_hn), jnp.float32) * 0.01, 'sign_b': jnp.zeros((n_hn,), jnp.float32), 'perm_W': jax.random.normal(ks[2], (D, H * N * N), jnp.float32) * 0.01, 'perm_b': jnp.zeros((H * N * N,), jnp.float32), 'gate_W': jax.random.normal(ks[3], (D, n_hn), jnp.float32) * 0.01, 'gate_b': jnp.full((n_hn,), 2.0, jnp.float32), 'in_W': jax.random.normal(ks[4], (D, n_hn), jnp.float32) * (1.0 / np.sqrt(D)), 'in_b': jnp.zeros((n_hn,), jnp.float32), 'out_W': jax.random.normal(ks[5], (n_hn, D), jnp.float32) * (1.0 / np.sqrt(n_hn)), 'out_b': jnp.zeros((D,), jnp.float32)}
        return inp
    _L0_attn_in = _L0_attn_setup()

    def _L0_ffn_setup():
        import jax, jax.numpy as jnp
        import numpy as np
        DIM = 128
        HIDDEN = 384
        SCALE = 1.0 / 127.0

        def _dequant(w_int, dtype):
            return w_int.astype(dtype) * jnp.asarray(SCALE, dtype)
        key = jax.random.key(seed)
        k_x, k_g, k_u, k_d = jax.random.split(key, 4)
        x = jax.random.normal(k_x, (4, 256, DIM), dtype=jnp.float32)
        w_gate = jax.random.randint(k_g, (HIDDEN, DIM), -127, 128, dtype=jnp.int32)
        w_up = jax.random.randint(k_u, (HIDDEN, DIM), -127, 128, dtype=jnp.int32)
        w_down = jax.random.randint(k_d, (DIM, HIDDEN), -127, 128, dtype=jnp.int32)
        return {'x': x, 'w_gate': w_gate, 'w_up': w_up, 'w_down': w_down}
    _L0_ffn_in = _L0_ffn_setup()

    def _L1_attn_setup():
        import math
        import jax, jax.numpy as jnp
        import numpy as np
        H = 16

        def get_alibi_slopes(n):

            def pow2_slopes(n):
                start = 2 ** (-2 ** (-(math.log2(n) - 3)))
                return [start * start ** i for i in range(n)]
            if math.log2(n).is_integer():
                return pow2_slopes(n)
            c = 2 ** math.floor(math.log2(n))
            return pow2_slopes(c) + get_alibi_slopes(2 * c)[0::2][:n - c]

        def alibi_bias(num_heads, L, dtype=jnp.float32):
            slopes = jnp.asarray(get_alibi_slopes(num_heads), dtype=dtype)
            pos = jnp.arange(L)
            rel = (pos[None, :] - pos[:, None]).astype(dtype)
            bias = slopes[:, None, None] * rel[None, :, :]
            causal = pos[None, :] <= pos[:, None]
            return jnp.where(causal[None, :, :], bias, -jnp.inf)
        key = jax.random.key(seed)
        ks = jax.random.split(key, 4)
        D = 128
        B, L = (2, 256)
        s_in = 1.0 / math.sqrt(D)
        return {'x': jax.random.normal(ks[0], (B, L, D), dtype=jnp.float32), 'w_in': jax.random.normal(ks[1], (D, 3 * D), dtype=jnp.float32) * s_in, 'b_in': jnp.zeros((3 * D,), dtype=jnp.float32), 'w_out': jax.random.normal(ks[2], (D, D), dtype=jnp.float32) * s_in, 'b_out': jnp.zeros((D,), dtype=jnp.float32)}
    _L1_attn_in = _L1_attn_setup()

    def _L1_ffn_setup():
        import jax, jax.numpy as jnp
        import numpy as np
        BLOCK_SIZE = 32
        FP6_E2M3_MAX = 7.5

        def _build_fp6_e2m3_grid():
            vals = set()
            for bits in range(64):
                s = bits >> 5 & 1
                e = bits >> 3 & 3
                m = bits & 7
                v = m / 8.0 if e == 0 else (1.0 + m / 8.0) * 2.0 ** (e - 1)
                vals.add(-v if s else v)
            return np.array(sorted(vals), dtype=np.float32)
        _GRID = jnp.asarray(_build_fp6_e2m3_grid())

        def _nearest_on_grid(x, grid):
            idx = jnp.clip(jnp.searchsorted(grid, x), 0, grid.shape[0] - 1)
            idx_lo = jnp.maximum(idx - 1, 0)
            v_hi = grid[idx]
            v_lo = grid[idx_lo]
            return jnp.where(jnp.abs(x - v_lo) <= jnp.abs(x - v_hi), v_lo, v_hi)

        def _mx_quantize(t, eps=1e-30):
            rows, K = t.shape
            blocks = t.reshape(rows, K // BLOCK_SIZE, BLOCK_SIZE)
            scales = jnp.maximum(jnp.max(jnp.abs(blocks), axis=-1) / FP6_E2M3_MAX, eps)
            q = _nearest_on_grid(blocks / scales[..., None], _GRID)
            return (q, scales)
        key = jax.random.key(seed)
        k1, k2, k3 = jax.random.split(key, 3)
        x = jax.random.normal(k1, (8, 1024, 128), dtype=jnp.float32)
        weight = jax.random.normal(k2, (128, 128), dtype=jnp.float32) * 0.02
        bias = jax.random.normal(k3, (128,), dtype=jnp.float32) * 0.02
        return {'x': x, 'weight': weight, 'bias': bias}
    _L1_ffn_in = _L1_ffn_setup()

    def _L2_attn_setup():
        import math
        import jax, jax.numpy as jnp
        import numpy as np
        from jax import lax
        D_MODEL = 128
        D_STATE = 8
        D_CONV = 4
        EXPAND = 2
        D_INNER = EXPAND * D_MODEL
        DT_RANK = math.ceil(D_MODEL / 16)
        R_RANK = 8
        BATCH, SEQLEN = (2, 512)

        def _silu(x):
            return x * jax.nn.sigmoid(x)

        def _mamba_fwd(hidden_states, in_proj_w, conv_w, conv_b, x_proj_w, dt_proj_w, dt_proj_b, A_log, D, out_proj_w, U_param, V_param, low_rank_scale):
            b, l, _ = hidden_states.shape
            xz = jnp.einsum('bld,ed->bel', hidden_states, in_proj_w)
            x, z = (xz[:, :D_INNER], xz[:, D_INNER:])
            xp = jnp.pad(x, ((0, 0), (0, 0), (D_CONV - 1, 0)))
            x = lax.conv_general_dilated(xp, conv_w[:, None, :], (1,), 'VALID', dimension_numbers=('NCH', 'OIH', 'NCH'), feature_group_count=D_INNER)
            x = _silu(x + conv_b[None, :, None])
            x_dbl = jnp.einsum('bdl,kd->blk', x, x_proj_w)
            dt_lr = x_dbl[..., :DT_RANK]
            B = x_dbl[..., DT_RANK:DT_RANK + D_STATE]
            C = x_dbl[..., DT_RANK + D_STATE:]
            dt = jnp.einsum('blr,dr->bld', dt_lr, dt_proj_w)
            A = -jnp.exp(A_log) + low_rank_scale * (U_param @ V_param) / math.sqrt(R_RANK)
            delta = jax.nn.softplus(dt + dt_proj_b[None, None, :])
            u = jnp.swapaxes(x, 1, 2)
            xs = (jnp.swapaxes(delta, 0, 1), jnp.swapaxes(B, 0, 1), jnp.swapaxes(u, 0, 1), jnp.swapaxes(C, 0, 1))
            h0 = jnp.zeros((b, D_INNER, D_STATE), dtype=jnp.float32)

            def step(h, t):
                dlt, Bt, ut, Ct = t
                dA = jnp.exp(dlt[..., None] * A)
                h = h * dA + (dlt * ut)[..., None] * Bt[:, None, :]
                y = jnp.einsum('bdn,bn->bd', h, Ct)
                return (h, y)
            _, ys = lax.scan(step, h0, xs)
            y = jnp.swapaxes(ys, 0, 1)
            y = y + u * D[None, None, :]
            y = y * _silu(jnp.swapaxes(z, 1, 2))
            return jnp.einsum('bld,md->blm', y, out_proj_w)
        key = jax.random.key(seed)
        ks = jax.random.split(key, 12)
        hidden_states = jax.random.normal(ks[0], (BATCH, SEQLEN, D_MODEL), dtype=jnp.float32)
        in_proj_w = jax.random.normal(ks[1], (2 * D_INNER, D_MODEL), dtype=jnp.float32) * D_MODEL ** (-0.5)
        conv_w = jax.random.normal(ks[2], (D_INNER, D_CONV), dtype=jnp.float32) * D_CONV ** (-0.5)
        conv_b = jax.random.normal(ks[3], (D_INNER,), dtype=jnp.float32) * 0.02
        x_proj_w = jax.random.normal(ks[4], (DT_RANK + 2 * D_STATE, D_INNER), dtype=jnp.float32) * D_INNER ** (-0.5)
        dt_init_std = DT_RANK ** (-0.5)
        dt_proj_w = jax.random.uniform(ks[5], (D_INNER, DT_RANK), minval=-dt_init_std, maxval=dt_init_std, dtype=jnp.float32)
        dt = jnp.exp(jax.random.uniform(ks[6], (D_INNER,)) * (math.log(0.1) - math.log(0.001)) + math.log(0.001))
        dt = jnp.clip(dt, 0.0001, None)
        dt_proj_b = dt + jnp.log(-jnp.expm1(-dt))
        A_log = jnp.log(jnp.broadcast_to(jnp.arange(1, D_STATE + 1, dtype=jnp.float32), (D_INNER, D_STATE)))
        D = jnp.ones((D_INNER,), dtype=jnp.float32)
        out_proj_w = jax.random.normal(ks[7], (D_MODEL, D_INNER), dtype=jnp.float32) * D_INNER ** (-0.5)
        U_param = jax.random.normal(ks[8], (D_INNER, R_RANK), dtype=jnp.float32) * 0.02
        V_param = jax.random.normal(ks[9], (R_RANK, D_STATE), dtype=jnp.float32) * 0.02
        low_rank_scale = jnp.float32(0.05)
        return dict(hidden_states=hidden_states, in_proj_w=in_proj_w, conv_w=conv_w, conv_b=conv_b, x_proj_w=x_proj_w, dt_proj_w=dt_proj_w, dt_proj_b=dt_proj_b, A_log=A_log, D=D, out_proj_w=out_proj_w, U_param=U_param, V_param=V_param, low_rank_scale=low_rank_scale)
    _L2_attn_in = _L2_attn_setup()

    def _L2_ffn_setup():
        import jax, jax.numpy as jnp
        import numpy as np
        D_MODEL, D_FF, N_EXPERTS, TOP_K = (128, 256, 8, 2)
        B, S = (2, 256)
        key = jax.random.key(seed)
        ks = jax.random.split(key, 6)
        sd = 1.0 / np.sqrt(D_MODEL)
        sf = 1.0 / np.sqrt(D_FF)
        return {'x': jax.random.normal(ks[0], (B, S, D_MODEL), jnp.float32), 'router_w': jax.random.normal(ks[1], (N_EXPERTS, D_MODEL), jnp.float32) * sd, 'gate_w': jax.random.normal(ks[2], (N_EXPERTS, D_MODEL, D_FF), jnp.float32) * sd, 'gate_b': jnp.zeros((N_EXPERTS, D_FF), jnp.float32), 'up_w': jax.random.normal(ks[3], (N_EXPERTS, D_MODEL, D_FF), jnp.float32) * sd, 'up_b': jnp.zeros((N_EXPERTS, D_FF), jnp.float32), 'down_w': jax.random.normal(ks[4], (N_EXPERTS, D_FF, D_MODEL), jnp.float32) * sf, 'down_b': jnp.zeros((N_EXPERTS, D_MODEL), jnp.float32)}
    _L2_ffn_in = _L2_ffn_setup()

    def _L3_attn_setup():
        import jax, jax.numpy as jnp
        import numpy as np
        D_MODEL = 128
        N_LAYERS = 4
        D_STATE = 16
        D_CONV = 4
        EXPAND = 2
        D_INNER = EXPAND * D_MODEL
        DT_RANK = D_MODEL // 16
        B_SZ = 2
        SEQ = 128
        EPS = 1e-05

        def _layer_norm(x, w, b):
            m = x.mean(-1, keepdims=True)
            v = x.var(-1, keepdims=True)
            return (x - m) * jax.lax.rsqrt(v + EPS) * w + b

        def _mamba(x, in_w, cw, cb, xpw, dtw, dtb, A_log, Dp, ow):
            B, L, _ = x.shape
            xz = x @ in_w
            u, z = jnp.split(xz, 2, axis=-1)
            up = jnp.pad(u, ((0, 0), (D_CONV - 1, 0), (0, 0)))
            uc = cb + sum((up[:, k:k + L, :] * cw[:, k] for k in range(D_CONV)))
            u = jax.nn.silu(uc)
            proj = u @ xpw
            dt = proj[..., :DT_RANK]
            Bm = proj[..., DT_RANK:DT_RANK + D_STATE]
            Cm = proj[..., DT_RANK + D_STATE:]
            delta = jax.nn.softplus(dt @ dtw + dtb)
            A = -jnp.exp(A_log)

            def step(h, inp):
                d_t, b_t, c_t, u_t = inp
                dA = jnp.exp(d_t[..., None] * A)
                h = dA * h + (d_t * u_t)[..., None] * b_t[:, None, :]
                y = jnp.einsum('bdn,bn->bd', h, c_t)
                return (h, y)
            h0 = jnp.zeros((B, D_INNER, D_STATE), x.dtype)
            xs = (jnp.moveaxis(delta, 1, 0), jnp.moveaxis(Bm, 1, 0), jnp.moveaxis(Cm, 1, 0), jnp.moveaxis(u, 1, 0))
            _, ys = jax.lax.scan(step, h0, xs)
            y = jnp.moveaxis(ys, 0, 1) + u * Dp
            y = y * jax.nn.silu(z)
            return y @ ow
        key = jax.random.key(seed)
        ks = jax.random.split(key, 8)

        def nrm(k, shape, s=0.02):
            return jax.random.normal(k, shape, jnp.float32) * s
        x = jax.random.normal(ks[0], (B_SZ, SEQ, D_MODEL), jnp.float32)
        in_proj_w = nrm(ks[1], (N_LAYERS, D_MODEL, 2 * D_INNER))
        conv_w = nrm(ks[2], (N_LAYERS, D_INNER, D_CONV), 0.1)
        conv_b = jnp.zeros((N_LAYERS, D_INNER), jnp.float32)
        x_proj_w = nrm(ks[3], (N_LAYERS, D_INNER, DT_RANK + 2 * D_STATE))
        dt_proj_w = nrm(ks[4], (N_LAYERS, DT_RANK, D_INNER), 0.1)
        dt_proj_b = jax.random.uniform(ks[5], (N_LAYERS, D_INNER), jnp.float32, -4.0, -2.0)
        A_log = jnp.tile(jnp.log(jnp.arange(1, D_STATE + 1, dtype=jnp.float32)), (N_LAYERS, D_INNER, 1))
        D = jnp.ones((N_LAYERS, D_INNER), jnp.float32)
        out_proj_w = nrm(ks[6], (N_LAYERS, D_INNER, D_MODEL))
        ln_w = jnp.ones((N_LAYERS, D_MODEL), jnp.float32)
        ln_b = jnp.zeros((N_LAYERS, D_MODEL), jnp.float32)
        return dict(x=x, in_proj_w=in_proj_w, conv_w=conv_w, conv_b=conv_b, x_proj_w=x_proj_w, dt_proj_w=dt_proj_w, dt_proj_b=dt_proj_b, A_log=A_log, D=D, out_proj_w=out_proj_w, ln_w=ln_w, ln_b=ln_b)
    _L3_attn_in = _L3_attn_setup()

    def _L3_ffn_setup():
        import jax, jax.numpy as jnp
        import numpy as np
        DIM = 128
        DEPTH = 2
        HEADS = 8
        DIM_HEAD = 64
        WINDOW = 64
        INNER = HEADS * DIM_HEAD
        HID = int(DIM * 4 * 2 / 3)
        B, N = (2, 1024)
        QK_SCALE = 8.0

        def shift_token(t):
            t1, t2 = jnp.split(t, 2, axis=-1)
            t2 = jnp.pad(t2, ((0, 0), (1, 0), (0, 0)))[:, :-1]
            return jnp.concatenate([t1, t2], axis=-1)

        def l2norm(t):
            return t / jnp.clip(jnp.linalg.norm(t, axis=-1, keepdims=True), 1e-12)

        def rotate_half(x):
            x1, x2 = jnp.split(x, 2, axis=-1)
            return jnp.concatenate([-x2, x1], axis=-1)

        def rotary_xpos(q, k):
            n = q.shape[-2]
            half_idx = jnp.arange(0, DIM_HEAD, 2, dtype=jnp.float32)
            inv_freq = 1.0 / 10000.0 ** (half_idx / DIM_HEAD)
            t = jnp.arange(n, dtype=jnp.float32)
            freqs = t[:, None] * inv_freq[None, :]
            freqs = jnp.concatenate([freqs, freqs], axis=-1)
            base = (half_idx + 0.4 * DIM_HEAD) / (1.4 * DIM_HEAD)
            power = (t - n // 2) / float(WINDOW // 2)
            scale = base[None, :] ** power[:, None]
            scale = jnp.concatenate([scale, scale], axis=-1)
            cos, sin = (jnp.cos(freqs), jnp.sin(freqs))
            q = q * cos * scale + rotate_half(q) * sin * scale
            k = k * cos / scale + rotate_half(k) * sin / scale
            return (q, k)

        def local_attention(q, k, v):
            b, h, n, d = q.shape
            w = n // WINDOW
            bq = q.reshape(b, h, w, WINDOW, d) * QK_SCALE
            bk = k.reshape(b, h, w, WINDOW, d)
            bv = v.reshape(b, h, w, WINDOW, d)

            def look_around(t):
                p = jnp.pad(t, ((0, 0), (0, 0), (1, 0), (0, 0), (0, 0)))
                return jnp.concatenate([p[:, :, :w], p[:, :, 1:]], axis=3)
            bk, bv = (look_around(bk), look_around(bv))
            bt = jnp.arange(n).reshape(w, WINDOW)
            btp = jnp.pad(bt, ((1, 0), (0, 0)), constant_values=-1)
            btk = jnp.concatenate([btp[:w], btp[1:]], axis=1)
            sim = jnp.einsum('bhwid,bhwjd->bhwij', bq, bk)
            i = bt[:, :, None]
            j = btk[:, None, :]
            mask = (i < j) | (i > j + WINDOW) | (j == -1)
            sim = jnp.where(mask, -jnp.finfo(sim.dtype).max, sim)
            attn = jax.nn.softmax(sim, axis=-1)
            out = jnp.einsum('bhwij,bhwjd->bhwid', attn, bv)
            return out.reshape(b, h, n, d)

        def _layer(x, wqkv, qs, ksc, wo, lg, lb, w1, b1, w2, b2):
            b, n, _ = x.shape
            h = shift_token(x)
            qkv = h @ wqkv
            q, k, v = jnp.split(qkv, 3, axis=-1)
            to_heads = lambda t: t.reshape(b, n, HEADS, DIM_HEAD).transpose(0, 2, 1, 3)
            q, k, v = (to_heads(q), to_heads(k), to_heads(v))
            q = l2norm(q) * qs
            k = l2norm(k) * ksc
            q, k = rotary_xpos(q, k)
            o = local_attention(q, k, v)
            o = o.transpose(0, 2, 1, 3).reshape(b, n, INNER)
            x = x + o @ wo
            h = shift_token(x)
            mu = h.mean(-1, keepdims=True)
            var = h.var(-1, keepdims=True)
            h = (h - mu) / jnp.sqrt(var + 1e-05) * lg + lb
            h = h @ w1 + b1
            a, g = jnp.split(h, 2, axis=-1)
            h = a * jax.nn.gelu(g, approximate=False)
            x = x + h @ w2 + b2
            return x
        key = jax.random.key(seed)
        ks = jax.random.split(key, 6)
        return {'x': jax.random.normal(ks[0], (B, N, DIM), jnp.float32), 'wqkv': jax.random.normal(ks[1], (DEPTH, DIM, 3 * INNER), jnp.float32) * 0.02, 'q_scale': jnp.ones((DEPTH, DIM_HEAD), jnp.float32), 'k_scale': jnp.ones((DEPTH, DIM_HEAD), jnp.float32), 'wo': jax.random.normal(ks[2], (DEPTH, INNER, DIM), jnp.float32) * 0.02, 'ln_g': jnp.ones((DEPTH, DIM), jnp.float32), 'ln_b': jnp.zeros((DEPTH, DIM), jnp.float32), 'w1': jax.random.normal(ks[3], (DEPTH, DIM, 2 * HID), jnp.float32) * 0.02, 'b1': jnp.zeros((DEPTH, 2 * HID), jnp.float32), 'w2': jax.random.normal(ks[4], (DEPTH, HID, DIM), jnp.float32) * 0.02, 'b2': jnp.zeros((DEPTH, DIM), jnp.float32)}
    _L3_ffn_in = _L3_ffn_setup()
    _d = {'L0_attn_x': _L0_attn_in['x'], 'L0_attn_ln_w': _L0_attn_in['ln_w'], 'L0_attn_ln_b': _L0_attn_in['ln_b'], 'L0_attn_sign_W': _L0_attn_in['sign_W'], 'L0_attn_sign_b': _L0_attn_in['sign_b'], 'L0_attn_perm_W': _L0_attn_in['perm_W'], 'L0_attn_perm_b': _L0_attn_in['perm_b'], 'L0_attn_gate_W': _L0_attn_in['gate_W'], 'L0_attn_gate_b': _L0_attn_in['gate_b'], 'L0_attn_in_W': _L0_attn_in['in_W'], 'L0_attn_in_b': _L0_attn_in['in_b'], 'L0_attn_out_W': _L0_attn_in['out_W'], 'L0_attn_out_b': _L0_attn_in['out_b'], 'L0_ffn_w_gate': _L0_ffn_in['w_gate'], 'L0_ffn_w_up': _L0_ffn_in['w_up'], 'L0_ffn_w_down': _L0_ffn_in['w_down'], 'L1_attn_w_in': _L1_attn_in['w_in'], 'L1_attn_b_in': _L1_attn_in['b_in'], 'L1_attn_w_out': _L1_attn_in['w_out'], 'L1_attn_b_out': _L1_attn_in['b_out'], 'L1_ffn_weight': _L1_ffn_in['weight'], 'L1_ffn_bias': _L1_ffn_in['bias'], 'L2_attn_in_proj_w': _L2_attn_in['in_proj_w'], 'L2_attn_conv_w': _L2_attn_in['conv_w'], 'L2_attn_conv_b': _L2_attn_in['conv_b'], 'L2_attn_x_proj_w': _L2_attn_in['x_proj_w'], 'L2_attn_dt_proj_w': _L2_attn_in['dt_proj_w'], 'L2_attn_dt_proj_b': _L2_attn_in['dt_proj_b'], 'L2_attn_A_log': _L2_attn_in['A_log'], 'L2_attn_D': _L2_attn_in['D'], 'L2_attn_out_proj_w': _L2_attn_in['out_proj_w'], 'L2_attn_U_param': _L2_attn_in['U_param'], 'L2_attn_V_param': _L2_attn_in['V_param'], 'L2_attn_low_rank_scale': _L2_attn_in['low_rank_scale'], 'L2_ffn_router_w': _L2_ffn_in['router_w'], 'L2_ffn_gate_w': _L2_ffn_in['gate_w'], 'L2_ffn_gate_b': _L2_ffn_in['gate_b'], 'L2_ffn_up_w': _L2_ffn_in['up_w'], 'L2_ffn_up_b': _L2_ffn_in['up_b'], 'L2_ffn_down_w': _L2_ffn_in['down_w'], 'L2_ffn_down_b': _L2_ffn_in['down_b'], 'L3_attn_in_proj_w': _L3_attn_in['in_proj_w'], 'L3_attn_conv_w': _L3_attn_in['conv_w'], 'L3_attn_conv_b': _L3_attn_in['conv_b'], 'L3_attn_x_proj_w': _L3_attn_in['x_proj_w'], 'L3_attn_dt_proj_w': _L3_attn_in['dt_proj_w'], 'L3_attn_dt_proj_b': _L3_attn_in['dt_proj_b'], 'L3_attn_A_log': _L3_attn_in['A_log'], 'L3_attn_D': _L3_attn_in['D'], 'L3_attn_out_proj_w': _L3_attn_in['out_proj_w'], 'L3_attn_ln_w': _L3_attn_in['ln_w'], 'L3_attn_ln_b': _L3_attn_in['ln_b'], 'L3_ffn_wqkv': _L3_ffn_in['wqkv'], 'L3_ffn_q_scale': _L3_ffn_in['q_scale'], 'L3_ffn_k_scale': _L3_ffn_in['k_scale'], 'L3_ffn_wo': _L3_ffn_in['wo'], 'L3_ffn_ln_g': _L3_ffn_in['ln_g'], 'L3_ffn_ln_b': _L3_ffn_in['ln_b'], 'L3_ffn_w1': _L3_ffn_in['w1'], 'L3_ffn_b1': _L3_ffn_in['b1'], 'L3_ffn_w2': _L3_ffn_in['w2'], 'L3_ffn_b2': _L3_ffn_in['b2']}
    _x0 = _d['L0_attn_x']
    _d['L0_attn_x'] = jax.random.normal(jax.random.fold_in(jax.random.key(seed), 1), (16, 256, 128), dtype=_x0.dtype)
    del _x0
    return _d

def reference(L0_attn_x, L0_attn_ln_w, L0_attn_ln_b, L0_attn_sign_W, L0_attn_sign_b, L0_attn_perm_W, L0_attn_perm_b, L0_attn_gate_W, L0_attn_gate_b, L0_attn_in_W, L0_attn_in_b, L0_attn_out_W, L0_attn_out_b, L0_ffn_w_gate, L0_ffn_w_up, L0_ffn_w_down, L1_attn_w_in, L1_attn_b_in, L1_attn_w_out, L1_attn_b_out, L1_ffn_weight, L1_ffn_bias, L2_attn_in_proj_w, L2_attn_conv_w, L2_attn_conv_b, L2_attn_x_proj_w, L2_attn_dt_proj_w, L2_attn_dt_proj_b, L2_attn_A_log, L2_attn_D, L2_attn_out_proj_w, L2_attn_U_param, L2_attn_V_param, L2_attn_low_rank_scale, L2_ffn_router_w, L2_ffn_gate_w, L2_ffn_gate_b, L2_ffn_up_w, L2_ffn_up_b, L2_ffn_down_w, L2_ffn_down_b, L3_attn_in_proj_w, L3_attn_conv_w, L3_attn_conv_b, L3_attn_x_proj_w, L3_attn_dt_proj_w, L3_attn_dt_proj_b, L3_attn_A_log, L3_attn_D, L3_attn_out_proj_w, L3_attn_ln_w, L3_attn_ln_b, L3_ffn_wqkv, L3_ffn_q_scale, L3_ffn_k_scale, L3_ffn_wo, L3_ffn_ln_g, L3_ffn_ln_b, L3_ffn_w1, L3_ffn_b1, L3_ffn_w2, L3_ffn_b2):

    def _L0_attn_ref(x, ln_w, ln_b, sign_W, sign_b, perm_W, perm_b, gate_W, gate_b, in_W, in_b, out_W, out_b):
        import jax, jax.numpy as jnp
        import numpy as np
        B, S, D, H, N = (8, 256, 128, 4, 8)
        TAU = 1.0
        SINKHORN_ITERS = 5
        LN_EPS = 1e-05

        def _sinkhorn(log_alpha):
            for _ in range(SINKHORN_ITERS):
                log_alpha = log_alpha - jax.nn.logsumexp(log_alpha, axis=-1, keepdims=True)
                log_alpha = log_alpha - jax.nn.logsumexp(log_alpha, axis=-2, keepdims=True)
            return jnp.exp(log_alpha)

        def _greedy_hard_one(soft):
            n = soft.shape[-1]
            order = jnp.argsort(-soft.max(axis=-1))

            def body(i, carry):
                avail, hard = carry
                r = order[i]
                scores = jnp.where(avail, soft[r], -jnp.inf)
                c = jnp.argmax(scores)
                return (avail.at[c].set(False), hard.at[r, c].set(1.0))
            avail0 = jnp.ones((n,), dtype=bool)
            hard0 = jnp.zeros_like(soft)
            _, hard = jax.lax.fori_loop(0, n, body, (avail0, hard0))
            return hard

        def _forward(x, ln_w, ln_b, sign_W, sign_b, perm_W, perm_b, gate_W, gate_b, in_W, in_b, out_W, out_b):
            b, s, d = x.shape
            residual = x
            mu = x.mean(axis=-1, keepdims=True)
            var = x.var(axis=-1, keepdims=True)
            xn = (x - mu) / jnp.sqrt(var + LN_EPS) * ln_w + ln_b
            signs = 2.0 * jax.nn.sigmoid((xn @ sign_W + sign_b).reshape(b, s, H, N)) - 1.0
            perm_logits = (xn @ perm_W + perm_b).reshape(b, s, H, N, N) / TAU
            gamma = jax.nn.sigmoid((xn @ gate_W + gate_b).reshape(b, s, H, N))
            b_in = (xn @ in_W + in_b).reshape(b, s, H, N)
            soft = _sinkhorn(perm_logits)
            soft_sg = jax.lax.stop_gradient(soft)
            hard = jax.vmap(_greedy_hard_one)(soft_sg.reshape(-1, N, N)).reshape(soft.shape)
            P = hard + soft - soft_sg
            xs = (jnp.moveaxis(P, 1, 0), jnp.moveaxis(signs, 1, 0), jnp.moveaxis(gamma, 1, 0), jnp.moveaxis(b_in, 1, 0))
            h0 = jnp.zeros((b, H, N), dtype=x.dtype)

            def step(h, inp):
                P_t, s_t, g_t, b_t = inp
                h_perm = jnp.einsum('bhij,bhj->bhi', P_t, h)
                h = g_t * (s_t * h_perm) + (1.0 - g_t) * b_t
                return (h, h)
            _, ys = jax.lax.scan(step, h0, xs)
            out = jnp.moveaxis(ys, 0, 1).reshape(b, s, H * N) @ out_W + out_b
            return residual + out
        return _forward(x, ln_w, ln_b, sign_W, sign_b, perm_W, perm_b, gate_W, gate_b, in_W, in_b, out_W, out_b)

    def _L0_ffn_ref(x, w_gate, w_up, w_down):
        import jax, jax.numpy as jnp
        import numpy as np
        DIM = 128
        HIDDEN = 384
        SCALE = 1.0 / 127.0

        def _dequant(w_int, dtype):
            return w_int.astype(dtype) * jnp.asarray(SCALE, dtype)
        wg = _dequant(w_gate, x.dtype)
        wu = _dequant(w_up, x.dtype)
        wd = _dequant(w_down, x.dtype)
        gate = jnp.einsum('bsd,hd->bsh', x, wg)
        up = jnp.einsum('bsd,hd->bsh', x, wu)
        h = jax.nn.silu(gate) * up
        return jnp.einsum('bsh,dh->bsd', h, wd)

    def _L1_attn_ref(x, w_in, b_in, w_out, b_out):
        import math
        import jax, jax.numpy as jnp
        import numpy as np
        H = 16

        def get_alibi_slopes(n):

            def pow2_slopes(n):
                start = 2 ** (-2 ** (-(math.log2(n) - 3)))
                return [start * start ** i for i in range(n)]
            if math.log2(n).is_integer():
                return pow2_slopes(n)
            c = 2 ** math.floor(math.log2(n))
            return pow2_slopes(c) + get_alibi_slopes(2 * c)[0::2][:n - c]

        def alibi_bias(num_heads, L, dtype=jnp.float32):
            slopes = jnp.asarray(get_alibi_slopes(num_heads), dtype=dtype)
            pos = jnp.arange(L)
            rel = (pos[None, :] - pos[:, None]).astype(dtype)
            bias = slopes[:, None, None] * rel[None, :, :]
            causal = pos[None, :] <= pos[:, None]
            return jnp.where(causal[None, :, :], bias, -jnp.inf)
        B, L, D = x.shape
        dh = D // H
        qkv = x @ w_in + b_in
        q, k, v = jnp.split(qkv, 3, axis=-1)

        def heads(t):
            return t.reshape(B, L, H, dh).transpose(0, 2, 1, 3)
        q, k, v = (heads(q), heads(k), heads(v))
        scores = jnp.einsum('bhqd,bhkd->bhqk', q, k) / math.sqrt(dh)
        scores = scores + alibi_bias(H, L, scores.dtype)[None]
        attn = jax.nn.softmax(scores, axis=-1)
        out = jnp.einsum('bhqk,bhkd->bhqd', attn, v)
        out = out.transpose(0, 2, 1, 3).reshape(B, L, D)
        return out @ w_out + b_out

    def _L1_ffn_ref(x, weight, bias):
        import jax, jax.numpy as jnp
        import numpy as np
        BLOCK_SIZE = 32
        FP6_E2M3_MAX = 7.5

        def _build_fp6_e2m3_grid():
            vals = set()
            for bits in range(64):
                s = bits >> 5 & 1
                e = bits >> 3 & 3
                m = bits & 7
                v = m / 8.0 if e == 0 else (1.0 + m / 8.0) * 2.0 ** (e - 1)
                vals.add(-v if s else v)
            return np.array(sorted(vals), dtype=np.float32)
        _GRID = jnp.asarray(_build_fp6_e2m3_grid())

        def _nearest_on_grid(x, grid):
            idx = jnp.clip(jnp.searchsorted(grid, x), 0, grid.shape[0] - 1)
            idx_lo = jnp.maximum(idx - 1, 0)
            v_hi = grid[idx]
            v_lo = grid[idx_lo]
            return jnp.where(jnp.abs(x - v_lo) <= jnp.abs(x - v_hi), v_lo, v_hi)

        def _mx_quantize(t, eps=1e-30):
            rows, K = t.shape
            blocks = t.reshape(rows, K // BLOCK_SIZE, BLOCK_SIZE)
            scales = jnp.maximum(jnp.max(jnp.abs(blocks), axis=-1) / FP6_E2M3_MAX, eps)
            q = _nearest_on_grid(blocks / scales[..., None], _GRID)
            return (q, scales)
        batch_shape = x.shape[:-1]
        in_features = x.shape[-1]
        x2 = x.astype(jnp.float32).reshape(-1, in_features)
        w2 = weight.astype(jnp.float32)
        xq, xs = _mx_quantize(x2)
        wq, ws = _mx_quantize(w2)
        xd = (xq * xs[..., None]).reshape(x2.shape)
        wd = (wq * ws[..., None]).reshape(w2.shape)
        out = xd @ wd.T + bias
        return out.reshape(*batch_shape, -1)

    def _L2_attn_ref(hidden_states, in_proj_w, conv_w, conv_b, x_proj_w, dt_proj_w, dt_proj_b, A_log, D, out_proj_w, U_param, V_param, low_rank_scale):
        import math
        import jax, jax.numpy as jnp
        import numpy as np
        from jax import lax
        D_MODEL = 128
        D_STATE = 8
        D_CONV = 4
        EXPAND = 2
        D_INNER = EXPAND * D_MODEL
        DT_RANK = math.ceil(D_MODEL / 16)
        R_RANK = 8
        BATCH, SEQLEN = (2, 512)

        def _silu(x):
            return x * jax.nn.sigmoid(x)

        def _mamba_fwd(hidden_states, in_proj_w, conv_w, conv_b, x_proj_w, dt_proj_w, dt_proj_b, A_log, D, out_proj_w, U_param, V_param, low_rank_scale):
            b, l, _ = hidden_states.shape
            xz = jnp.einsum('bld,ed->bel', hidden_states, in_proj_w)
            x, z = (xz[:, :D_INNER], xz[:, D_INNER:])
            xp = jnp.pad(x, ((0, 0), (0, 0), (D_CONV - 1, 0)))
            x = lax.conv_general_dilated(xp, conv_w[:, None, :], (1,), 'VALID', dimension_numbers=('NCH', 'OIH', 'NCH'), feature_group_count=D_INNER)
            x = _silu(x + conv_b[None, :, None])
            x_dbl = jnp.einsum('bdl,kd->blk', x, x_proj_w)
            dt_lr = x_dbl[..., :DT_RANK]
            B = x_dbl[..., DT_RANK:DT_RANK + D_STATE]
            C = x_dbl[..., DT_RANK + D_STATE:]
            dt = jnp.einsum('blr,dr->bld', dt_lr, dt_proj_w)
            A = -jnp.exp(A_log) + low_rank_scale * (U_param @ V_param) / math.sqrt(R_RANK)
            delta = jax.nn.softplus(dt + dt_proj_b[None, None, :])
            u = jnp.swapaxes(x, 1, 2)
            xs = (jnp.swapaxes(delta, 0, 1), jnp.swapaxes(B, 0, 1), jnp.swapaxes(u, 0, 1), jnp.swapaxes(C, 0, 1))
            h0 = jnp.zeros((b, D_INNER, D_STATE), dtype=jnp.float32)

            def step(h, t):
                dlt, Bt, ut, Ct = t
                dA = jnp.exp(dlt[..., None] * A)
                h = h * dA + (dlt * ut)[..., None] * Bt[:, None, :]
                y = jnp.einsum('bdn,bn->bd', h, Ct)
                return (h, y)
            _, ys = lax.scan(step, h0, xs)
            y = jnp.swapaxes(ys, 0, 1)
            y = y + u * D[None, None, :]
            y = y * _silu(jnp.swapaxes(z, 1, 2))
            return jnp.einsum('bld,md->blm', y, out_proj_w)
        return _mamba_fwd(hidden_states, in_proj_w, conv_w, conv_b, x_proj_w, dt_proj_w, dt_proj_b, A_log, D, out_proj_w, U_param, V_param, low_rank_scale)

    def _L2_ffn_ref(x, router_w, gate_w, gate_b, up_w, up_b, down_w, down_b):
        import jax, jax.numpy as jnp
        import numpy as np
        D_MODEL, D_FF, N_EXPERTS, TOP_K = (128, 256, 8, 2)
        B, S = (2, 256)
        b, s, d = x.shape
        xf = x.reshape(b * s, d)
        n = xf.shape[0]
        router_logits = xf @ router_w.T
        probs = jax.nn.softmax(router_logits, axis=-1)
        topv, topi = jax.lax.top_k(probs, TOP_K)
        mask = jnp.zeros_like(probs).at[jnp.arange(n)[:, None], topi].set(1.0)
        probs = probs * mask
        probs = probs / (probs.sum(axis=-1, keepdims=True) + 1e-09)
        g = jnp.einsum('nd,edf->nef', xf, gate_w) + gate_b
        u = jnp.einsum('nd,edf->nef', xf, up_w) + up_b
        h = jax.nn.silu(g) * u
        expert_out = jnp.einsum('nef,efd->ned', h, down_w) + down_b
        y = jnp.einsum('ne,ned->nd', probs, expert_out)
        return y.reshape(b, s, d)

    def _L3_attn_ref(x, in_proj_w, conv_w, conv_b, x_proj_w, dt_proj_w, dt_proj_b, A_log, D, out_proj_w, ln_w, ln_b):
        import jax, jax.numpy as jnp
        import numpy as np
        D_MODEL = 128
        N_LAYERS = 4
        D_STATE = 16
        D_CONV = 4
        EXPAND = 2
        D_INNER = EXPAND * D_MODEL
        DT_RANK = D_MODEL // 16
        B_SZ = 2
        SEQ = 128
        EPS = 1e-05

        def _layer_norm(x, w, b):
            m = x.mean(-1, keepdims=True)
            v = x.var(-1, keepdims=True)
            return (x - m) * jax.lax.rsqrt(v + EPS) * w + b

        def _mamba(x, in_w, cw, cb, xpw, dtw, dtb, A_log, Dp, ow):
            B, L, _ = x.shape
            xz = x @ in_w
            u, z = jnp.split(xz, 2, axis=-1)
            up = jnp.pad(u, ((0, 0), (D_CONV - 1, 0), (0, 0)))
            uc = cb + sum((up[:, k:k + L, :] * cw[:, k] for k in range(D_CONV)))
            u = jax.nn.silu(uc)
            proj = u @ xpw
            dt = proj[..., :DT_RANK]
            Bm = proj[..., DT_RANK:DT_RANK + D_STATE]
            Cm = proj[..., DT_RANK + D_STATE:]
            delta = jax.nn.softplus(dt @ dtw + dtb)
            A = -jnp.exp(A_log)

            def step(h, inp):
                d_t, b_t, c_t, u_t = inp
                dA = jnp.exp(d_t[..., None] * A)
                h = dA * h + (d_t * u_t)[..., None] * b_t[:, None, :]
                y = jnp.einsum('bdn,bn->bd', h, c_t)
                return (h, y)
            h0 = jnp.zeros((B, D_INNER, D_STATE), x.dtype)
            xs = (jnp.moveaxis(delta, 1, 0), jnp.moveaxis(Bm, 1, 0), jnp.moveaxis(Cm, 1, 0), jnp.moveaxis(u, 1, 0))
            _, ys = jax.lax.scan(step, h0, xs)
            y = jnp.moveaxis(ys, 0, 1) + u * Dp
            y = y * jax.nn.silu(z)
            return y @ ow
        for i in range(in_proj_w.shape[0]):
            y = _mamba(x, in_proj_w[i], conv_w[i], conv_b[i], x_proj_w[i], dt_proj_w[i], dt_proj_b[i], A_log[i], D[i], out_proj_w[i])
            x = _layer_norm(y + x, ln_w[i], ln_b[i])
        return x

    def _L3_ffn_ref(x, wqkv, q_scale, k_scale, wo, ln_g, ln_b, w1, b1, w2, b2):
        import jax, jax.numpy as jnp
        import numpy as np
        DIM = 128
        DEPTH = 2
        HEADS = 8
        DIM_HEAD = 64
        WINDOW = 64
        INNER = HEADS * DIM_HEAD
        HID = int(DIM * 4 * 2 / 3)
        B, N = (2, 1024)
        QK_SCALE = 8.0

        def shift_token(t):
            t1, t2 = jnp.split(t, 2, axis=-1)
            t2 = jnp.pad(t2, ((0, 0), (1, 0), (0, 0)))[:, :-1]
            return jnp.concatenate([t1, t2], axis=-1)

        def l2norm(t):
            return t / jnp.clip(jnp.linalg.norm(t, axis=-1, keepdims=True), 1e-12)

        def rotate_half(x):
            x1, x2 = jnp.split(x, 2, axis=-1)
            return jnp.concatenate([-x2, x1], axis=-1)

        def rotary_xpos(q, k):
            n = q.shape[-2]
            half_idx = jnp.arange(0, DIM_HEAD, 2, dtype=jnp.float32)
            inv_freq = 1.0 / 10000.0 ** (half_idx / DIM_HEAD)
            t = jnp.arange(n, dtype=jnp.float32)
            freqs = t[:, None] * inv_freq[None, :]
            freqs = jnp.concatenate([freqs, freqs], axis=-1)
            base = (half_idx + 0.4 * DIM_HEAD) / (1.4 * DIM_HEAD)
            power = (t - n // 2) / float(WINDOW // 2)
            scale = base[None, :] ** power[:, None]
            scale = jnp.concatenate([scale, scale], axis=-1)
            cos, sin = (jnp.cos(freqs), jnp.sin(freqs))
            q = q * cos * scale + rotate_half(q) * sin * scale
            k = k * cos / scale + rotate_half(k) * sin / scale
            return (q, k)

        def local_attention(q, k, v):
            b, h, n, d = q.shape
            w = n // WINDOW
            bq = q.reshape(b, h, w, WINDOW, d) * QK_SCALE
            bk = k.reshape(b, h, w, WINDOW, d)
            bv = v.reshape(b, h, w, WINDOW, d)

            def look_around(t):
                p = jnp.pad(t, ((0, 0), (0, 0), (1, 0), (0, 0), (0, 0)))
                return jnp.concatenate([p[:, :, :w], p[:, :, 1:]], axis=3)
            bk, bv = (look_around(bk), look_around(bv))
            bt = jnp.arange(n).reshape(w, WINDOW)
            btp = jnp.pad(bt, ((1, 0), (0, 0)), constant_values=-1)
            btk = jnp.concatenate([btp[:w], btp[1:]], axis=1)
            sim = jnp.einsum('bhwid,bhwjd->bhwij', bq, bk)
            i = bt[:, :, None]
            j = btk[:, None, :]
            mask = (i < j) | (i > j + WINDOW) | (j == -1)
            sim = jnp.where(mask, -jnp.finfo(sim.dtype).max, sim)
            attn = jax.nn.softmax(sim, axis=-1)
            out = jnp.einsum('bhwij,bhwjd->bhwid', attn, bv)
            return out.reshape(b, h, n, d)

        def _layer(x, wqkv, qs, ksc, wo, lg, lb, w1, b1, w2, b2):
            b, n, _ = x.shape
            h = shift_token(x)
            qkv = h @ wqkv
            q, k, v = jnp.split(qkv, 3, axis=-1)
            to_heads = lambda t: t.reshape(b, n, HEADS, DIM_HEAD).transpose(0, 2, 1, 3)
            q, k, v = (to_heads(q), to_heads(k), to_heads(v))
            q = l2norm(q) * qs
            k = l2norm(k) * ksc
            q, k = rotary_xpos(q, k)
            o = local_attention(q, k, v)
            o = o.transpose(0, 2, 1, 3).reshape(b, n, INNER)
            x = x + o @ wo
            h = shift_token(x)
            mu = h.mean(-1, keepdims=True)
            var = h.var(-1, keepdims=True)
            h = (h - mu) / jnp.sqrt(var + 1e-05) * lg + lb
            h = h @ w1 + b1
            a, g = jnp.split(h, 2, axis=-1)
            h = a * jax.nn.gelu(g, approximate=False)
            x = x + h @ w2 + b2
            return x
        for l in range(DEPTH):
            x = _layer(x, wqkv[l], q_scale[l], k_scale[l], wo[l], ln_g[l], ln_b[l], w1[l], b1[l], w2[l], b2[l])
        return x
    x = L0_attn_x
    x = x + _L0_attn_ref(_layernorm(x, axis=-1), L0_attn_ln_w, L0_attn_ln_b, L0_attn_sign_W, L0_attn_sign_b, L0_attn_perm_W, L0_attn_perm_b, L0_attn_gate_W, L0_attn_gate_b, L0_attn_in_W, L0_attn_in_b, L0_attn_out_W, L0_attn_out_b)
    x = x + _L0_ffn_ref(_layernorm(x, axis=-1), L0_ffn_w_gate, L0_ffn_w_up, L0_ffn_w_down)
    x = x + _L1_attn_ref(_layernorm(x, axis=-1), L1_attn_w_in, L1_attn_b_in, L1_attn_w_out, L1_attn_b_out)
    x = x + _L1_ffn_ref(_layernorm(x, axis=-1), L1_ffn_weight, L1_ffn_bias)
    x = x + _L2_attn_ref(_layernorm(x, axis=-1), L2_attn_in_proj_w, L2_attn_conv_w, L2_attn_conv_b, L2_attn_x_proj_w, L2_attn_dt_proj_w, L2_attn_dt_proj_b, L2_attn_A_log, L2_attn_D, L2_attn_out_proj_w, L2_attn_U_param, L2_attn_V_param, L2_attn_low_rank_scale)
    x = x + _L2_ffn_ref(_layernorm(x, axis=-1), L2_ffn_router_w, L2_ffn_gate_w, L2_ffn_gate_b, L2_ffn_up_w, L2_ffn_up_b, L2_ffn_down_w, L2_ffn_down_b)
    x = x + _L3_attn_ref(_layernorm(x, axis=-1), L3_attn_in_proj_w, L3_attn_conv_w, L3_attn_conv_b, L3_attn_x_proj_w, L3_attn_dt_proj_w, L3_attn_dt_proj_b, L3_attn_A_log, L3_attn_D, L3_attn_out_proj_w, L3_attn_ln_w, L3_attn_ln_b)
    x = x + _L3_ffn_ref(_layernorm(x, axis=-1), L3_ffn_wqkv, L3_ffn_q_scale, L3_ffn_k_scale, L3_ffn_wo, L3_ffn_ln_g, L3_ffn_ln_b, L3_ffn_w1, L3_ffn_b1, L3_ffn_w2, L3_ffn_b2)
    return x

_drawn_inputs = setup_inputs


def setup_inputs(seed=0):
    import zlib

    import numpy as np

    out = dict(_drawn_inputs(seed))
    spreads = {'L0_attn_ln_w': (1.0, 0.2),
     'L0_attn_ln_b': (0.0, 0.1),
     'L0_attn_sign_b': (0.0, 0.1),
     'L0_attn_perm_b': (0.0, 0.1),
     'L0_attn_gate_b': (2.0, 0.2),
     'L0_attn_in_b': (0.0, 0.1),
     'L0_attn_out_b': (0.0, 0.1),
     'L1_attn_b_in': (0.0, 0.1),
     'L1_attn_b_out': (0.0, 0.1),
     'L2_attn_D': (1.0, 0.2),
     'L2_ffn_gate_b': (0.0, 0.1),
     'L2_ffn_up_b': (0.0, 0.1),
     'L2_ffn_down_b': (0.0, 0.1),
     'L3_attn_conv_b': (0.0, 0.1),
     'L3_attn_D': (1.0, 0.2),
     'L3_attn_ln_w': (1.0, 0.2),
     'L3_attn_ln_b': (0.0, 0.1),
     'L3_ffn_q_scale': (1.0, 0.2),
     'L3_ffn_k_scale': (1.0, 0.2),
     'L3_ffn_ln_g': (1.0, 0.2),
     'L3_ffn_ln_b': (0.0, 0.1),
     'L3_ffn_b1': (0.0, 0.1),
     'L3_ffn_b2': (0.0, 0.1)}
    factors = {}
    for name, (base, spread) in spreads.items():
        noise = np.random.default_rng([zlib.crc32(name.encode()), seed]).standard_normal(out[name].shape)
        drawn = base * np.exp(spread * noise) if base else spread * noise
        out[name] = jnp.asarray(drawn.astype(out[name].dtype))
    for name, factor in factors.items():
        out[name] = (out[name] * factor).astype(out[name].dtype)
    return out
```

```python
from contextlib import ExitStack, contextmanager

import numpy as np
import concourse.bass as bass
from concourse import mybir

F32 = mybir.dt.float32
I32 = mybir.dt.int32
BF16 = mybir.dt.bfloat16
ALU = mybir.AluOpType
ACT = mybir.ActivationFunctionType
X = mybir.AxisListType.X

P = 128
BATCH, SEQ = 16, 256
T = BATCH * SEQ
G = 512
NG = T // G
EPS = 1e-5
MASKED = -1e30


@contextmanager
def semaphore(nc, name):
    s = nc.alloc_semaphore(name)
    yield s
    nc.gpsimd.sem_clear(s)
    nc.release_semaphore(s)


class Steps:

    LEAD = 2

    def __init__(self, ctx, nc, name, steps, loops=1):
        self.sem = ctx.enter_context(semaphore(nc, name))
        self.names = {s: n for n, s in enumerate(steps)}
        assert len(self.names) == len(steps)
        self.n = len(steps)
        self.order = list(steps)
        self.said = 0

    def credit(self, eng):
        eng.sem_inc(self.sem, self.LEAD * self.n)

    def step(self, name):
        assert self.order[self.said % self.n] == name, (self.order[self.said % self.n], name)
        self.said += 1
        return 1

    def done(self):
        assert self.said == self.n, (self.said, self.n)

    def at(self, i, name, back=0):
        assert 0 <= back <= self.LEAD
        return i * self.n + (self.LEAD - back) * self.n + self.names[name] + 1

    def last(self, loops):
        return (loops + self.LEAD) * self.n


def open_tools(ctx, nc, block_name=""):
    def sb(name, shape, dt=F32):
        return ctx.enter_context(nc.sbuf_tensor(name, shape, dt))

    def ps(name, shape, dt=F32):
        return ctx.enter_context(nc.psum_tensor(name, shape, dt))

    def sem(name):
        return ctx.enter_context(semaphore(nc, name))

    return sb, ps, sem


def load_tiles(nc, name, pairs):
    with ExitStack() as ctx:
        loaded = ctx.enter_context(semaphore(nc, f"{name}_loaded"))
        block = ctx.enter_context(nc.Block())

        @block.sync
        def _(sp):
            for dst, src in pairs[0::2]:
                sp.dma_start(dst, src).then_inc(loaded, 16)
            sp.wait_ge(loaded, 16 * len(pairs))

        @block.scalar
        def _(act):
            for dst, src in pairs[1::2]:
                act.dma_start(dst, src).then_inc(loaded, 16)


def layernorm(nc, name, src, dst, C, gain=None, shift=None, tokens=T):
    with ExitStack() as ctx:
        sb, ps, sem = open_tools(ctx, nc)
        sq = sb(f"{name}_sq", [P, 2, G])
        rstd = sb(f"{name}_rstd", [P, 2, G])
        mean_ps = ps(f"{name}_mean", [P, 2, G])
        var_ps = ps(f"{name}_var", [P, 2, G])
        LOOPS = tokens // G // 2
        two = (0, 1)
        PE = Steps(ctx, nc, f"{name}_pe", [("mean", j) for j in two] + [("var", j) for j in two])
        AC = Steps(ctx, nc, f"{name}_act", [("square", j) for j in two] + [(s, j) for j in two for s in ("ln", "rstd")])
        VE = Steps(ctx, nc, f"{name}_dve", [("center", j) for j in two] + [("scale", j) for j in two]
                   + ([("affine", j) for j in two] if gain is not None else []))
        block = ctx.enter_context(nc.Block())

        @block.tensor
        def _(pe):
            PE.credit(pe)
            with pe.Fori(0, LOOPS) as i:
                for j in two:
                    pe.wait_ge(VE.sem, VE.at(i, ("center", j), 1))
                    nc.tensor.matmul(mean_ps[:, j, :], C.mean[:], src[:, bass.ds(i * (2 * G) + j * G, G)],
                                     start=True, stop=True).then_inc(PE.sem, PE.step(("mean", j)))
                for j in two:
                    pe.wait_ge(AC.sem, AC.at(i, ("square", j)))
                    nc.tensor.matmul(var_ps[:, j, :], C.mean[:], sq[:, j, :], start=True, stop=True)\
                        .then_inc(PE.sem, PE.step(("var", j)))
            PE.done()

        @block.scalar
        def _(act):
            AC.credit(act)
            act.preload_act_table_set("natural_log_exp_and_others")
            with act.Fori(0, LOOPS) as i:
                for j in two:
                    act.wait_ge(VE.sem, VE.at(i, ("center", j)))
                    act.wait_ge(PE.sem, PE.at(i, ("var", j), 1))
                    nc.scalar.activation(sq[:, j, :], dst[:, bass.ds(i * (2 * G) + j * G, G)], ACT.Square)\
                        .then_inc(AC.sem, AC.step(("square", j)))
                for j in two:
                    act.wait_ge(PE.sem, PE.at(i, ("var", j)))
                    act.wait_ge(VE.sem, VE.at(i, ("scale", j), 1))
                    nc.scalar.activation(rstd[:, j, :], var_ps[:, j, :], ACT.Ln, bias=C.eps[:])\
                        .then_inc(AC.sem, AC.step(("ln", j)))
                    act.wait_ge(AC.sem, AC.at(i, ("ln", j)))
                    nc.scalar.activation(rstd[:, j, :], rstd[:, j, :], ACT.Exp, scale=-0.5)\
                        .then_inc(AC.sem, AC.step(("rstd", j)))
            AC.done()

        @block.vector
        def _(dve):
            VE.credit(dve)
            with dve.Fori(0, LOOPS) as i:
                at = [bass.ds(i * (2 * G) + j * G, G) for j in two]
                for j in two:
                    dve.wait_ge(PE.sem, PE.at(i, ("mean", j)))
                    nc.vector.tensor_tensor(dst[:, at[j]], src[:, at[j]], mean_ps[:, j, :], ALU.subtract)\
                        .then_inc(VE.sem, VE.step(("center", j)))
                for j in two:
                    dve.wait_ge(AC.sem, AC.at(i, ("rstd", j)))
                    dve.wait_ge(VE.sem, VE.at(i, ("center", j)))
                    nc.vector.tensor_tensor(dst[:, at[j]], dst[:, at[j]], rstd[:, j, :], ALU.mult)\
                        .then_inc(VE.sem, VE.step(("scale", j)))
                if gain is not None:
                    for j in two:
                        dve.wait_ge(VE.sem, VE.at(i, ("scale", j)))
                        nc.vector.tensor_scalar(dst[:, at[j]], dst[:, at[j]], gain, shift, ALU.mult, ALU.add)\
                            .then_inc(VE.sem, VE.step(("affine", j)))
            VE.done()


def residual_add(nc, name, x, y):
    with ExitStack() as ctx:
        block = ctx.enter_context(nc.Block())

        @block.vector
        def _(dve):
            nc.vector.tensor_tensor(x[:, 0:T * 5 // 8], x[:, 0:T * 5 // 8], y[:, 0:T * 5 // 8], ALU.add)

        @block.gpsimd
        def _(pool):
            nc.gpsimd.tensor_tensor(x[:, T * 5 // 8:T], x[:, T * 5 // 8:T], y[:, T * 5 // 8:T], ALU.add)


def gated_ffn(nc, name, res, src, gate_w, up_w, down_w, sizes, func, C, gate_b=None, up_b=None, down_b=None):
    with ExitStack() as ctx:
        sb, ps, sem = open_tools(ctx, nc)
        HC = len(sizes)
        hid = sb(f"{name}_hid", [P, 2, G])
        sg = sb(f"{name}_sg", [P, 2, G])
        gate_ps = ps(f"{name}_gate", [P, 2, G])
        up_ps = ps(f"{name}_up", [P, 2, G])
        out_ps = ps(f"{name}_out", [P, G])
        U = range(2 * HC)
        n = len(U)
        PE = Steps(ctx, nc, f"{name}_pe", ["gateup0", "gateup1"] + [s for u in U for s in
                   (["gateup%d" % (u + 2)] if u + 2 in U else []) + ["down%d" % u]])
        AC = Steps(ctx, nc, f"{name}_act", ["func%d" % u for u in U])
        VE = Steps(ctx, nc, f"{name}_dve", [s for u in U for s in ["hid%d" % u] + (["out%d" % u] if u % HC == HC - 1 else [])])
        block = ctx.enter_context(nc.Block())

        @block.tensor
        def _(pe):
            PE.credit(pe)

            def gate_up(i, u):
                g, c = divmod(u, HC)
                k = sizes[c]
                at = bass.ds(i * (2 * G) + g * G, G)
                pe.wait_ge(VE.sem, VE.at(i, "hid%d" % ((u - 2) % n), 0 if u >= 2 else 1))
                nc.tensor.matmul(gate_ps[:k, u % 2, :], gate_w[:, c * P:c * P + k], src[:, at], start=True, stop=True)
                nc.tensor.matmul(up_ps[:k, u % 2, :], up_w[:, c * P:c * P + k], src[:, at], start=True, stop=True)\
                    .then_inc(PE.sem, PE.step("gateup%d" % u))

            with pe.Fori(0, NG // 2) as i:
                gate_up(i, 0)
                gate_up(i, 1)
                for u in U:
                    if u + 2 in U:
                        gate_up(i, u + 2)
                    c = u % HC
                    k = sizes[c]
                    pe.wait_ge(VE.sem, VE.at(i, "hid%d" % u))
                    if c == 0:
                        pe.wait_ge(VE.sem, VE.at(i, "out%d" % ((u - 1) % n), 0 if u else 1))
                    nc.tensor.matmul(out_ps[:], down_w[:k, c, :], hid[:k, u % 2, :],
                                     start=c == 0, stop=c == HC - 1).then_inc(PE.sem, PE.step("down%d" % u))
            PE.done()

        @block.scalar
        def _(act):
            AC.credit(act)
            act.preload_act_table(func)
            with act.Fori(0, NG // 2) as i:
                for u in U:
                    k = sizes[u % HC]
                    act.wait_ge(PE.sem, PE.at(i, "gateup%d" % u))
                    act.wait_ge(VE.sem, VE.at(i, "hid%d" % ((u - 2) % n), 0 if u >= 2 else 1))
                    bias = {} if gate_b is None else {"bias": gate_b[:k, u % HC:u % HC + 1]}
                    nc.scalar.activation(sg[:k, u % 2, :], gate_ps[:k, u % 2, :], func, **bias)\
                        .then_inc(AC.sem, AC.step("func%d" % u))
            AC.done()

        @block.vector
        def _(dve):
            VE.credit(dve)
            with dve.Fori(0, NG // 2) as i:
                for u in U:
                    g, c = divmod(u, HC)
                    k = sizes[c]
                    dve.wait_ge(AC.sem, AC.at(i, "func%d" % u))
                    dve.wait_ge(PE.sem, PE.at(i, "down%d" % ((u - 2) % n), 0 if u >= 2 else 1))
                    h, up, s = hid[:k, u % 2, :], up_ps[:k, u % 2, :], sg[:k, u % 2, :]
                    if up_b is None:
                        ins = nc.vector.tensor_tensor(h, up, s, ALU.mult)
                    else:
                        ins = nc.vector.scalar_tensor_tensor(h, up, up_b[:k, c:c + 1], s, ALU.add, ALU.mult)
                    ins.then_inc(VE.sem, VE.step("hid%d" % u))
                    if c == HC - 1:
                        at = bass.ds(i * (2 * G) + g * G, G)
                        dve.wait_ge(PE.sem, PE.at(i, "down%d" % u))
                        if down_b is None:
                            ins = nc.vector.tensor_tensor(res[:, at], res[:, at], out_ps[:], ALU.add)
                        else:
                            ins = nc.vector.scalar_tensor_tensor(res[:, at], out_ps[:], down_b, res[:, at], ALU.add, ALU.add)
                        ins.then_inc(VE.sem, VE.step("out%d" % u))
            VE.done()


def int8_swiglu(nc, x, z, w, C):
    with ExitStack() as stage:
        sb, ps, sem = open_tools(stage, nc)
        HC = w["L0_ffn_w_gate"].shape[1] // P
        wi = sb("q_wi", [P, 3, HC * P], I32)
        wf = sb("q_wf", [P, 3, HC * P])
        load_tiles(nc, "q", [(wi[:, 0, :], w["L0_ffn_w_gate"]), (wi[:, 1, :], w["L0_ffn_w_up"]),
                             (wi[:, 2, :].rearrange("p (c n) -> p c n", c=HC),
                              w["L0_ffn_w_down"].rearrange("(c p) n -> p c n", p=P))])
        with ExitStack() as ctx:
            block = ctx.enter_context(nc.Block())

            @block.scalar
            def _(act):
                nc.scalar.activation(wf[:], wi[:], ACT.Copy, scale=1.0 / 127.0)

        gated_ffn(nc, "q", x, z, wf[:, 0, :], wf[:, 1, :], wf[:, 2, :].rearrange("p (c n) -> p c n", c=HC),
                  [P] * HC, ACT.Silu, C)


def selector(nc, stage, name, w, N):
    sel = stage.enter_context(nc.sbuf_tensor(f"{name}_sel", [96, 2 * N, P], BF16))
    with ExitStack() as ctx:
        wide = ctx.enter_context(nc.sbuf_tensor(f"{name}_sel32", [96, 2 * N, P], F32))
        load_tiles(nc, f"{name}_sel", [(wide[:], w[f"c_sel{2 * N}"])])
        block = ctx.enter_context(nc.Block())

        @block.vector
        def _(dve):
            nc.vector.tensor_copy(sel[:], wide[:])
    return sel


def mamba(nc, name, src, res, w, C, sel, N, low_rank=False):
    H = 2
    R = 8
    NSEQ = G // SEQ
    CH = N // 2
    KN = 2 * N
    with ExitStack() as stage:
        sb, ps, sem = open_tools(stage, nc)
        in_w = sb(f"{name}_in_w", [P, 2 * H, P])
        conv_w = sb(f"{name}_conv_w", [P, H, 4])
        col = sb(f"{name}_col", [P, 3, H])
        conv_b, dt_b, skip = col[:, 0, :], col[:, 1, :], col[:, 2, :]
        xp_w = sb(f"{name}_xp_w", [P, H, R + 96])
        dt_w = sb(f"{name}_dt_w", [R, H, P])
        a_log = sb(f"{name}_a_log", [P, H, N])
        decay = sb(f"{name}_decay", [P, H, N])
        out_w = sb(f"{name}_out_w", [P, H, P])
        u = sb(f"{name}_u", [P, H, T])
        sz = sb(f"{name}_sz", [P, H, T])
        delta = sb(f"{name}_delta", [P, H, T])
        bc = sb(f"{name}_bc", [96, T], BF16)
        pairs = [(in_w[:], w[f"{name}_in_w"]), (conv_w[:], w[f"{name}_conv_w"]), (col[:], w[f"{name}_col"]),
                 (xp_w[:], w[f"{name}_xp_w"]), (dt_w[:], w[f"{name}_dt_w"]), (a_log[:], w[f"{name}_a_log"]),
                 (out_w[:], w[f"{name}_out_w"])]
        if low_rank:
            u_t = sb(f"{name}_ut", [R, H, P])
            v_w = sb(f"{name}_v", [R, N])
            lrs = sb(f"{name}_lrs", [P, 1])
            pairs += [(u_t[:], w[f"{name}_ut"]), (v_w[:], w[f"{name}_v"]), (lrs[:], w[f"{name}_lrs"])]
        load_tiles(nc, name, pairs)

        with ExitStack() as ctx:
            sb, ps, sem = open_tools(ctx, nc)
            conv = sb(f"{name}_conv", [P, H, G])
            in_ps = ps(f"{name}_inps", [P, 2 * H, G])
            PE = Steps(ctx, nc, f"{name}_a_pe", [("in", c) for c in range(4)])
            AC = Steps(ctx, nc, f"{name}_a_act", [("silu", c) for c in (2, 3, 0, 1)])
            VE = Steps(ctx, nc, f"{name}_a_dve", [("tap", h, k) for h in range(H) for k in range(4)])
            block = ctx.enter_context(nc.Block())

            @block.tensor
            def _(pe):
                PE.credit(pe)
                with pe.Fori(0, NG) as i:
                    for c in range(4):
                        if c < H:
                            pe.wait_ge(VE.sem, VE.at(i, ("tap", c, 3), 1))
                        else:
                            pe.wait_ge(AC.sem, AC.at(i, ("silu", c), 1))
                        nc.tensor.matmul(in_ps[:, c, :], in_w[:, c, :], src[:, bass.ds(i * G, G)],
                                         start=True, stop=True).then_inc(PE.sem, PE.step(("in", c)))
                PE.done()

            @block.vector
            def _(dve):
                VE.credit(dve)
                with dve.Fori(0, NG) as i:
                    for h in range(H):
                        xin = in_ps[:, h, :].rearrange("p (b t) -> p b t", b=NSEQ)
                        acc = conv[:, h, :].rearrange("p (b t) -> p b t", b=NSEQ)
                        dve.wait_ge(PE.sem, PE.at(i, ("in", h)))
                        dve.wait_ge(AC.sem, AC.at(i, ("silu", h), 1))
                        nc.vector.tensor_scalar(acc, xin, conv_w[:, h, 3:4], None, ALU.mult)\
                            .then_inc(VE.sem, VE.step(("tap", h, 0)))
                        for k in range(1, 4):
                            dve.wait_ge(VE.sem, VE.at(i, ("tap", h, k - 1)))
                            nc.vector.scalar_tensor_tensor(acc[:, :, k:], xin[:, :, :SEQ - k], conv_w[:, h, 3 - k:4 - k],
                                                           acc[:, :, k:], ALU.mult, ALU.add)\
                                .then_inc(VE.sem, VE.step(("tap", h, k)))
                VE.done()

            @block.scalar
            def _(act):
                AC.credit(act)
                act.preload_act_table(ACT.Silu)
                with act.Fori(0, NG) as i:
                    for c in (2, 3):
                        act.wait_ge(PE.sem, PE.at(i, ("in", c)))
                        nc.scalar.activation(sz[:, c - H, bass.ds(i * G, G)], in_ps[:, c, :], ACT.Silu)\
                            .then_inc(AC.sem, AC.step(("silu", c)))
                    for h in range(H):
                        act.wait_ge(VE.sem, VE.at(i, ("tap", h, 3)))
                        nc.scalar.activation(u[:, h, bass.ds(i * G, G)], conv[:, h, :], ACT.Silu, bias=conv_b[:, h:h + 1])\
                            .then_inc(AC.sem, AC.step(("silu", h)))
                AC.done()

        with ExitStack() as ctx:
            sb, ps, sem = open_tools(ctx, nc)
            dt_low = sb(f"{name}_dt_low", [R, G])
            mag = sb(f"{name}_mag", [P, H, G])
            pos = sb(f"{name}_pos", [P, H, G])
            low_ps = ps(f"{name}_low", [R, G])
            bc_ps = ps(f"{name}_bcps", [96, G])
            rest = sb(f"{name}_rest", [96, G])
            mid = sb(f"{name}_mid", [96, G], BF16)
            dt_ps = ps(f"{name}_dtps", [P, H, G])
            PE = Steps(ctx, nc, f"{name}_b_pe", ["low", "bc", ("dt", 0), ("dt", 1)])
            AC = Steps(ctx, nc, f"{name}_b_act", ["low", "bc", "bc_mid"] + [(s, h) for h in range(H) for s in ("abs", "exp", "ln")])
            VE = Steps(ctx, nc, f"{name}_b_dve", ["rest", "bc_low"] + [(s, h) for h in range(H) for s in ("pos", "delta")])
            rank_done = sem(f"{name}_rank")
            rates = sem(f"{name}_rates")
            block = ctx.enter_context(nc.Block())

            @block.tensor
            def _(pe):
                PE.credit(pe)
                if low_rank:
                    for h in range(H):
                        mm = nc.tensor.matmul(dt_ps[:, h, 0:N], u_t[:, h, :], v_w[:], start=True, stop=True)
                    mm.then_inc(rank_done, 1)
                    pe.wait_ge(rates, 2)
                with pe.Fori(0, NG) as i:
                    at = bass.ds(i * G, G)
                    pe.wait_ge(AC.sem, AC.at(i, "low", 1))
                    for h in range(H):
                        mm = nc.tensor.matmul(low_ps[:], xp_w[:, h, 0:R], u[:, h, at], start=h == 0, stop=h == H - 1)
                    mm.then_inc(PE.sem, PE.step("low"))
                    pe.wait_ge(AC.sem, AC.at(i, "bc", 1))
                    pe.wait_ge(VE.sem, VE.at(i, "rest", 1))
                    for h in range(H):
                        mm = nc.tensor.matmul(bc_ps[:], xp_w[:, h, R:], u[:, h, at], start=h == 0, stop=h == H - 1)
                    mm.then_inc(PE.sem, PE.step("bc"))
                    pe.wait_ge(AC.sem, AC.at(i, "low"))
                    for h in range(H):
                        pe.wait_ge(AC.sem, AC.at(i, ("abs", h), 1))
                        pe.wait_ge(VE.sem, VE.at(i, ("pos", h), 1))
                        nc.tensor.matmul(dt_ps[:, h, :], dt_w[:, h, :], dt_low[:], start=True, stop=True)\
                            .then_inc(PE.sem, PE.step(("dt", h)))
                PE.done()

            @block.scalar
            def _(act):
                AC.credit(act)
                act.preload_act_table_set("natural_log_exp_and_others")
                nc.scalar.activation(decay[:], a_log[:], ACT.Exp).then_inc(rates, 1)
                with act.Fori(0, NG) as i:
                    act.wait_ge(PE.sem, PE.at(i, "low"))
                    act.wait_ge(PE.sem, PE.at(i, ("dt", 1), 1))
                    nc.scalar.activation(dt_low[:], low_ps[:], ACT.Copy).then_inc(AC.sem, AC.step("low"))
                    act.wait_ge(PE.sem, PE.at(i, "bc"))
                    at = bass.ds(i * G, G)
                    nc.scalar.activation(bc[:, at], bc_ps[:], ACT.Copy).then_inc(AC.sem, AC.step("bc"))
                    act.wait_ge(VE.sem, VE.at(i, "rest"))
                    nc.scalar.activation(bc[32:64, at], rest[32:64, :], ACT.Copy)
                    nc.scalar.activation(mid[64:96, :], rest[64:96, :], ACT.Copy).then_inc(AC.sem, AC.step("bc_mid"))
                    for h in range(H):
                        act.wait_ge(PE.sem, PE.at(i, ("dt", h)))
                        act.wait_ge(VE.sem, VE.at(i, ("delta", h), 1))
                        nc.scalar.activation(mag[:, h, :], dt_ps[:, h, :], ACT.Abs, bias=dt_b[:, h:h + 1])\
                            .then_inc(AC.sem, AC.step(("abs", h)))
                        act.wait_ge(AC.sem, AC.at(i, ("abs", h)))
                        nc.scalar.activation(mag[:, h, :], mag[:, h, :], ACT.Exp, scale=-1.0)\
                            .then_inc(AC.sem, AC.step(("exp", h)))
                        act.wait_ge(AC.sem, AC.at(i, ("exp", h)))
                        nc.scalar.activation(mag[:, h, :], mag[:, h, :], ACT.Ln, bias=C.one[:])\
                            .then_inc(AC.sem, AC.step(("ln", h)))
                AC.done()

            @block.vector
            def _(dve):
                VE.credit(dve)
                dve.wait_ge(rates, 1)
                if low_rank:
                    dve.wait_ge(rank_done, 1)
                    nc.vector.tensor_scalar(a_log[:], dt_ps[:, :, 0:N], lrs[:], float(R) ** -0.5, ALU.mult, ALU.mult)\
                        .then_inc(rates, 1)
                    dve.wait_ge(rates, 2)
                    nc.vector.tensor_tensor(decay[:], a_log[:], decay[:], ALU.subtract)
                else:
                    nc.vector.tensor_scalar(decay[:], decay[:], -1.0, None, ALU.mult)
                with dve.Fori(0, NG) as i:
                    at = bass.ds(i * G, G)
                    dve.wait_ge(AC.sem, AC.at(i, "bc"))
                    nc.vector.tensor_tensor(rest[:], bc_ps[:], bc[:, at], ALU.subtract).then_inc(VE.sem, VE.step("rest"))
                    dve.wait_ge(AC.sem, AC.at(i, "bc_mid"))
                    dve.wait_ge(VE.sem, VE.at(i, "rest"))
                    nc.vector.tensor_tensor(bc[64:96, at], rest[64:96, :], mid[64:96, :], ALU.subtract)\
                        .then_inc(VE.sem, VE.step("bc_low"))
                    for h in range(H):
                        dve.wait_ge(AC.sem, AC.at(i, ("abs", h)))
                        nc.vector.tensor_scalar(pos[:, h, :], dt_ps[:, h, :], dt_b[:, h:h + 1], 0.0, ALU.add, ALU.max)\
                            .then_inc(VE.sem, VE.step(("pos", h)))
                        dve.wait_ge(VE.sem, VE.at(i, ("pos", h)))
                        dve.wait_ge(AC.sem, AC.at(i, ("ln", h)))
                        nc.vector.tensor_tensor(delta[:, h, bass.ds(i * G, G)], pos[:, h, :], mag[:, h, :], ALU.add)\
                            .then_inc(VE.sem, VE.step(("delta", h)))
                VE.done()

        with ExitStack() as ctx:
            sb, ps, sem = open_tools(ctx, nc)
            dA = sb(f"{name}_dA", [P, 2, H, 2, G])
            inp = sb(f"{name}_inp", [P, H, 2, G])
            hs = sb(f"{name}_hs", [P, 2, H, 2, G])
            cb = sb(f"{name}_cb", [P, 2, 2, G])
            du = sb(f"{name}_du", [P, H, G])
            y = delta
            b_ps = ps(f"{name}_bps", [P, 2, G])
            c_ps = ps(f"{name}_cps", [P, 2, G])
            y_ps = ps(f"{name}_yps", [P, H, G])
            o_ps = ps(f"{name}_ops", [P, G])
            CS, HS = range(CH), range(H)
            PE = Steps(ctx, nc, f"{name}_c_pe",
                       [("bcast", c) for c in (0,)] + [s for c in CS for s in ([("bcast", c + 1)] if c + 1 < CH else [])
                        + [("sum", c, h) for h in HS]] + ["out"])
            AC = Steps(ctx, nc, f"{name}_c_act", [s for c in CS for s in [("decay", c, h) for h in HS] + [("c", c)]])
            VE = Steps(ctx, nc, f"{name}_c_dve", [s for c in CS for s in [("in", c, h) for h in HS] + [("scan", c, h) for h in HS]]
                       + [(s, h) for h in HS for s in ("skip", "gate")] + ["res"])
            PO = Steps(ctx, nc, f"{name}_c_pool", [("du", h) for h in HS] + [("hc", c, h) for c in CS for h in HS])
            zeros = sem(f"{name}_zeros")
            decays_begun = sem(f"{name}_decays_begun")
            block = ctx.enter_context(nc.Block())

            @block.gpsimd
            def _(pool):
                PO.credit(pool)
                nc.gpsimd.memset(dA[:], 0.0).then_inc(zeros, 1)
                with pool.Fori(0, NG) as i:
                    at = bass.ds(i * G, G)
                    for h in HS:
                        pool.wait_ge(VE.sem, VE.at(i, ("in", CH - 1, h), 1))
                        nc.gpsimd.tensor_tensor(du[:, h, :], delta[:, h, at], u[:, h, at], ALU.mult)\
                            .then_inc(PO.sem, PO.step(("du", h)))
                    for c in CS:
                        pool.wait_ge(AC.sem, AC.at(i, ("c", c)))
                        for h in HS:
                            pool.wait_ge(VE.sem, VE.at(i, ("scan", c, h)))
                            nc.gpsimd.tensor_tensor(hs[:, c % 2, h], hs[:, c % 2, h], cb[:, c % 2], ALU.mult)\
                                .then_inc(PO.sem, PO.step(("hc", c, h)))
                PO.done()

            @block.tensor
            def _(pe):
                PE.credit(pe)

                def bcast(i, c):
                    at = bass.ds(i * G, G)
                    for s in range(2):
                        n = 2 * c + s
                        if s == 0:
                            pe.wait_ge(VE.sem, VE.at(i, ("in", (c - 1) % CH, 1), 0 if c else 1))
                        nc.tensor.matmul(b_ps[:, s, :], sel[:, n, :], bc[:, at], start=True, stop=True)
                        if s == 0:
                            pe.wait_ge(AC.sem, AC.at(i, ("c", (c - 1) % CH), 0 if c else 1))
                        mm = nc.tensor.matmul(c_ps[:, s, :], sel[:, N + n, :], bc[:, at], start=True, stop=True)
                    mm.then_inc(PE.sem, PE.step(("bcast", c)))

                with pe.Fori(0, NG) as i:
                    bcast(i, 0)
                    for c in CS:
                        if c + 1 < CH:
                            bcast(i, c + 1)
                        for h in HS:
                            pe.wait_ge(PO.sem, PO.at(i, ("hc", c, h)))
                            if c == 0:
                                pe.wait_ge(VE.sem, VE.at(i, ("skip", h), 1))
                            for s in range(2):
                                mm = nc.tensor.matmul(y_ps[:, h, :], C.ident[:], hs[:, c % 2, h, s, :],
                                                      start=c == 0 and s == 0, stop=c == CH - 1 and s == 1)
                            mm.then_inc(PE.sem, PE.step(("sum", c, h)))
                    at = bass.ds(i * G, G)
                    pe.wait_ge(VE.sem, VE.at(i, "res", 1))
                    for h in HS:
                        pe.wait_ge(VE.sem, VE.at(i, ("gate", h)))
                        mm = nc.tensor.matmul(o_ps[:], out_w[:, h, :], y[:, h, at], start=h == 0, stop=h == H - 1)
                    mm.then_inc(PE.sem, PE.step("out"))
                PE.done()

            @block.scalar
            def _(act):
                AC.credit(act)
                act.wait_ge(zeros, 1)
                act.preload_act_table_set("natural_log_exp_and_others")
                with act.Fori(0, NG) as i:
                    for c in CS:
                        for h in HS:
                            act.wait_ge(VE.sem, VE.at(i, ("scan", (c - 2) % CH, h), 0 if c >= 2 else 1))
                            act.sem_inc(decays_begun, 1)
                            for s in range(2):
                                dl = delta[:, h, bass.ds(i * G, G)].rearrange("p (b t) -> p b t", b=NSEQ)[:, :, 1:]
                                o = dA[:, c % 2, h, s, :].rearrange("p (b t) -> p b t", b=NSEQ)[:, :, 1:]
                                a = nc.scalar.activation(o, dl, ACT.Exp, scale=decay[:, h, 2 * c + s:2 * c + s + 1])
                            a.then_inc(AC.sem, AC.step(("decay", c, h)))
                        act.wait_ge(PE.sem, PE.at(i, ("bcast", c)))
                        act.wait_ge(PO.sem, PO.at(i, ("hc", (c - 2) % CH, 1), 0 if c >= 2 else 1))
                        nc.scalar.activation(cb[:, c % 2], c_ps[:], ACT.Copy).then_inc(AC.sem, AC.step(("c", c)))
                AC.done()

            @block.vector
            def _(dve):
                VE.credit(dve)
                with dve.Fori(0, NG) as i:
                    for c in CS:
                        dve.wait_ge(PE.sem, PE.at(i, ("bcast", c)))
                        for h in HS:
                            if c == 0:
                                dve.wait_ge(PO.sem, PO.at(i, ("du", h)))
                            dve.wait_ge(VE.sem, VE.at(i, ("scan", (c - 1) % CH, h), 0 if c else 1))
                            nc.vector.tensor_tensor(inp[:, h], b_ps[:], du[:, h:h + 1, :].to_broadcast([P, 2, G]), ALU.mult)\
                                .then_inc(VE.sem, VE.step(("in", c, h)))
                        for h in HS:
                            dve.wait_ge(VE.sem, VE.at(i, ("in", c, h)))
                            dve.wait_ge(AC.sem, AC.at(i, ("decay", c, h)))
                            dve.wait_ge(PE.sem, PE.at(i, ("sum", (c - 2) % CH, h), 0 if c >= 2 else 1))
                            nc.vector.tensor_tensor_scan(hs[:, c % 2, h].rearrange("p s t -> p (s t)"),
                                                         dA[:, c % 2, h].rearrange("p s t -> p (s t)"),
                                                         inp[:, h].rearrange("p s t -> p (s t)"), 0.0, ALU.mult, ALU.add)\
                                .then_inc(VE.sem, VE.step(("scan", c, h)))
                    at = bass.ds(i * G, G)
                    for h in HS:
                        dve.wait_ge(PE.sem, PE.at(i, ("sum", CH - 1, h)))
                        dve.wait_ge(PE.sem, PE.at(i, "out", 1))
                        nc.vector.scalar_tensor_tensor(y[:, h, at], u[:, h, at], skip[:, h:h + 1], y_ps[:, h, :], ALU.mult, ALU.add)\
                            .then_inc(VE.sem, VE.step(("skip", h)))
                        dve.wait_ge(VE.sem, VE.at(i, ("skip", h)))
                        nc.vector.tensor_tensor(y[:, h, at], y[:, h, at], sz[:, h, at], ALU.mult)\
                            .then_inc(VE.sem, VE.step(("gate", h)))
                    dve.wait_ge(PE.sem, PE.at(i, "out"))
                    nc.vector.tensor_tensor(res[:, at], res[:, at], o_ps[:], ALU.add).then_inc(VE.sem, VE.step("res"))
                VE.done()


def mamba_layer(nc, x, z, w, C):
    with ExitStack() as stage:
        mamba(nc, "m2", z, x, w, C, selector(nc, stage, "m2", w, 8), 8, low_rank=True)


def mamba_stack(nc, x, z, w, C):
    with ExitStack() as stage:
        sb, ps, sem = open_tools(stage, nc)
        ln = sb("m3_ln", [P, 2, 4])
        load_tiles(nc, "m3", [(ln[:], w["m3_ln"])])
        sel = selector(nc, stage, "m3", w, 16)
        for l in range(4):
            mamba(nc, f"m3{l}", z, z, w, C, sel, 16)
            layernorm(nc, f"m3{l}_post", z, z, C, ln[:, 0, l:l + 1], ln[:, 1, l:l + 1])
        residual_add(nc, "m3", x, z)


def mamba_layout(a, w):
    def halves(v):
        return v.reshape(2, P, -1).transpose(1, 0, 2)

    def one(name, in_w, conv_w, conv_b, xp, dtw, dtb, alog, D, ow):
        w[f"{name}_in_w"] = in_w.reshape(P, 4, P)
        w[f"{name}_conv_w"] = halves(conv_w)
        w[f"{name}_col"] = np.stack([conv_b.reshape(2, P).T, dtb.reshape(2, P).T, D.reshape(2, P).T], 1)
        bc = np.concatenate([xp[:, 8:], np.zeros((256, 32 - (xp.shape[1] - 8)), np.float32)], 1)
        w[f"{name}_xp_w"] = halves(np.concatenate([xp[:, :8], bc, bc, bc], 1))
        w[f"{name}_dt_w"] = dtw.reshape(8, 2, P)
        w[f"{name}_a_log"] = halves(alog)
        w[f"{name}_out_w"] = halves(ow)

    q = lambda k: a["L2_attn_" + k]
    one("m2", q("in_proj_w").T, q("conv_w"), q("conv_b"), q("x_proj_w").T, q("dt_proj_w").T, q("dt_proj_b"),
        q("A_log"), q("D"), q("out_proj_w").T)
    w["m2_ut"] = q("U_param").T.reshape(8, 2, P)
    w["m2_v"] = q("V_param")
    w["m2_lrs"] = np.broadcast_to(q("low_rank_scale").reshape(1, 1), (P, 1))
    q = lambda k: a["L3_attn_" + k]
    for l in range(4):
        one(f"m3{l}", *[q(k)[l] for k in ("in_proj_w", "conv_w", "conv_b", "x_proj_w", "dt_proj_w", "dt_proj_b",
                                          "A_log", "D", "out_proj_w")])
    w["m3_ln"] = np.stack([q("ln_w").T, q("ln_b").T], 1)


def selector_tables():
    return {f"c_sel{k}": np.repeat(np.tile(np.eye(32, k, dtype=np.float32), (3, 1))[:, :, None], P, 2)
            for k in (16, 32)}


def mx_linear(nc, x, z, w, C):
    BLK, TOP = 32, 7.5
    MAGIC = 1.5 * 2 ** 23
    NB = G // BLK
    QUANT = ["amax", "scale", "rscale", "ratio", "square", "ge2", "ge4", "step", "magic",
             "shifted", "rounded", "excess", "tie", "lower", "fixed", "value"]
    with ExitStack() as ctx:
        sb, ps, sem = open_tools(ctx, nc)
        wq = sb("mx_wq", [P, P])
        w_t = sb("mx_wt", [P, P])
        bias = sb("mx_bias", [P, 1])
        zs = sb("mx_zs", [P, G])
        xd_t = sb("mx_xdt", [P, G])
        amax, scale, rscale = (sb(f"mx_{n}", [P, NB]) for n in ("amax", "scale", "rscale"))
        ratio, ge2, ge4, step, magic, val, exc = (sb(f"mx_{n}", [P, G]) for n in
                                                  ("ratio", "ge2", "ge4", "step", "magic", "val", "exc"))
        t_ps = ps("mx_tps", [P, G])
        f_ps = ps("mx_fps", [P, G])
        o_ps = ps("mx_ops", [P, G])
        w_ps = ps("mx_wps", [P, P])
        load_tiles(nc, "mx", [(wq[:], w["L1_ffn_weight"]), (bias[:], w["mx_bias"])])
        PE = Steps(ctx, nc, "mx_pe", ["turn", "back", "out"])
        AC = Steps(ctx, nc, "mx_act", ["stage", "xd"])
        VE = Steps(ctx, nc, "mx_dve", QUANT + ["res"])
        WQ = Steps(ctx, nc, "mx_wq_steps", QUANT)
        w_turned = sem("mx_w_turned")
        w_ready = sem("mx_w_ready")
        block = ctx.enter_context(nc.Block())

        def quantise(dve, S, i, src, out, n):
            b = n // BLK

            def blocks(t):
                return t[:, :n].rearrange("p (b k) -> p b k", k=BLK)

            def wide(t):
                return t[:, :b].rearrange("p (b k) -> p b k", k=1).to_broadcast([P, b, BLK])

            def after(name):
                dve.wait_ge(S.sem, S.at(i, name))

            v = nc.vector
            v.tensor_reduce(amax[:, :b], blocks(src), X, ALU.max, apply_absolute_value=True)\
                .then_inc(S.sem, S.step("amax"))
            after("amax")
            v.tensor_scalar(scale[:, :b], amax[:, :b], 1.0 / TOP, 1e-30, ALU.mult, ALU.max)\
                .then_inc(S.sem, S.step("scale"))
            after("scale")
            v.reciprocal(rscale[:, :b], scale[:, :b]).then_inc(S.sem, S.step("rscale"))
            after("rscale")
            v.tensor_tensor(blocks(ratio), blocks(src), wide(rscale), ALU.mult).then_inc(S.sem, S.step("ratio"))
            after("ratio")
            if S is VE:
                dve.wait_ge(PE.sem, PE.at(i, "back", 1))
            v.tensor_tensor(exc[:, :n], ratio[:, :n], ratio[:, :n], ALU.mult).then_inc(S.sem, S.step("square"))
            after("square")
            v.tensor_scalar(ge2[:, :n], exc[:, :n], 4.0, 0.125, ALU.is_ge, ALU.mult).then_inc(S.sem, S.step("ge2"))
            v.tensor_scalar(ge4[:, :n], exc[:, :n], 16.0, 0.25, ALU.is_ge, ALU.mult).then_inc(S.sem, S.step("ge4"))
            after("ge4")
            v.scalar_tensor_tensor(step[:, :n], ge2[:, :n], 0.125, ge4[:, :n], ALU.add, ALU.add)\
                .then_inc(S.sem, S.step("step"))
            after("step")
            v.tensor_scalar(magic[:, :n], step[:, :n], MAGIC, None, ALU.mult).then_inc(S.sem, S.step("magic"))
            after("magic")
            v.tensor_tensor(val[:, :n], ratio[:, :n], magic[:, :n], ALU.add).then_inc(S.sem, S.step("shifted"))
            after("shifted")
            v.tensor_tensor(val[:, :n], val[:, :n], magic[:, :n], ALU.subtract).then_inc(S.sem, S.step("rounded"))
            after("rounded")
            v.tensor_tensor(exc[:, :n], val[:, :n], ratio[:, :n], ALU.subtract).then_inc(S.sem, S.step("excess"))
            after("excess")
            v.scalar_tensor_tensor(exc[:, :n], exc[:, :n], 2.0, step[:, :n], ALU.mult, ALU.is_ge)\
                .then_inc(S.sem, S.step("tie"))
            after("tie")
            v.tensor_tensor(exc[:, :n], exc[:, :n], step[:, :n], ALU.mult).then_inc(S.sem, S.step("lower"))
            after("lower")
            v.tensor_tensor(val[:, :n], val[:, :n], exc[:, :n], ALU.subtract).then_inc(S.sem, S.step("fixed"))
            after("fixed")
            v.tensor_tensor(blocks(out), blocks(val), wide(scale), ALU.mult).then_inc(S.sem, S.step("value"))
            after("value")

        @block.tensor
        def _(pe):
            PE.credit(pe)
            pe.wait_ge(WQ.sem, WQ.at(0, "value"))
            nc.tensor.transpose(w_ps[:], exc[:, :P], C.ident[:]).then_inc(w_turned, 1)
            pe.wait_ge(w_ready, 1)
            with pe.Fori(0, NG) as i:
                pe.wait_ge(AC.sem, AC.at(i, "stage"))
                pe.wait_ge(VE.sem, VE.at(i, "ratio", 1))
                for t in range(G // P):
                    mm = nc.tensor.transpose(t_ps[:, t * P:(t + 1) * P], zs[:, t * P:(t + 1) * P], C.ident[:])
                mm.then_inc(PE.sem, PE.step("turn"))
                pe.wait_ge(VE.sem, VE.at(i, "value"))
                pe.wait_ge(AC.sem, AC.at(i, "xd", 1))
                for t in range(G // P):
                    mm = nc.tensor.transpose(f_ps[:, t * P:(t + 1) * P], exc[:, t * P:(t + 1) * P], C.ident[:])
                mm.then_inc(PE.sem, PE.step("back"))
                pe.wait_ge(AC.sem, AC.at(i, "xd"))
                pe.wait_ge(VE.sem, VE.at(i, "res", 1))
                nc.tensor.matmul(o_ps[:], w_t[:], xd_t[:], start=True, stop=True).then_inc(PE.sem, PE.step("out"))
            PE.done()

        @block.scalar
        def _(act):
            AC.credit(act)
            act.wait_ge(w_turned, 1)
            nc.scalar.activation(w_t[:], w_ps[:], ACT.Copy).then_inc(w_ready, 1)
            with act.Fori(0, NG) as i:
                act.wait_ge(PE.sem, PE.at(i, "turn", 1))
                nc.scalar.activation(zs[:], z[:, bass.ds(i * G, G)], ACT.Copy).then_inc(AC.sem, AC.step("stage"))
                act.wait_ge(PE.sem, PE.at(i, "back"))
                nc.scalar.activation(xd_t[:], f_ps[:], ACT.Copy).then_inc(AC.sem, AC.step("xd"))
            AC.done()

        @block.vector
        def _(dve):
            VE.credit(dve)
            WQ.credit(dve)
            quantise(dve, WQ, 0, wq, exc, P)
            WQ.done()
            dve.wait_ge(w_turned, 1)
            with dve.Fori(0, NG) as i:
                dve.wait_ge(PE.sem, PE.at(i, "turn"))
                quantise(dve, VE, i, t_ps, exc, G)
                dve.wait_ge(PE.sem, PE.at(i, "out"))
                at = bass.ds(i * G, G)
                nc.vector.scalar_tensor_tensor(x[:, at], o_ps[:], bias[:], x[:, at], ALU.add, ALU.add)\
                    .then_inc(VE.sem, VE.step("res"))
            VE.done()


def moe(nc, x, z, w, C):
    E = w["moe_router"].shape[1]
    F = w["moe_gate"].shape[2] // P
    NT = T // P
    with ExitStack() as stage:
        sb, ps, sem = open_tools(stage, nc)
        router = sb("moe_router", [P, E])
        gate_w = sb("moe_gate", [P, E, F * P])
        up_w = sb("moe_up", [P, E, F * P])
        down_w = sb("moe_down", [P, E, F, P])
        gu_b = sb("moe_gub", [P, 2, E, F])
        down_b = sb("moe_downb", [E, P])
        falling = sb("moe_falling", [P, NT, E])
        sel = sb("moe_sel", [E, E, P])
        prob_t = sb("moe_prob_t", [E, T])
        load_tiles(nc, "moe", [(router[:], w["moe_router"]), (gate_w[:], w["moe_gate"]), (up_w[:], w["moe_up"]),
                               (down_w[:], w["moe_down"]), (gu_b[:], w["moe_gub"]), (down_b[:], w["L2_ffn_down_b"]),
                               (falling[:], w["c_falling"]), (sel[:], w["c_sel8"])])
        prob = sb("moe_prob", [P, NT, E])

        with ExitStack() as ctx:
            sb, ps, sem = open_tools(ctx, nc)
            zs = sb("moe_zs", [P, 2, G])
            l_ps = ps("moe_lps", [P, 2, 512])
            PE = Steps(ctx, nc, "moe_r_pe", [("logits", j) for j in (0, 1)])
            AC = Steps(ctx, nc, "moe_r_act", [("logits", j) for j in (0, 1)])
            PO = Steps(ctx, nc, "moe_r_pool", [("stage", j) for j in (0, 1)])
            block = ctx.enter_context(nc.Block())

            @block.gpsimd
            def _(pool):
                PO.credit(pool)
                with pool.Fori(0, NG // 2) as i:
                    for j in (0, 1):
                        pool.wait_ge(PE.sem, PE.at(i, ("logits", j), 1))
                        nc.gpsimd.tensor_copy(zs[:, j, :], z[:, bass.ds(i * (2 * G) + j * G, G)])\
                            .then_inc(PO.sem, PO.step(("stage", j)))
                PO.done()

            @block.tensor
            def _(pe):
                PE.credit(pe)
                with pe.Fori(0, NG // 2) as i:
                    for j in (0, 1):
                        pe.wait_ge(PO.sem, PO.at(i, ("stage", j)))
                        pe.wait_ge(AC.sem, AC.at(i, ("logits", j), 1))
                        for t in range(G // P):
                            mm = nc.tensor.matmul(l_ps[:, j, t * E:(t + 1) * E], zs[:, j, t * P:(t + 1) * P], router[:],
                                                  start=True, stop=True)
                        mm.then_inc(PE.sem, PE.step(("logits", j)))
                PE.done()

            @block.scalar
            def _(act):
                AC.credit(act)
                with act.Fori(0, NG // 2) as i:
                    for j in (0, 1):
                        act.wait_ge(PE.sem, PE.at(i, ("logits", j)))
                        nc.scalar.activation(prob[:, bass.ds(i * (2 * G // P) + j * (G // P), G // P), :],
                                             l_ps[:, j, 0:G // P * E].rearrange("p (t e) -> p t e", e=E), ACT.Copy)\
                            .then_inc(AC.sem, AC.step(("logits", j)))
                AC.done()

        with ExitStack() as ctx:
            sb, ps, sem = open_tools(ctx, nc)
            one = sb("moe_one", [P, NT])
            left = sb("moe_left", [P, NT, E])
            rank = sb("moe_rank", [P, NT, E])
            pick = sb("moe_pick", [P, NT, E])
            mask = sb("moe_mask", [P, NT, E])
            t_ps = ps("moe_tps", [E, T])
            vstep = sem("moe_vstep")
            shifted = sem("moe_shifted")
            expd = sem("moe_exp")
            routed = sem("moe_routed")
            turned = sem("moe_turned")
            block = ctx.enter_context(nc.Block())

            @block.vector
            def _(dve):
                done = [0]

                def then(ins):
                    done[0] += 1
                    ins.then_inc(vstep, 1)
                    dve.wait_ge(vstep, done[0])

                def wide(t):
                    return t[:].rearrange("p (t e) -> p t e", e=1).to_broadcast([P, NT, E])

                v = nc.vector
                then(v.tensor_reduce(one[:], prob[:], X, ALU.max))
                v.tensor_tensor(prob[:], prob[:], wide(one), ALU.subtract).then_inc(shifted, 1)
                dve.wait_ge(expd, 1)
                then(v.tensor_reduce(one[:], prob[:], X, ALU.add))
                then(v.reciprocal(one[:], one[:]))
                then(v.tensor_tensor(prob[:], prob[:], wide(one), ALU.mult))
                then(v.tensor_copy(left[:], prob[:]))
                for k in range(2):
                    then(v.tensor_reduce(one[:], left[:], X, ALU.max))
                    then(v.tensor_tensor(rank[:], left[:], wide(one), ALU.is_equal))
                    then(v.tensor_tensor(rank[:], rank[:], falling[:], ALU.mult))
                    then(v.tensor_reduce(one[:], rank[:], X, ALU.max))
                    dst = mask if k == 0 else pick
                    then(v.tensor_tensor(dst[:], falling[:], wide(one), ALU.is_equal))
                    if k == 0:
                        then(v.scalar_tensor_tensor(left[:], mask[:], -2.0, left[:], ALU.mult, ALU.add))
                then(v.tensor_tensor(mask[:], mask[:], pick[:], ALU.add))
                then(v.tensor_tensor(prob[:], prob[:], mask[:], ALU.mult))
                then(v.tensor_reduce(one[:], prob[:], X, ALU.add))
                then(v.tensor_scalar(one[:], one[:], 1e-9, None, ALU.add))
                then(v.reciprocal(one[:], one[:]))
                v.tensor_tensor(prob[:], prob[:], wide(one), ALU.mult).then_inc(routed, 1)

            @block.scalar
            def _(act):
                act.wait_ge(shifted, 1)
                nc.scalar.activation(prob[:], prob[:], ACT.Exp).then_inc(expd, 1)
                for b in range(NG):
                    act.wait_ge(turned, b + 1)
                    nc.scalar.activation(prob_t[:, b * G:(b + 1) * G], t_ps[:, b * G:(b + 1) * G], ACT.Copy)

            @block.tensor
            def _(pe):
                pe.wait_ge(routed, 1)
                for t in range(NT):
                    mm = nc.tensor.transpose(t_ps[:, t * P:(t + 1) * P], prob[:, t, :], C.ident[:])
                    if t % (G // P) == G // P - 1:
                        mm.then_inc(turned, 1)

        with ExitStack() as ctx:
            sb, ps, sem = open_tools(ctx, nc)
            sg = sb("moe_sg", [P, 2, G])
            hid = sb("moe_hid", [P, 2, G])
            g_ps = ps("moe_gps", [P, 2, G])
            u_ps = ps("moe_ups", [P, 2, G])
            p_ps = ps("moe_pps", [P, 2, G])
            o_ps = ps("moe_ops", [P, G])
            U = range(E * F)
            n = len(U)
            PE = Steps(ctx, nc, "moe_pe", ["gateup0", "gateup1"] + [s for k in U for s in
                       (["gateup%d" % (k + 2)] if k + 2 < n else []) + ["down%d" % k]])
            AC = Steps(ctx, nc, "moe_act", ["silu%d" % k for k in U])
            VE = Steps(ctx, nc, "moe_dve", [s for k in U for s in ("hid%d" % k, "weigh%d" % k)] + ["res"])
            block = ctx.enter_context(nc.Block())

            @block.tensor
            def _(pe):
                PE.credit(pe)

                def gate_up(i, k):
                    e, f = divmod(k, F)
                    at = bass.ds(i * G, G)
                    pe.wait_ge(VE.sem, VE.at(i, "weigh%d" % ((k - 2) % n), 0 if k >= 2 else 1))
                    nc.tensor.matmul(g_ps[:, k % 2, :], gate_w[:, e, f * P:(f + 1) * P], z[:, at], start=True, stop=True)
                    if f == 0:
                        nc.tensor.matmul(p_ps[:, e % 2, :], sel[:, e, :], prob_t[:, at], start=True, stop=True)
                    nc.tensor.matmul(u_ps[:, k % 2, :], up_w[:, e, f * P:(f + 1) * P], z[:, at], start=True, stop=True)\
                        .then_inc(PE.sem, PE.step("gateup%d" % k))

                with pe.Fori(0, NG) as i:
                    at = bass.ds(i * G, G)
                    gate_up(i, 0)
                    gate_up(i, 1)
                    for k in U:
                        if k + 2 < n:
                            gate_up(i, k + 2)
                        pe.wait_ge(VE.sem, VE.at(i, "weigh%d" % k))
                        mm = nc.tensor.matmul(o_ps[:], down_w[:, k // F, k % F, :], hid[:, k % 2, :], start=k == 0, stop=False)
                        if k == n - 1:
                            mm = nc.tensor.matmul(o_ps[:], down_b[:], prob_t[:, at], start=False, stop=True)
                        mm.then_inc(PE.sem, PE.step("down%d" % k))
                PE.done()

            @block.scalar
            def _(act):
                AC.credit(act)
                act.preload_act_table(ACT.Silu)
                with act.Fori(0, NG) as i:
                    for k in U:
                        act.wait_ge(PE.sem, PE.at(i, "gateup%d" % k))
                        act.wait_ge(VE.sem, VE.at(i, "hid%d" % ((k - 2) % n), 0 if k >= 2 else 1))
                        nc.scalar.activation(sg[:, k % 2, :], g_ps[:, k % 2, :], ACT.Silu,
                                             bias=gu_b[:, 0, k // F, k % F:k % F + 1]).then_inc(AC.sem, AC.step("silu%d" % k))
                AC.done()

            @block.vector
            def _(dve):
                VE.credit(dve)
                with dve.Fori(0, NG) as i:
                    for k in U:
                        dve.wait_ge(AC.sem, AC.at(i, "silu%d" % k))
                        dve.wait_ge(PE.sem, PE.at(i, "down%d" % ((k - 2) % n), 0 if k >= 2 else 1))
                        nc.vector.scalar_tensor_tensor(hid[:, k % 2, :], u_ps[:, k % 2, :], gu_b[:, 1, k // F, k % F:k % F + 1],
                                                       sg[:, k % 2, :], ALU.add, ALU.mult)\
                            .then_inc(VE.sem, VE.step("hid%d" % k))
                        dve.wait_ge(VE.sem, VE.at(i, "hid%d" % k))
                        nc.vector.tensor_tensor(hid[:, k % 2, :], hid[:, k % 2, :], p_ps[:, (k // F) % 2, :], ALU.mult)\
                            .then_inc(VE.sem, VE.step("weigh%d" % k))
                    dve.wait_ge(PE.sem, PE.at(i, "down%d" % (n - 1)))
                    at = bass.ds(i * G, G)
                    nc.vector.tensor_tensor(x[:, at], x[:, at], o_ps[:], ALU.add).then_inc(VE.sem, VE.step("res"))
                VE.done()


def ffn_layout(a, w):
    w["mx_bias"] = a["L1_ffn_bias"].reshape(P, 1)
    q = lambda k: a["L2_ffn_" + k]
    w["moe_router"] = q("router_w").T
    w["moe_gate"] = q("gate_w").transpose(1, 0, 2)
    w["moe_up"] = q("up_w").transpose(1, 0, 2)
    w["moe_down"] = q("down_w").reshape(8, 2, P, P).transpose(2, 0, 1, 3)
    w["moe_gub"] = np.stack([q("gate_b").reshape(8, 2, P).transpose(2, 0, 1), q("up_b").reshape(8, 2, P).transpose(2, 0, 1)], 1)


def ffn_tables():
    return {"c_falling": np.broadcast_to(np.arange(8, 0, -1, dtype=np.float32), (P, T // P, 8)),
            "c_sel8": np.repeat(np.eye(8, dtype=np.float32)[:, :, None], P, 2)}


def attention(nc, name, src, res, w, C, heads, dh, scale, rotary):
    HPC = 4
    QC = 4
    step = 32 if dh < 32 else dh
    FC = heads * dh // P
    VW = heads * dh
    units = [(c, qt) for c in range(heads // HPC) for qt in range(2)]
    NU = len(units)
    with ExitStack() as stage:
        sb, ps, sem = open_tools(stage, nc)
        qk_w = sb(f"{name}_qkw", [P, 2, QC, P])
        v_w = sb(f"{name}_vw", [P, VW])
        o_w = sb(f"{name}_ow", [P, FC, P])
        tab = sb(f"{name}_tab", [P, 1 if rotary else heads, 3 * P])
        pairs = [(qk_w[:], w[f"{name}_qkw"]), (v_w[:], w[f"{name}_vw"]), (o_w[:], w[f"{name}_ow"]),
                 (tab[:], w["c_band" if rotary else "c_alibi"])]
        if rotary:
            rot = sb(f"{name}_rot", [P, P])
            blk = sb(f"{name}_blk", [P, P])
            trig = sb(f"{name}_trig", [P, 2, 2, SEQ])
            qk_s = sb(f"{name}_qks", [P, 2])
            pairs += [(rot[:], w["c_rot"]), (blk[:], w["c_blk"]), (trig[:], w["c_trig"]), (qk_s[:], w[f"{name}_qks"])]
        else:
            qk_b = sb(f"{name}_qkb", [P, 2, QC, 1])
            v_b = sb(f"{name}_vb", [1, VW])
            o_b = sb(f"{name}_ob", [P, 1])
            pairs += [(qk_b[:], w[f"{name}_qkb"]), (v_b[:], w[f"{name}_vb"]), (o_b[:], w[f"{name}_ob"])]
        load_tiles(nc, name, pairs)

        with ExitStack() as ctx:
            sb, ps, sem = open_tools(ctx, nc)
            zs = sb(f"{name}_zs", [P, SEQ])
            qk = sb(f"{name}_qk", [P, 2, QC, SEQ])
            v1 = sb(f"{name}_v1", [P, 2, heads, dh + 1])
            s_sb = sb(f"{name}_s", [P, 2, HPC * 2 * P])
            mx = sb(f"{name}_mx", [P, 2, HPC])
            pt = sb(f"{name}_pt", [P, 2, HPC * 2 * P])
            rden = sb(f"{name}_rden", [P, 2, HPC])
            o_sb = sb(f"{name}_o", [P, 2, heads, dh])
            ot = sb(f"{name}_ot", [P, FC, SEQ])
            big = [ps(f"{name}_big{j}", [P, 2 * G]) for j in (0, 1)]
            pt_ps = ps(f"{name}_ptps", [P, 2 * G])
            o_ps = ps(f"{name}_ops", [P, G])
            m_ps = ps(f"{name}_mps", [P, G])
            if rotary:
                sq = sb(f"{name}_sq", [P, 2, 2 * G])
                raw = sb(f"{name}_raw", [P, 2, 2 * G])
                turn = sb(f"{name}_turn", [P, 2, 2 * G])
            QK = ("q", "k")
            prep_pe = [("proj", a) for a in QK] + ["v"]
            prep_act, prep_dve, prep_pool = ["v"], [("qk", a) for a in QK], ["stage"]
            if rotary:
                prep_pe += [(s, a) for a in QK for s in ("norm", "rot")]
                prep_act = [("square", a) for a in QK] + ["v"] + [(s, a) for a in QK for s in ("ln", "rnorm")]
                prep_dve = [("raw", a) for a in QK] + [(s, a) for a in QK for s in ("clip", "sin")] \
                    + [(s, a) for a in QK for s in ("sum", "qk")]
                prep_pool = ["stage"] + [("cos", a) for a in QK]
            PE = Steps(ctx, nc, f"{name}_pe", prep_pe + ["s0"] + [s for u in range(NU) for s in
                       (["s%d" % (u + 1)] if u + 1 < NU else []) + ["turn%d" % u, "pv%d" % u]] + ["oturn", "out"])
            AC = Steps(ctx, nc, f"{name}_act", prep_act + [s for u in range(NU) for s in ("exp%d" % u, "pt%d" % u)] + ["ot"])
            VE = Steps(ctx, nc, f"{name}_dve", prep_dve + [s for u in range(NU + 1) for s in
                       (["bias%d" % u, "max%d" % u, "sub%d" % u] if u < NU else [])
                       + (["rden%d" % (u - 1), "o%d" % (u - 1)] if u else [])] + ["res"])
            PO = Steps(ctx, nc, f"{name}_pool", prep_pool)
            ones = sem(f"{name}_ones")
            block = ctx.enter_context(nc.Block())

            @block.gpsimd
            def _(pool):
                PO.credit(pool)
                nc.gpsimd.memset(v1[:], 1.0).then_inc(ones, 1)
                with pool.Fori(0, BATCH) as i:
                    pool.wait_ge(PE.sem, PE.at(i, "v", 1))
                    nc.gpsimd.tensor_copy(zs[:], src[:, bass.ds(i * SEQ, SEQ)]).then_inc(PO.sem, PO.step("stage"))
                    if rotary:
                        for a, q in enumerate(QK):
                            pool.wait_ge(VE.sem, VE.at(i, ("raw", q)))
                            nc.gpsimd.tensor_tensor(turn[:, a, :].rearrange("p (c t) -> p c t", c=QC),
                                                    raw[:, a, :].rearrange("p (c t) -> p c t", c=QC),
                                                    trig[:, a, 0:1, :].to_broadcast([P, QC, SEQ]), ALU.mult)\
                                .then_inc(PO.sem, PO.step(("cos", q)))
                PO.done()

            @block.tensor
            def _(pe):
                PE.credit(pe)

                def scores(i, u):
                    c, qt = units[u]
                    nk = (qt + 1) * P
                    if u == 0:
                        pe.wait_ge(VE.sem, VE.at(i, ("qk", "k")))
                    if u >= 2:
                        pe.wait_ge(VE.sem, VE.at(i, "bias%d" % (u - 2)))
                    for j in range(HPC):
                        h = c * HPC + j
                        at = slice(h // QC * step, h // QC * step + dh)
                        mm = nc.tensor.matmul(big[u % 2][:, j * nk:(j + 1) * nk], qk[at, 0, h % QC, qt * P:(qt + 1) * P],
                                              qk[at, 1, h % QC, 0:nk], start=True, stop=True)
                    mm.then_inc(PE.sem, PE.step("s%d" % u))

                with pe.Fori(0, BATCH) as i:
                    at = bass.ds(i * SEQ, SEQ)
                    for a, q in enumerate(QK):
                        if a == 0:
                            pe.wait_ge(AC.sem, AC.at(i, "ot", 1))
                        else:
                            pe.wait_ge(VE.sem, VE.at(i, "bias%d" % (NU - 1), 1))
                        for c in range(QC):
                            mm = nc.tensor.matmul(big[a][:, c * SEQ:(c + 1) * SEQ], qk_w[:, a, c, :], src[:, at],
                                                  start=True, stop=True)
                        mm.then_inc(PE.sem, PE.step(("proj", q)))
                    pe.wait_ge(PO.sem, PO.at(i, "stage"))
                    pe.wait_ge(AC.sem, AC.at(i, "pt%d" % (NU - 1), 1))
                    for kt in range(2):
                        mm = nc.tensor.matmul(pt_ps[:, kt * G:kt * G + VW], zs[:, kt * P:(kt + 1) * P], v_w[:],
                                              start=True, stop=rotary)
                        if not rotary:
                            mm = nc.tensor.matmul(pt_ps[:, kt * G:kt * G + VW], C.ones[:, 0:P], v_b[:], start=False, stop=True)
                    mm.then_inc(PE.sem, PE.step("v"))
                    if rotary:
                        for a, q in enumerate(QK):
                            pe.wait_ge(AC.sem, AC.at(i, ("square", q)))
                            pe.wait_ge(VE.sem, VE.at(i, ("raw", q)))
                            for k in range(2):
                                mm = nc.tensor.matmul(big[a][:, k * G:(k + 1) * G], blk[:], sq[:, a, k * G:(k + 1) * G],
                                                      start=True, stop=True)
                            mm.then_inc(PE.sem, PE.step(("norm", q)))
                            if a == 0:
                                pe.wait_ge(AC.sem, AC.at(i, "v"))
                            else:
                                pe.wait_ge(VE.sem, VE.at(i, ("sin", "q")))
                            for k in range(2):
                                mm = nc.tensor.matmul(pt_ps[:, k * G:(k + 1) * G], rot[:], raw[:, a, k * G:(k + 1) * G],
                                                      start=True, stop=True)
                            mm.then_inc(PE.sem, PE.step(("rot", q)))
                    scores(i, 0)
                    for u, (c, qt) in enumerate(units):
                        if u + 1 < NU:
                            scores(i, u + 1)
                        pe.wait_ge(AC.sem, AC.at(i, "exp%d" % u))
                        pe.wait_ge(AC.sem, AC.at(i, "pt%d" % (u - 1) if u else "v"))
                        n = HPC * (qt + 1)
                        for k in range(n):
                            mm = nc.tensor.transpose(pt_ps[:, k * P:(k + 1) * P], s_sb[:, u % 2, k * P:(k + 1) * P], C.ident[:])
                        mm.then_inc(PE.sem, PE.step("turn%d" % u))
                        pe.wait_ge(AC.sem, AC.at(i, "pt%d" % u))
                        pe.wait_ge(VE.sem, VE.at(i, "o%d" % ((u - 1) % NU), 0 if u else 1))
                        for j in range(HPC):
                            for kt in range(qt + 1):
                                mm = nc.tensor.matmul(o_ps[:, j * (dh + 1):(j + 1) * (dh + 1)],
                                                      pt[:, u % 2, (j * (qt + 1) + kt) * P:(j * (qt + 1) + kt + 1) * P],
                                                      v1[:, kt, c * HPC + j, :], start=kt == 0, stop=kt == qt)
                        mm.then_inc(PE.sem, PE.step("pv%d" % u))
                    pe.wait_ge(VE.sem, VE.at(i, "o%d" % (NU - 1)))
                    for f in range(FC):
                        for qt in range(2):
                            mm = nc.tensor.transpose(big[0][:, f * SEQ + qt * P:f * SEQ + (qt + 1) * P],
                                                     o_sb[:, qt].rearrange("p h d -> p (h d)")[:, f * P:(f + 1) * P], C.ident[:])
                    mm.then_inc(PE.sem, PE.step("oturn"))
                    pe.wait_ge(AC.sem, AC.at(i, "ot"))
                    pe.wait_ge(VE.sem, VE.at(i, "res", 1))
                    for f in range(FC):
                        mm = nc.tensor.matmul(m_ps[:, 0:SEQ], o_w[:, f, :], ot[:, f, :], start=f == 0, stop=f == FC - 1)
                    mm.then_inc(PE.sem, PE.step("out"))
                PE.done()

            @block.scalar
            def _(act):
                AC.credit(act)
                act.preload_act_table_set("natural_log_exp_and_others")
                act.wait_ge(ones, 1)
                with act.Fori(0, BATCH) as i:
                    if rotary:
                        for a, q in enumerate(QK):
                            act.wait_ge(PE.sem, PE.at(i, ("proj", q)))
                            nc.scalar.activation(sq[:, a, :], big[a][:], ACT.Square).then_inc(AC.sem, AC.step(("square", q)))
                    act.wait_ge(PE.sem, PE.at(i, "v"))
                    for kt in range(2):
                        a = nc.scalar.activation(v1[:, kt, :, 0:dh], pt_ps[:, kt * G:kt * G + VW].rearrange("p (h d) -> p h d", d=dh),
                                                 ACT.Copy)
                    a.then_inc(AC.sem, AC.step("v"))
                    if rotary:
                        for a, q in enumerate(QK):
                            act.wait_ge(VE.sem, VE.at(i, ("clip", q)))
                            nc.scalar.activation(sq[:, a, :], sq[:, a, :], ACT.Ln).then_inc(AC.sem, AC.step(("ln", q)))
                            act.wait_ge(AC.sem, AC.at(i, ("ln", q)))
                            nc.scalar.activation(sq[:, a, :], sq[:, a, :], ACT.Exp, scale=-0.5)\
                                .then_inc(AC.sem, AC.step(("rnorm", q)))
                    for u, (c, qt) in enumerate(units):
                        n = HPC * (qt + 1) * P
                        act.wait_ge(VE.sem, VE.at(i, "sub%d" % u))
                        nc.scalar.activation(s_sb[:, u % 2, 0:n], s_sb[:, u % 2, 0:n], ACT.Exp)\
                            .then_inc(AC.sem, AC.step("exp%d" % u))
                        act.wait_ge(PE.sem, PE.at(i, "turn%d" % u))
                        nc.scalar.activation(pt[:, u % 2, 0:n], pt_ps[:, 0:n], ACT.Copy).then_inc(AC.sem, AC.step("pt%d" % u))
                    act.wait_ge(PE.sem, PE.at(i, "oturn"))
                    nc.scalar.activation(ot[:].rearrange("p f t -> p (f t)"), big[0][:, 0:FC * SEQ], ACT.Copy)\
                        .then_inc(AC.sem, AC.step("ot"))
                AC.done()

            @block.vector
            def _(dve):
                VE.credit(dve)
                v = nc.vector
                with dve.Fori(0, BATCH) as i:
                    if not rotary:
                        for a, q in enumerate(QK):
                            dve.wait_ge(PE.sem, PE.at(i, ("proj", q)))
                            v.tensor_tensor(qk[:, a], big[a][:].rearrange("p (c t) -> p c t", c=QC),
                                            qk_b[:, a].to_broadcast([P, QC, SEQ]), ALU.add).then_inc(VE.sem, VE.step(("qk", q)))
                    else:
                        for a, q in enumerate(QK):
                            dve.wait_ge(AC.sem, AC.at(i, ("square", q)))
                            v.tensor_scalar(raw[:, a, :], big[a][:], qk_s[:, a:a + 1], None, ALU.mult)\
                                .then_inc(VE.sem, VE.step(("raw", q)))
                        for a, q in enumerate(QK):
                            dve.wait_ge(PE.sem, PE.at(i, ("norm", q)))
                            v.tensor_scalar(sq[:, a, :], big[a][:], 1e-24, None, ALU.max).then_inc(VE.sem, VE.step(("clip", q)))
                            dve.wait_ge(PE.sem, PE.at(i, ("rot", q)))
                            dve.wait_ge(PO.sem, PO.at(i, ("cos", q)))
                            v.tensor_tensor(raw[:, a, :].rearrange("p (c t) -> p c t", c=QC),
                                            pt_ps[:].rearrange("p (c t) -> p c t", c=QC),
                                            trig[:, a, 1:2, :].to_broadcast([P, QC, SEQ]), ALU.mult)\
                                .then_inc(VE.sem, VE.step(("sin", q)))
                        for a, q in enumerate(QK):
                            dve.wait_ge(VE.sem, VE.at(i, ("sin", q)))
                            v.tensor_tensor(raw[:, a, :], raw[:, a, :], turn[:, a, :], ALU.add).then_inc(VE.sem, VE.step(("sum", q)))
                            dve.wait_ge(VE.sem, VE.at(i, ("sum", q)))
                            dve.wait_ge(AC.sem, AC.at(i, ("rnorm", q)))
                            v.tensor_tensor(qk[:, a].rearrange("p c t -> p (c t)"), raw[:, a, :], sq[:, a, :], ALU.mult)\
                                .then_inc(VE.sem, VE.step(("qk", q)))
                    for u in range(NU + 1):
                        if u < NU:
                            c, qt = units[u]
                            nk = (qt + 1) * P
                            b = u % 2
                            s = s_sb[:, b, 0:HPC * nk].rearrange("p (h k) -> p h k", h=HPC)
                            bias = (tab[:, 0:1] if rotary else tab[:, c * HPC:(c + 1) * HPC])[:, :, qt * P:qt * P + nk]
                            dve.wait_ge(PE.sem, PE.at(i, "s%d" % u))
                            dve.wait_ge(PE.sem, PE.at(i, "turn%d" % ((u - 2) % NU), 0 if u >= 2 else 1))
                            v.scalar_tensor_tensor(s, big[b][:, 0:HPC * nk].rearrange("p (h k) -> p h k", h=HPC), scale,
                                                   bias.to_broadcast([P, HPC, nk]) if rotary else bias,
                                                   ALU.mult, ALU.add).then_inc(VE.sem, VE.step("bias%d" % u))
                            dve.wait_ge(VE.sem, VE.at(i, "bias%d" % u))
                            v.tensor_reduce(mx[:, b, :], s, X, ALU.max).then_inc(VE.sem, VE.step("max%d" % u))
                            dve.wait_ge(VE.sem, VE.at(i, "max%d" % u))
                            v.tensor_tensor(s, s, mx[:, b, :].rearrange("p (h k) -> p h k", k=1).to_broadcast([P, HPC, nk]),
                                            ALU.subtract).then_inc(VE.sem, VE.step("sub%d" % u))
                        if u:
                            c, qt = units[u - 1]
                            b = (u - 1) % 2
                            o = o_ps[:, 0:HPC * (dh + 1)].rearrange("p (h d) -> p h d", h=HPC)
                            dve.wait_ge(PE.sem, PE.at(i, "pv%d" % (u - 1)))
                            v.reciprocal(rden[:, b, :], o[:, :, dh]).then_inc(VE.sem, VE.step("rden%d" % (u - 1)))
                            dve.wait_ge(VE.sem, VE.at(i, "rden%d" % (u - 1)))
                            if u == 1:
                                dve.wait_ge(PE.sem, PE.at(i, "oturn", 1))
                            v.tensor_tensor(o_sb[:, qt, c * HPC:(c + 1) * HPC, :], o[:, :, 0:dh],
                                            rden[:, b, :].rearrange("p (h k) -> p h k", k=1).to_broadcast([P, HPC, dh]), ALU.mult)\
                                .then_inc(VE.sem, VE.step("o%d" % (u - 1)))
                    at = bass.ds(i * SEQ, SEQ)
                    dve.wait_ge(PE.sem, PE.at(i, "out"))
                    if rotary:
                        ins = v.tensor_tensor(res[:, at], res[:, at], m_ps[:, 0:SEQ], ALU.add)
                    else:
                        ins = v.scalar_tensor_tensor(res[:, at], m_ps[:, 0:SEQ], o_b[:], res[:, at], ALU.add, ALU.add)
                    ins.then_inc(VE.sem, VE.step("res"))
                VE.done()


def alibi_attention(nc, x, z, w, C):
    attention(nc, "a1", z, x, w, C, 16, 8, 8 ** -0.5, False)


def shift_tokens(nc, name, src, dst):
    with ExitStack() as ctx:
        block = ctx.enter_context(nc.Block())
        seqs = lambda t, lo: t[lo:lo + 64, :].rearrange("p (b t) -> p b t", b=BATCH)

        @block.scalar
        def _(act):
            nc.scalar.activation(dst[0:64, :], src[0:64, :], ACT.Copy)

        @block.vector
        def _(dve):
            nc.vector.tensor_copy(seqs(dst, 64)[:, :, 1:], seqs(src, 64)[:, :, :SEQ - 1])

        @block.gpsimd
        def _(pool):
            nc.gpsimd.memset(seqs(dst, 64)[:, :, 0:1], 0.0)


def local_transformer(nc, x, z, w, C):
    HID = w["l3_w1"].shape[2] // 2
    sizes = [min(P, HID - c) for c in range(0, HID, P)]
    HC = len(sizes)
    with ExitStack() as stage:
        sb, ps, sem = open_tools(stage, nc)
        h = sb("l3_h", [P, T])
        for l in range(2):
            shift_tokens(nc, f"l3{l}a", z, h)
            attention(nc, f"l3{l}", h, z, w, C, 8, 64, 1.0, True)
            shift_tokens(nc, f"l3{l}f", z, h)
            with ExitStack() as ctx:
                sb, ps, sem = open_tools(ctx, nc)
                w1 = sb(f"l3{l}_w1", [P, 2 * HID])
                w2 = sb(f"l3{l}_w2", [P, HC, P])
                b1 = sb(f"l3{l}_b1", [P, 2, HC])
                col = sb(f"l3{l}_col", [P, 3])
                pairs = [(w1[:], w["l3_w1"][l]), (col[:], w["l3_col"][l])]
                for c, k in enumerate(sizes):
                    pairs.append((w2[:k, c, :], w["l3_w2"][l, c * P:c * P + k, :]))
                    for a in range(2):
                        pairs.append((b1[:k, a, c:c + 1], w["l3_b1"][l, a * HID + c * P:a * HID + c * P + k, :]))
                load_tiles(nc, f"l3{l}_ff", pairs)
                layernorm(nc, f"l3{l}_ln", h, h, C, col[:, 0:1], col[:, 1:2])
                gated_ffn(nc, f"l3{l}_ff", z, h, w1[:, HID:], w1[:, :HID], w2, sizes, ACT.Gelu, C,
                          b1[:, 1, :], b1[:, 0, :], col[:, 2:3])
        residual_add(nc, "l3", x, z)


def attn_layout(a, w):
    q = lambda k: a["L1_attn_" + k]
    win, bin_ = q("w_in"), q("b_in").reshape(1, 384)

    def spread(m):
        r = m.shape[0]
        t = np.zeros((r, 4, 4, 32), m.dtype)
        t[:, :, :, :8] = m.reshape(r, 4, 4, 8).transpose(0, 2, 1, 3)
        return t.reshape(r, 4, P)

    w["a1_qkw"] = np.stack([spread(win[:, :128]), spread(win[:, 128:256])], 1)
    w["a1_qkb"] = np.stack([spread(bin_[:, :128])[0].T, spread(bin_[:, 128:256])[0].T], 1)[..., None]
    w["a1_vw"] = win[:, 256:]
    w["a1_vb"] = bin_[:, 256:]
    w["a1_ow"] = q("w_out").reshape(1, P, P).transpose(1, 0, 2)
    w["a1_ob"] = q("b_out").reshape(P, 1)
    q = lambda k: a["L3_ffn_" + k]
    for l in range(2):
        m = q("wqkv")[l]
        w[f"l3{l}_qkw"] = m[:, :1024].reshape(P, 2, 2, 4, 64).transpose(0, 1, 3, 2, 4).reshape(P, 2, 4, P)
        w[f"l3{l}_vw"] = m[:, 1024:]
        w[f"l3{l}_ow"] = q("wo")[l].reshape(4, P, P).transpose(1, 0, 2)
        w[f"l3{l}_qks"] = np.stack([np.tile(q("q_scale")[l], 2), np.tile(q("k_scale")[l], 2)], 1)
    w["l3_w1"], w["l3_w2"] = q("w1"), q("w2")
    w["l3_b1"] = q("b1")[:, :, None]
    w["l3_col"] = np.stack([q("ln_g"), q("ln_b"), q("b2")], 2)


def attn_tables():
    f = np.float32
    i, j = np.arange(SEQ)[:, None], np.arange(SEQ)[None, :]

    def two_tiles(m):
        return np.moveaxis(np.concatenate([m[..., :P, :P], m[..., P:, :]], -1), -2, 0)

    slopes = np.array([2.0 ** (-0.5 * (h + 1)) for h in range(16)], f)
    alibi = np.where(j <= i, slopes[:, None, None] * (j - i).astype(f), f(MASKED)).astype(f)
    band = np.where((j <= i) & (i <= j + 64), f(0), f(MASKED)).astype(f)[None]
    half = np.arange(0, 64, 2, dtype=f)
    t = np.arange(SEQ, dtype=f)
    freqs = t[:, None] * (f(1) / f(10000) ** (half / f(64)))[None]
    freqs = np.concatenate([freqs, freqs], -1)
    base = (half + f(0.4 * 64)) / f(1.4 * 64)
    sc = base[None, :] ** ((t - SEQ // 2) / f(32))[:, None]
    sc = np.concatenate([sc, sc], -1)
    cos, sin = np.cos(freqs), np.sin(freqs)
    parts = [[f(8) * cos * sc, f(8) * sin * sc], [cos / sc, sin / sc]]
    trig = np.stack([np.stack([np.tile(m.T, (2, 1)) for m in r], 1) for r in parts], 1)
    rot = np.zeros((P, P), f)
    for b in (0, 64):
        for d in range(32):
            rot[b + 32 + d, b + d] = -1
            rot[b + d, b + 32 + d] = 1
    blk = np.kron(np.eye(2, dtype=f), np.ones((64, 64), f))
    return {"c_alibi": two_tiles(alibi), "c_band": two_tiles(band), "c_trig": trig.astype(f), "c_rot": rot, "c_blk": blk}


def permutation_scan(nc, x, z, w, C):
    NH, N = 4, 8
    NN = N * N
    NT = T // P
    M = NT * NH
    BH = BATCH * NH
    REC = N * (N + 1)
    STATE = N + 1
    md = nc.dram_tensor("p_records", (BATCH, NH, SEQ, REC), F32).ap()
    with ExitStack() as stage:
        sb, ps, sem = open_tools(stage, nc)
        soft = sb("p_soft", [P, M, NN])
        gates = sb("p_gates", [P, NT, 3, NH * N])

        with ExitStack() as mid:
            sb, ps, sem = open_tools(mid, nc)
            xn = sb("p_xn", [P, T])
            lnw = sb("p_ln", [P, 2])
            pw = sb("p_w", [P, 3 * NH * N + NH * NN])
            pb = sb("p_b", [1, 3 * NH * N + NH * NN])
            load_tiles(nc, "p", [(lnw[:], w["l0_ln"]), (pw[:], w["l0_w"]), (pb[:], w["l0_b"])])
            layernorm(nc, "p_ln", z, xn, C, lnw[:, 0:1], lnw[:, 1:2])
            with ExitStack() as ctx:
                sb, ps, sem = open_tools(ctx, nc)
                xs = sb("p_xs", [P, 2, G])
                TG = G // P
                NG3 = 3 * NH * N
                p_ps = ps("p_ps", [P, 2, TG, 512])
                PE = Steps(ctx, nc, "p_pe", [("proj", j) for j in (0, 1)])
                AC = Steps(ctx, nc, "p_act", [("copy", j) for j in (0, 1)])
                PO = Steps(ctx, nc, "p_pool", [("stage", j) for j in (0, 1)])
                block = ctx.enter_context(nc.Block())

                @block.gpsimd
                def _(pool):
                    PO.credit(pool)
                    with pool.Fori(0, NG // 2) as i:
                        for j in (0, 1):
                            pool.wait_ge(PE.sem, PE.at(i, ("proj", j), 1))
                            nc.gpsimd.tensor_copy(xs[:, j, :], xn[:, bass.ds(i * (2 * G) + j * G, G)])\
                                .then_inc(PO.sem, PO.step(("stage", j)))
                    PO.done()

                @block.tensor
                def _(pe):
                    PE.credit(pe)
                    with pe.Fori(0, NG // 2) as i:
                        for j in (0, 1):
                            pe.wait_ge(PO.sem, PO.at(i, ("stage", j)))
                            pe.wait_ge(AC.sem, AC.at(i, ("copy", j), 1))
                            for t in range(TG):
                                o = p_ps[:, j, t, 0:NG3 + NH * NN]
                                nc.tensor.matmul(o, xs[:, j, t * P:(t + 1) * P], pw[:], start=True, stop=False)
                                mm = nc.tensor.matmul(o, C.ones[:, 0:P], pb[:], start=False, stop=True)
                            mm.then_inc(PE.sem, PE.step(("proj", j)))
                    PE.done()

                @block.scalar
                def _(act):
                    AC.credit(act)
                    with act.Fori(0, NG // 2) as i:
                        for j in (0, 1):
                            act.wait_ge(PE.sem, PE.at(i, ("proj", j)))
                            nc.scalar.activation(gates[:, bass.ds(i * (2 * TG) + j * TG, TG), :, :].rearrange("p t a n -> p t (a n)"),
                                                 p_ps[:, j, :, 0:NG3], ACT.Copy)
                            nc.scalar.activation(soft[:, bass.ds(i * (2 * TG * NH) + j * (TG * NH), TG * NH), :]
                                                 .rearrange("p (t h) k -> p t (h k)", h=NH),
                                                 p_ps[:, j, :, NG3:NG3 + NH * NN], ACT.Copy)\
                                .then_inc(AC.sem, AC.step(("copy", j)))
                    AC.done()

        with ExitStack() as ctx:
            sb, ps, sem = open_tools(ctx, nc)
            MD = 80
            MG = M - MD
            vec = sb("p_vec", [P, M, N])
            rows = sb("p_rows", [P, M, N])
            used = sb("p_used", [P, M, N])
            taken = sb("p_taken", [P, M, N])
            one = sb("p_one", [P, M])
            sel = sb("p_sel", [P, N, M, N])
            falling = sb("p_falling", [P, N])
            rec = sb("p_rec", [P, M, REC])
            prod = rec[:].rearrange("p m r -> p (m r)")[:, 0:MD * NN].rearrange("p (m k) -> p m k", k=NN)
            prod_g = sb("p_prodg", [P, MG, NN])
            col = sb("p_col", [P, M, N])
            load_tiles(nc, "p2", [(falling[:], w["c_fall"])])
            vstep = sem("p_vstep")
            centred = sem("p_centred")
            expd = sem("p_expd")
            sigd = sem("p_sigd")
            picked = sem("p_picked")
            multiplied = sem("p_multiplied")
            summed = sem("p_summed")
            recorded = sem("p_recorded")
            stored = sem("p_stored")
            block = ctx.enter_context(nc.Block())
            by_row = lambda t: t[:].rearrange("p m (i j) -> p m i j", i=N)
            by_col = lambda t: t[:].rearrange("p m (i j) -> p m j i", i=N)
            wide = lambda t: t.rearrange("p m (i k) -> p m i k", k=1).to_broadcast([P, M, N, N])
            wide1 = lambda t: t[:].rearrange("p (m k) -> p m k", k=1).to_broadcast([P, M, N])
            fall = falling[:].rearrange("p (m i) -> p m i", m=1).to_broadcast([P, M, N])

            @block.gpsimd
            def _(pool):
                for k in range(N):
                    pool.wait_ge(picked, k + 1)
                    if k:
                        pool.wait_ge(summed, k)
                    nc.gpsimd.tensor_tensor(prod_g[:].rearrange("p m (i j) -> p m i j", i=N),
                                            soft[:, MD:, :].rearrange("p m (i j) -> p m i j", i=N),
                                            sel[:, k, MD:, :].rearrange("p m (i k) -> p m i k", k=1).to_broadcast([P, MG, N, N]),
                                            ALU.mult).then_inc(multiplied, 1)

            @block.scalar
            def _(act):
                nc.scalar.activation(gates[:, :, 0:2, :], gates[:, :, 0:2, :], ACT.Sigmoid).then_inc(sigd, 1)
                act.wait_ge(centred, 1)
                nc.scalar.activation(soft[:], soft[:], ACT.Exp).then_inc(expd, 1)

            @block.vector
            def _(dve):
                v = nc.vector
                done = [0]

                def then(ins):
                    done[0] += 1
                    ins.then_inc(vstep, 1)
                    dve.wait_ge(vstep, done[0])

                then(v.tensor_reduce(vec[:], by_row(soft), X, ALU.max))
                then(v.tensor_tensor(by_row(soft), by_row(soft), wide(vec[:]), ALU.subtract))
                then(v.tensor_reduce(vec[:], by_col(soft), X, ALU.max))
                v.tensor_tensor(by_col(soft), by_col(soft), wide(vec[:]), ALU.subtract).then_inc(centred, 1)
                dve.wait_ge(expd, 1)
                for _ in range(5):
                    for view in (by_row, by_col):
                        then(v.tensor_reduce(vec[:], view(soft), X, ALU.add))
                        then(v.reciprocal(vec[:], vec[:]))
                        then(v.tensor_tensor(view(soft), view(soft), wide(vec[:]), ALU.mult))

                then(v.tensor_reduce(vec[:], by_row(soft), X, ALU.max))
                for k in range(N):
                    then(v.tensor_reduce(one[:], vec[:], X, ALU.max))
                    then(v.tensor_tensor(rows[:], vec[:], wide1(one), ALU.is_equal))
                    then(v.tensor_tensor(rows[:], rows[:], fall, ALU.mult))
                    then(v.tensor_reduce(one[:], rows[:], X, ALU.max))
                    then(v.tensor_tensor(sel[:, k], fall, wide1(one), ALU.is_equal))
                    v.scalar_tensor_tensor(vec[:], sel[:, k], -4.0, vec[:], ALU.mult, ALU.add).then_inc(picked, 1)
                    dve.wait_ge(picked, k + 1)

                then(v.memset(used[:], 0.0))
                for k in range(N):
                    sk = sel[:, k, :MD, :].rearrange("p m (i k) -> p m i k", k=1).to_broadcast([P, MD, N, N])
                    then(v.tensor_tensor(prod.rearrange("p m (i j) -> p m i j", i=N),
                                         soft[:, :MD, :].rearrange("p m (i j) -> p m i j", i=N), sk, ALU.mult))
                    then(v.tensor_reduce(rows[:, :MD, :], prod.rearrange("p m (i j) -> p m j i", i=N), X, ALU.add))
                    dve.wait_ge(multiplied, k + 1)
                    v.tensor_reduce(rows[:, MD:, :], prod_g[:].rearrange("p m (i j) -> p m j i", i=N), X, ALU.add)\
                        .then_inc(summed, 1)
                    dve.wait_ge(summed, k + 1)
                    then(v.tensor_tensor(rows[:], rows[:], used[:], ALU.add))
                    then(v.tensor_reduce(one[:], rows[:], X, ALU.max))
                    then(v.tensor_tensor(rows[:], rows[:], wide1(one), ALU.is_equal))
                    then(v.tensor_tensor(rows[:], rows[:], fall, ALU.mult))
                    then(v.tensor_reduce(one[:], rows[:], X, ALU.max))
                    then(v.tensor_tensor(taken[:], fall, wide1(one), ALU.is_equal))
                    then(v.scalar_tensor_tensor(used[:], taken[:], -4.0, used[:], ALU.mult, ALU.add))
                    if k == 0:
                        then(v.tensor_tensor(col[:], sel[:, k], wide1(one), ALU.mult))
                    else:
                        then(v.tensor_tensor(taken[:], sel[:, k], wide1(one), ALU.mult))
                        then(v.tensor_tensor(col[:], col[:], taken[:], ALU.add))

                dve.wait_ge(sigd, 1)
                gv = lambda a: gates[:, :, a, :].rearrange("p t (h i) -> p t h i", h=NH)
                vt = lambda t: t[:].rearrange("p (t h) i -> p t h i", h=NH)
                then(v.tensor_scalar(vt(vec), gv(0), 2.0, -1.0, ALU.mult, ALU.add))
                then(v.tensor_tensor(vt(vec), vt(vec), gv(1), ALU.mult))
                then(v.tensor_scalar(vt(rows), gv(1), -1.0, 1.0, ALU.mult, ALU.add))
                then(v.tensor_tensor(vt(rows), vt(rows), gv(2), ALU.mult))
                body = rec[:].rearrange("p m (i q) -> p m i q", i=N)[:, :, :, 0:N]
                tail = rec[:].rearrange("p m (i q) -> p m i q", i=N)[:, :, :, N]
                fall_j = falling[:].rearrange("p (m i j) -> p m i j", m=1, i=1).to_broadcast([P, M, N, N])
                then(v.tensor_tensor(body, fall_j, wide(col[:]), ALU.is_equal))
                then(v.tensor_tensor(body, body, by_row(soft), ALU.add))
                then(v.tensor_tensor(body, body, by_row(soft), ALU.subtract))
                then(v.tensor_tensor(body, body, wide(vec[:]), ALU.mult))
                v.tensor_copy(tail, rows[:]).then_inc(recorded, 1)

            def store(eng, tiles):
                eng.wait_ge(recorded, 1)
                for t in tiles:
                    b, s = t // 2, t % 2 * P
                    eng.dma_start(md[b, :, s:s + P, :].rearrange("h s r -> s h r"), rec[:, t * NH:(t + 1) * NH, :])\
                        .then_inc(stored, 16)
                eng.wait_ge(stored, 16 * NT)

            @block.sync
            def _(sp):
                store(sp, range(NT))

    with ExitStack() as stage:
        sb, ps, sem = open_tools(stage, nc)
        SL = P // N
        NSH = SEQ // SL
        state = sb("p_state", [BH, SEQ + 1, STATE])
        ow = sb("p_ow", [P, SL, NH, P])
        ob = sb("p_ob", [P, 1])
        with ExitStack() as ctx:
            sb, ps, sem = open_tools(ctx, nc)
            steps = sb("p_steps", [BH, SEQ, REC])
            prod = sb("p_prod", [BH, REC])
            LOADS = 8
            UN = 8
            loaded = [sem(f"p_loaded{q}") for q in range(LOADS)]
            oload = sem("p_oload")
            VE = Steps(ctx, nc, "p_dve", [(s, k) for k in range(UN) for s in ("mult", "sum")])
            start = sem("p_start")
            block = ctx.enter_context(nc.Block())
            mdv = md.rearrange("b h s r -> (b h) s r")

            @block.sync
            def _(sp):
                for q in range(LOADS):
                    at = slice(q * SEQ // LOADS, (q + 1) * SEQ // LOADS)
                    sp.dma_start(steps[:, at, :], mdv[:, at, :]).then_inc(loaded[q], 16)
                sp.dma_start(ow[:], w["l0_ow"]).then_inc(oload, 16)
                sp.dma_start(ob[:], w["l0_ob"]).then_inc(oload, 16)
                sp.wait_ge(oload, 32)

            @block.vector
            def _(dve):
                VE.credit(dve)
                v = nc.vector
                v.memset(state[:], 1.0).then_inc(start, 1)
                dve.wait_ge(start, 1)
                v.memset(state[:, 0, 0:N], 0.0).then_inc(start, 1)
                dve.wait_ge(start, 2)
                for q in range(LOADS):
                    per = SEQ // LOADS // UN
                    dve.wait_ge(loaded[q], 16)
                    with dve.Fori(q * per, (q + 1) * per) as i:
                        for k in range(UN):
                            if k:
                                dve.wait_ge(VE.sem, VE.at(i, ("sum", k - 1)))
                            else:
                                dve.wait_ge(VE.sem, VE.at(i, ("sum", UN - 1), 1))
                            v.tensor_tensor(prod[:].rearrange("p (o i q) -> p o i q", o=1, i=N),
                                            steps[:, bass.ds(i * UN + k, 1), :].rearrange("p s (i q) -> p s i q", i=N),
                                            state[:, bass.ds(i * UN + k, 1), :].rearrange("p s (o q) -> p s o q", o=1)
                                            .to_broadcast([BH, 1, N, STATE]), ALU.mult)\
                                .then_inc(VE.sem, VE.step(("mult", k)))
                            dve.wait_ge(VE.sem, VE.at(i, ("mult", k)))
                            v.tensor_reduce(state[:, bass.ds(i * UN + k + 1, 1), 0:N],
                                            prod[:].rearrange("p (o i q) -> p o i q", o=1, i=N), X, ALU.add)\
                                .then_inc(VE.sem, VE.step(("sum", k)))
                    VE.done()
                    VE.said = 0

        with ExitStack() as ctx:
            sb, ps, sem = open_tools(ctx, nc)
            packed = sb("p_packed", [BH, SEQ * N])
            turned = sb("p_turned", [P, NH, BATCH, NSH])
            t_ps = ps("p_tps", [P, NSH, BH])
            o_ps = ps("p_ops", [P, 4, 512])
            s_packed = sem("p_s_packed")
            s_turned = sem("p_s_turned")
            s_copied = sem("p_s_copied")
            s_proj = sem("p_s_proj")
            s_added = sem("p_s_added")
            s_pre = sem("p_s_pre")
            block = ctx.enter_context(nc.Block())

            @block.scalar
            def _(act):
                nc.scalar.activation(packed[:].rearrange("p (s n) -> p s n", n=N), state[:, 1:, 0:N], ACT.Copy)\
                    .then_inc(s_packed, 1)
                act.wait_ge(s_turned, 1)
                for h in range(NH):
                    a = nc.scalar.activation(turned[:, h].rearrange("p b s -> p s b"),
                                             t_ps[:].rearrange("p s (b h) -> p h s b", h=NH)[:, h], ACT.Copy)
                a.then_inc(s_copied, 1)

            @block.tensor
            def _(pe):
                pe.wait_ge(s_packed, 1)
                for s in range(NSH):
                    mm = nc.tensor.transpose(t_ps[:, s, :], packed[:, s * P:(s + 1) * P], C.ident[0:BH, 0:BH])
                mm.then_inc(s_turned, 1)
                pe.wait_ge(s_copied, 1)
                for l in range(SL):
                    if l >= 4:
                        pe.wait_ge(s_added, l - 3)
                    for h in range(NH):
                        mm = nc.tensor.matmul(o_ps[:, l % 4, 0:BATCH * NSH], ow[:, l, h, :],
                                              turned[:, h].rearrange("p b s -> p (b s)"), start=h == 0, stop=h == NH - 1)
                    mm.then_inc(s_proj, 1)

            @block.vector
            def _(dve):
                nc.vector.scalar_tensor_tensor(x[:], z[:], ob[:], x[:], ALU.add, ALU.add).then_inc(s_pre, 1)
                dve.wait_ge(s_pre, 1)
                xv = x[:].rearrange("p (b s l) -> p b s l", b=BATCH, l=SL)
                for l in range(SL):
                    dve.wait_ge(s_proj, l + 1)
                    nc.vector.tensor_tensor(xv[:, :, :, l], xv[:, :, :, l],
                                            o_ps[:, l % 4, 0:BATCH * NSH].rearrange("p (b s) -> p b s", b=BATCH), ALU.add)\
                        .then_inc(s_added, 1)


def perm_layout(a, w):
    q = lambda k: a["L0_attn_" + k]
    w["l0_ln"] = np.stack([q("ln_w"), q("ln_b")], 1)
    w["l0_w"] = np.concatenate([q("sign_W"), q("gate_W"), q("in_W"), q("perm_W")], 1)
    w["l0_b"] = np.concatenate([q("sign_b"), q("gate_b"), q("in_b"), q("perm_b")])[None]
    ow = np.zeros((16, 8, 16, 4, P), np.float32)
    for l in range(16):
        ow[l, :, l] = q("out_W").reshape(4, 8, P).transpose(1, 0, 2)
    w["l0_ow"] = ow.reshape(P, 16, 4, P)
    w["l0_ob"] = q("out_b").reshape(P, 1)


def perm_tables():
    return {"c_fall": np.broadcast_to(np.arange(8, 0, -1, dtype=np.float32), (P, 8))}


def more_layout(a, w):
    perm_layout(a, w)
    attn_layout(a, w)
    ffn_layout(a, w)
    mamba_layout(a, w)


def shape_tables():
    return {**selector_tables(), **ffn_tables(), **attn_tables(), **perm_tables()}


STAGE = {"L0_attn": permutation_scan, "L0_ffn": int8_swiglu, "L1_attn": alibi_attention, "L1_ffn": mx_linear,
         "L2_attn": mamba_layer, "L2_ffn": moe, "L3_attn": mamba_stack, "L3_ffn": local_transformer}
ALL_STAGES = tuple(STAGE)


class Tables:
    pass


def transformer_program(nc, w, out, stages=ALL_STAGES):
    with ExitStack() as ctx:
        sb, ps, sem = open_tools(ctx, nc)
        C = Tables()
        C.mean = sb("c_mean", [P, P])
        C.ident = sb("c_ident", [P, P])
        C.eps = sb("c_eps", [P, 1])
        C.one = sb("c_one", [P, 1])
        C.warm = sb("c_warm", [P, 2])
        C.ones = sb("c_ones", [1, G])
        x = sb("x", [P, T])
        z = sb("z", [P, T])
        load_tiles(nc, "start", [(x[:], w["x"]), (C.mean[:], w["c_mean"]), (C.ident[:], w["c_ident"]),
                                 (C.eps[:], w["c_eps"]), (C.one[:], w["c_one"]), (C.ones[:], w["c_ones"])])
        for s in stages:
            layernorm(nc, f"{s}_ln", x, z, C)
            STAGE[s](nc, x, z, w, C)
        with ExitStack() as end:
            stored = end.enter_context(semaphore(nc, "stored"))
            block = end.enter_context(nc.Block())

            @block.sync
            def _(sp):
                sp.dma_start(out, x[:]).then_inc(stored, 16)
                sp.wait_ge(stored, 16)


def lay_out(inputs):
    a = {k: np.asarray(v) for k, v in inputs.items()}
    w = {"x": a["L0_attn_x"].reshape(T, P).T}
    for k, v in a.items():
        if k != "L0_attn_x":
            w[k] = v
    for k in ("L0_ffn_w_gate", "L0_ffn_w_up", "L0_ffn_w_down"):
        w[k] = a[k].T
    more_layout(a, w)
    w["c_mean"] = np.full((P, P), 1.0 / P, np.float32)
    w["c_ident"] = np.eye(P, dtype=np.float32)
    w["c_eps"] = np.full((P, 1), EPS, np.float32)
    w["c_one"] = np.full((P, 1), 1.0, np.float32)
    w["c_ones"] = np.full((1, G), 1.0, np.float32)
    w.update(shape_tables())
    return {k: np.ascontiguousarray(v) for k, v in w.items()}


def build(nc, w, stages=None):
    args = {k: nc.dram_tensor(f"in_{k}", v.shape, mybir.dt.from_np(v.dtype), kind="ExternalInput").ap()
            for k, v in w.items()}
    out = nc.dram_tensor("out", (P, T), F32, kind="ExternalOutput").ap()
    transformer_program(nc, args, out, stages or ALL_STAGES)
    return {f"in_{k}": v for k, v in w.items()}


def kernel(**inputs):
    import concourse.bacc as bacc
    from concourse.bass_utils import run_bass_kernel_spmd

    nc = bacc.Bacc("TRN2", target_bir_lowering=False, num_devices=1)
    arrays = build(nc, lay_out(inputs))
    r = run_bass_kernel_spmd(nc, [arrays], core_ids=[0])
    return np.ascontiguousarray(r.results[0]["out"].T).reshape(BATCH, SEQ, P)
```

```python
from contextlib import ExitStack, contextmanager

import numpy as np
import concourse.bass as bass
from concourse import mybir

F32 = mybir.dt.float32
I32 = mybir.dt.int32
BF16 = mybir.dt.bfloat16
ALU = mybir.AluOpType
ACT = mybir.ActivationFunctionType
X = mybir.AxisListType.X

P = 128
BATCH, SEQ = 16, 256
T = BATCH * SEQ
G = 512
NG = T // G
EPS = 1e-5
MASKED = -1e30


@contextmanager
def semaphore(nc, name):
    s = nc.alloc_semaphore(name)
    yield s
    nc.gpsimd.sem_clear(s)
    nc.release_semaphore(s)


class Steps:

    LEAD = 2

    def __init__(self, ctx, nc, name, steps, loops=1):
        self.sem = ctx.enter_context(semaphore(nc, name))
        self.names = {s: n for n, s in enumerate(steps)}
        assert len(self.names) == len(steps)
        self.n = len(steps)
        self.order = list(steps)
        self.said = 0

    def credit(self, eng):
        eng.sem_inc(self.sem, self.LEAD * self.n)

    def step(self, name):
        assert self.order[self.said % self.n] == name, (self.order[self.said % self.n], name)
        self.said += 1
        return 1

    def done(self):
        assert self.said % self.n == 0, (self.said, self.n)

    def at(self, i, name, back=0):
        assert 0 <= back <= self.LEAD
        return i * self.n + (self.LEAD - back) * self.n + self.names[name] + 1

    def last(self, loops):
        return (loops + self.LEAD) * self.n


def open_tools(ctx, nc, block_name=""):
    def sb(name, shape, dt=F32):
        return ctx.enter_context(nc.sbuf_tensor(name, shape, dt))

    def ps(name, shape, dt=F32):
        return ctx.enter_context(nc.psum_tensor(name, shape, dt))

    def sem(name):
        return ctx.enter_context(semaphore(nc, name))

    return sb, ps, sem


def load_tiles(nc, name, pairs):
    with ExitStack() as ctx:
        loaded = ctx.enter_context(semaphore(nc, f"{name}_loaded"))
        block = ctx.enter_context(nc.Block())

        @block.sync
        def _(sp):
            for dst, src in pairs[0::2]:
                sp.dma_start(dst, src).then_inc(loaded, 16)
            sp.wait_ge(loaded, 16 * len(pairs))

        @block.scalar
        def _(act):
            for dst, src in pairs[1::2]:
                act.dma_start(dst, src).then_inc(loaded, 16)


def layernorm(nc, name, src, dst, C, gain=None, shift=None, tokens=T):
    with ExitStack() as ctx:
        sb, ps, sem = open_tools(ctx, nc)
        sq = sb(f"{name}_sq", [P, 2, G])
        rstd = sb(f"{name}_rstd", [P, 2, G])
        mean_ps = ps(f"{name}_mean", [P, 2, G])
        var_ps = ps(f"{name}_var", [P, 2, G])
        LOOPS = tokens // G // 2
        two = (0, 1)
        PE = Steps(ctx, nc, f"{name}_pe", [("mean", j) for j in two] + [("var", j) for j in two])
        AC = Steps(ctx, nc, f"{name}_act", [("square", j) for j in two] + [(s, j) for j in two for s in ("ln", "rstd")])
        VE = Steps(ctx, nc, f"{name}_dve", [("center", j) for j in two] + [("scale", j) for j in two]
                   + ([("affine", j) for j in two] if gain is not None else []))
        block = ctx.enter_context(nc.Block())

        @block.tensor
        def _(pe):
            PE.credit(pe)
            with pe.Fori(0, LOOPS) as i:
                for j in two:
                    pe.wait_ge(VE.sem, VE.at(i, ("center", j), 1))
                    nc.tensor.matmul(mean_ps[:, j, :], C.mean[:], src[:, bass.ds(i * (2 * G) + j * G, G)],
                                     start=True, stop=True).then_inc(PE.sem, PE.step(("mean", j)))
                for j in two:
                    pe.wait_ge(AC.sem, AC.at(i, ("square", j)))
                    nc.tensor.matmul(var_ps[:, j, :], C.mean[:], sq[:, j, :], start=True, stop=True)\
                        .then_inc(PE.sem, PE.step(("var", j)))
            PE.done()

        @block.scalar
        def _(act):
            AC.credit(act)
            act.preload_act_table_set("natural_log_exp_and_others")
            with act.Fori(0, LOOPS) as i:
                for j in two:
                    act.wait_ge(VE.sem, VE.at(i, ("center", j)))
                    act.wait_ge(PE.sem, PE.at(i, ("var", j), 1))
                    nc.scalar.activation(sq[:, j, :], dst[:, bass.ds(i * (2 * G) + j * G, G)], ACT.Square)\
                        .then_inc(AC.sem, AC.step(("square", j)))
                for j in two:
                    act.wait_ge(PE.sem, PE.at(i, ("var", j)))
                    act.wait_ge(VE.sem, VE.at(i, ("scale", j), 1))
                    nc.scalar.activation(rstd[:, j, :], var_ps[:, j, :], ACT.Ln, bias=C.eps[:])\
                        .then_inc(AC.sem, AC.step(("ln", j)))
                    act.wait_ge(AC.sem, AC.at(i, ("ln", j)))
                    nc.scalar.activation(rstd[:, j, :], rstd[:, j, :], ACT.Exp, scale=-0.5)\
                        .then_inc(AC.sem, AC.step(("rstd", j)))
            AC.done()

        @block.vector
        def _(dve):
            VE.credit(dve)
            with dve.Fori(0, LOOPS) as i:
                at = [bass.ds(i * (2 * G) + j * G, G) for j in two]
                for j in two:
                    dve.wait_ge(PE.sem, PE.at(i, ("mean", j)))
                    nc.vector.tensor_tensor(dst[:, at[j]], src[:, at[j]], mean_ps[:, j, :], ALU.subtract)\
                        .then_inc(VE.sem, VE.step(("center", j)))
                for j in two:
                    dve.wait_ge(AC.sem, AC.at(i, ("rstd", j)))
                    dve.wait_ge(VE.sem, VE.at(i, ("center", j)))
                    nc.vector.tensor_tensor(dst[:, at[j]], dst[:, at[j]], rstd[:, j, :], ALU.mult)\
                        .then_inc(VE.sem, VE.step(("scale", j)))
                if gain is not None:
                    for j in two:
                        dve.wait_ge(VE.sem, VE.at(i, ("scale", j)))
                        nc.vector.tensor_scalar(dst[:, at[j]], dst[:, at[j]], gain, shift, ALU.mult, ALU.add)\
                            .then_inc(VE.sem, VE.step(("affine", j)))
            VE.done()


def residual_add(nc, name, x, y):
    with ExitStack() as ctx:
        block = ctx.enter_context(nc.Block())

        @block.vector
        def _(dve):
            nc.vector.tensor_tensor(x[:, 0:T * 5 // 8], x[:, 0:T * 5 // 8], y[:, 0:T * 5 // 8], ALU.add)

        @block.gpsimd
        def _(pool):
            nc.gpsimd.tensor_tensor(x[:, T * 5 // 8:T], x[:, T * 5 // 8:T], y[:, T * 5 // 8:T], ALU.add)


def gated_ffn(nc, name, res, src, gate_w, up_w, down_w, sizes, func, C, gate_b=None, up_b=None, down_b=None):
    with ExitStack() as ctx:
        sb, ps, sem = open_tools(ctx, nc)
        HC = len(sizes)
        hid = sb(f"{name}_hid", [P, 2, G])
        sg = sb(f"{name}_sg", [P, 2, G])
        gate_ps = ps(f"{name}_gate", [P, 2, G])
        up_ps = ps(f"{name}_up", [P, 2, G])
        out_ps = ps(f"{name}_out", [P, G])
        U = range(2 * HC)
        n = len(U)
        PE = Steps(ctx, nc, f"{name}_pe", ["gateup0", "gateup1"] + [s for u in U for s in
                   (["gateup%d" % (u + 2)] if u + 2 in U else []) + ["down%d" % u]])
        AC = Steps(ctx, nc, f"{name}_act", ["func%d" % u for u in U])
        VE = Steps(ctx, nc, f"{name}_dve", [s for u in U for s in ["hid%d" % u] + (["out%d" % u] if u % HC == HC - 1 else [])])
        block = ctx.enter_context(nc.Block())

        @block.tensor
        def _(pe):
            PE.credit(pe)

            def gate_up(i, u):
                g, c = divmod(u, HC)
                k = sizes[c]
                at = bass.ds(i * (2 * G) + g * G, G)
                pe.wait_ge(VE.sem, VE.at(i, "hid%d" % ((u - 2) % n), 0 if u >= 2 else 1))
                nc.tensor.matmul(gate_ps[:k, u % 2, :], gate_w[:, c * P:c * P + k], src[:, at], start=True, stop=True)
                nc.tensor.matmul(up_ps[:k, u % 2, :], up_w[:, c * P:c * P + k], src[:, at], start=True, stop=True)\
                    .then_inc(PE.sem, PE.step("gateup%d" % u))

            with pe.Fori(0, NG // 2) as i:
                gate_up(i, 0)
                gate_up(i, 1)
                for u in U:
                    if u + 2 in U:
                        gate_up(i, u + 2)
                    c = u % HC
                    k = sizes[c]
                    pe.wait_ge(VE.sem, VE.at(i, "hid%d" % u))
                    if c == 0:
                        pe.wait_ge(VE.sem, VE.at(i, "out%d" % ((u - 1) % n), 0 if u else 1))
                    nc.tensor.matmul(out_ps[:], down_w[:k, c, :], hid[:k, u % 2, :],
                                     start=c == 0, stop=c == HC - 1).then_inc(PE.sem, PE.step("down%d" % u))
            PE.done()

        @block.scalar
        def _(act):
            AC.credit(act)
            act.preload_act_table(func)
            with act.Fori(0, NG // 2) as i:
                for u in U:
                    k = sizes[u % HC]
                    act.wait_ge(PE.sem, PE.at(i, "gateup%d" % u))
                    act.wait_ge(VE.sem, VE.at(i, "hid%d" % ((u - 2) % n), 0 if u >= 2 else 1))
                    bias = {} if gate_b is None else {"bias": gate_b[:k, u % HC:u % HC + 1]}
                    nc.scalar.activation(sg[:k, u % 2, :], gate_ps[:k, u % 2, :], func, **bias)\
                        .then_inc(AC.sem, AC.step("func%d" % u))
            AC.done()

        @block.vector
        def _(dve):
            VE.credit(dve)
            with dve.Fori(0, NG // 2) as i:
                for u in U:
                    g, c = divmod(u, HC)
                    k = sizes[c]
                    dve.wait_ge(AC.sem, AC.at(i, "func%d" % u))
                    dve.wait_ge(PE.sem, PE.at(i, "down%d" % ((u - 2) % n), 0 if u >= 2 else 1))
                    h, up, s = hid[:k, u % 2, :], up_ps[:k, u % 2, :], sg[:k, u % 2, :]
                    if up_b is None:
                        ins = nc.vector.tensor_tensor(h, up, s, ALU.mult)
                    else:
                        ins = nc.vector.scalar_tensor_tensor(h, up, up_b[:k, c:c + 1], s, ALU.add, ALU.mult)
                    ins.then_inc(VE.sem, VE.step("hid%d" % u))
                    if c == HC - 1:
                        at = bass.ds(i * (2 * G) + g * G, G)
                        dve.wait_ge(PE.sem, PE.at(i, "down%d" % u))
                        if down_b is None:
                            ins = nc.vector.tensor_tensor(res[:, at], res[:, at], out_ps[:], ALU.add)
                        else:
                            ins = nc.vector.scalar_tensor_tensor(res[:, at], out_ps[:], down_b, res[:, at], ALU.add, ALU.add)
                        ins.then_inc(VE.sem, VE.step("out%d" % u))
            VE.done()


def int8_swiglu(nc, x, z, w, C):
    with ExitStack() as stage:
        sb, ps, sem = open_tools(stage, nc)
        HC = w["L0_ffn_w_gate"].shape[1] // P
        wi = sb("q_wi", [P, 3, HC * P], I32)
        wf = sb("q_wf", [P, 3, HC * P])
        load_tiles(nc, "q", [(wi[:, 0, :], w["L0_ffn_w_gate"]), (wi[:, 1, :], w["L0_ffn_w_up"]),
                             (wi[:, 2, :].rearrange("p (c n) -> p c n", c=HC),
                              w["L0_ffn_w_down"].rearrange("(c p) n -> p c n", p=P))])
        with ExitStack() as ctx:
            block = ctx.enter_context(nc.Block())

            @block.scalar
            def _(act):
                nc.scalar.activation(wf[:], wi[:], ACT.Copy, scale=1.0 / 127.0)

        gated_ffn(nc, "q", x, z, wf[:, 0, :], wf[:, 1, :], wf[:, 2, :].rearrange("p (c n) -> p c n", c=HC),
                  [P] * HC, ACT.Silu, C)


def selector(nc, stage, name, w, N):
    sel = stage.enter_context(nc.sbuf_tensor(f"{name}_sel", [96, 2 * N, P], BF16))
    with ExitStack() as ctx:
        wide = ctx.enter_context(nc.sbuf_tensor(f"{name}_sel32", [96, 2 * N, P], F32))
        load_tiles(nc, f"{name}_sel", [(wide[:], w[f"c_sel{2 * N}"])])
        block = ctx.enter_context(nc.Block())

        @block.vector
        def _(dve):
            nc.vector.tensor_copy(sel[:], wide[:])
    return sel


def mamba(nc, name, src, res, w, C, sel, N, low_rank=False):
    H = 2
    R = 8
    NSEQ = G // SEQ
    CH = N // 2
    KN = 2 * N
    with ExitStack() as stage:
        sb, ps, sem = open_tools(stage, nc)
        in_w = sb(f"{name}_in_w", [P, 2 * H, P])
        conv_w = sb(f"{name}_conv_w", [P, H, 4])
        col = sb(f"{name}_col", [P, 3, H])
        conv_b, dt_b, skip = col[:, 0, :], col[:, 1, :], col[:, 2, :]
        xp_w = sb(f"{name}_xp_w", [P, H, R + 96])
        dt_w = sb(f"{name}_dt_w", [R, H, P])
        a_log = sb(f"{name}_a_log", [P, H, N])
        decay = sb(f"{name}_decay", [P, H, N])
        out_w = sb(f"{name}_out_w", [P, H, P])
        u = sb(f"{name}_u", [P, H, T])
        sz = sb(f"{name}_sz", [P, H, T])
        delta = sb(f"{name}_delta", [P, H, T])
        bc = sb(f"{name}_bc", [96, T], BF16)
        pairs = [(in_w[:], w[f"{name}_in_w"]), (conv_w[:], w[f"{name}_conv_w"]), (col[:], w[f"{name}_col"]),
                 (xp_w[:], w[f"{name}_xp_w"]), (dt_w[:], w[f"{name}_dt_w"]), (a_log[:], w[f"{name}_a_log"]),
                 (out_w[:], w[f"{name}_out_w"])]
        if low_rank:
            u_t = sb(f"{name}_ut", [R, H, P])
            v_w = sb(f"{name}_v", [R, N])
            lrs = sb(f"{name}_lrs", [P, 1])
            pairs += [(u_t[:], w[f"{name}_ut"]), (v_w[:], w[f"{name}_v"]), (lrs[:], w[f"{name}_lrs"])]
        load_tiles(nc, name, pairs)

        with ExitStack() as ctx:
            sb, ps, sem = open_tools(ctx, nc)
            conv = sb(f"{name}_conv", [P, H, G])
            in_ps = ps(f"{name}_inps", [P, 2 * H, G])
            PE = Steps(ctx, nc, f"{name}_a_pe", [("in", c) for c in range(4)])
            AC = Steps(ctx, nc, f"{name}_a_act", [("silu", c) for c in (2, 3, 0, 1)])
            VE = Steps(ctx, nc, f"{name}_a_dve", [("tap", h, k) for h in range(H) for k in range(4)])
            block = ctx.enter_context(nc.Block())

            @block.tensor
            def _(pe):
                PE.credit(pe)
                with pe.Fori(0, NG) as i:
                    for c in range(4):
                        if c < H:
                            pe.wait_ge(VE.sem, VE.at(i, ("tap", c, 3), 1))
                        else:
                            pe.wait_ge(AC.sem, AC.at(i, ("silu", c), 1))
                        nc.tensor.matmul(in_ps[:, c, :], in_w[:, c, :], src[:, bass.ds(i * G, G)],
                                         start=True, stop=True).then_inc(PE.sem, PE.step(("in", c)))
                PE.done()

            @block.vector
            def _(dve):
                VE.credit(dve)
                with dve.Fori(0, NG) as i:
                    for h in range(H):
                        xin = in_ps[:, h, :].rearrange("p (b t) -> p b t", b=NSEQ)
                        acc = conv[:, h, :].rearrange("p (b t) -> p b t", b=NSEQ)
                        dve.wait_ge(PE.sem, PE.at(i, ("in", h)))
                        dve.wait_ge(AC.sem, AC.at(i, ("silu", h), 1))
                        nc.vector.tensor_scalar(acc, xin, conv_w[:, h, 3:4], None, ALU.mult)\
                            .then_inc(VE.sem, VE.step(("tap", h, 0)))
                        for k in range(1, 4):
                            dve.wait_ge(VE.sem, VE.at(i, ("tap", h, k - 1)))
                            nc.vector.scalar_tensor_tensor(acc[:, :, k:], xin[:, :, :SEQ - k], conv_w[:, h, 3 - k:4 - k],
                                                           acc[:, :, k:], ALU.mult, ALU.add)\
                                .then_inc(VE.sem, VE.step(("tap", h, k)))
                VE.done()

            @block.scalar
            def _(act):
                AC.credit(act)
                act.preload_act_table(ACT.Silu)
                with act.Fori(0, NG) as i:
                    for c in (2, 3):
                        act.wait_ge(PE.sem, PE.at(i, ("in", c)))
                        nc.scalar.activation(sz[:, c - H, bass.ds(i * G, G)], in_ps[:, c, :], ACT.Silu)\
                            .then_inc(AC.sem, AC.step(("silu", c)))
                    for h in range(H):
                        act.wait_ge(VE.sem, VE.at(i, ("tap", h, 3)))
                        nc.scalar.activation(u[:, h, bass.ds(i * G, G)], conv[:, h, :], ACT.Silu, bias=conv_b[:, h:h + 1])\
                            .then_inc(AC.sem, AC.step(("silu", h)))
                AC.done()

        with ExitStack() as ctx:
            sb, ps, sem = open_tools(ctx, nc)
            dt_low = sb(f"{name}_dt_low", [R, G])
            mag = sb(f"{name}_mag", [P, H, G])
            pos = sb(f"{name}_pos", [P, H, G])
            low_ps = ps(f"{name}_low", [R, G])
            bc_ps = ps(f"{name}_bcps", [96, G])
            rest = sb(f"{name}_rest", [96, G])
            mid = sb(f"{name}_mid", [96, G], BF16)
            dt_ps = ps(f"{name}_dtps", [P, H, G])
            PE = Steps(ctx, nc, f"{name}_b_pe", ["low", "bc", ("dt", 0), ("dt", 1)])
            AC = Steps(ctx, nc, f"{name}_b_act", ["low", "bc", "bc_mid"] + [(s, h) for h in range(H) for s in ("abs", "exp", "ln")])
            VE = Steps(ctx, nc, f"{name}_b_dve", ["rest", "bc_low"] + [(s, h) for h in range(H) for s in ("pos", "delta")])
            rank_done = sem(f"{name}_rank")
            rates = sem(f"{name}_rates")
            block = ctx.enter_context(nc.Block())

            @block.tensor
            def _(pe):
                PE.credit(pe)
                if low_rank:
                    for h in range(H):
                        mm = nc.tensor.matmul(dt_ps[:, h, 0:N], u_t[:, h, :], v_w[:], start=True, stop=True)
                    mm.then_inc(rank_done, 1)
                    pe.wait_ge(rates, 2)
                with pe.Fori(0, NG) as i:
                    at = bass.ds(i * G, G)
                    pe.wait_ge(AC.sem, AC.at(i, "low", 1))
                    for h in range(H):
                        mm = nc.tensor.matmul(low_ps[:], xp_w[:, h, 0:R], u[:, h, at], start=h == 0, stop=h == H - 1)
                    mm.then_inc(PE.sem, PE.step("low"))
                    pe.wait_ge(AC.sem, AC.at(i, "bc", 1))
                    pe.wait_ge(VE.sem, VE.at(i, "rest", 1))
                    for h in range(H):
                        mm = nc.tensor.matmul(bc_ps[:], xp_w[:, h, R:], u[:, h, at], start=h == 0, stop=h == H - 1)
                    mm.then_inc(PE.sem, PE.step("bc"))
                    pe.wait_ge(AC.sem, AC.at(i, "low"))
                    for h in range(H):
                        pe.wait_ge(AC.sem, AC.at(i, ("abs", h), 1))
                        pe.wait_ge(VE.sem, VE.at(i, ("pos", h), 1))
                        nc.tensor.matmul(dt_ps[:, h, :], dt_w[:, h, :], dt_low[:], start=True, stop=True)\
                            .then_inc(PE.sem, PE.step(("dt", h)))
                PE.done()

            @block.scalar
            def _(act):
                AC.credit(act)
                act.preload_act_table_set("natural_log_exp_and_others")
                nc.scalar.activation(decay[:], a_log[:], ACT.Exp).then_inc(rates, 1)
                with act.Fori(0, NG) as i:
                    act.wait_ge(PE.sem, PE.at(i, "low"))
                    act.wait_ge(PE.sem, PE.at(i, ("dt", 1), 1))
                    nc.scalar.activation(dt_low[:], low_ps[:], ACT.Copy).then_inc(AC.sem, AC.step("low"))
                    act.wait_ge(PE.sem, PE.at(i, "bc"))
                    at = bass.ds(i * G, G)
                    nc.scalar.activation(bc[:, at], bc_ps[:], ACT.Copy).then_inc(AC.sem, AC.step("bc"))
                    act.wait_ge(VE.sem, VE.at(i, "rest"))
                    nc.scalar.activation(bc[32:64, at], rest[32:64, :], ACT.Copy)
                    nc.scalar.activation(mid[64:96, :], rest[64:96, :], ACT.Copy).then_inc(AC.sem, AC.step("bc_mid"))
                    for h in range(H):
                        act.wait_ge(PE.sem, PE.at(i, ("dt", h)))
                        act.wait_ge(VE.sem, VE.at(i, ("delta", h), 1))
                        nc.scalar.activation(mag[:, h, :], dt_ps[:, h, :], ACT.Abs, bias=dt_b[:, h:h + 1])\
                            .then_inc(AC.sem, AC.step(("abs", h)))
                        act.wait_ge(AC.sem, AC.at(i, ("abs", h)))
                        nc.scalar.activation(mag[:, h, :], mag[:, h, :], ACT.Exp, scale=-1.0)\
                            .then_inc(AC.sem, AC.step(("exp", h)))
                        act.wait_ge(AC.sem, AC.at(i, ("exp", h)))
                        nc.scalar.activation(mag[:, h, :], mag[:, h, :], ACT.Ln, bias=C.one[:])\
                            .then_inc(AC.sem, AC.step(("ln", h)))
                AC.done()

            @block.vector
            def _(dve):
                VE.credit(dve)
                dve.wait_ge(rates, 1)
                if low_rank:
                    dve.wait_ge(rank_done, 1)
                    nc.vector.tensor_scalar(a_log[:], dt_ps[:, :, 0:N], lrs[:], float(R) ** -0.5, ALU.mult, ALU.mult)\
                        .then_inc(rates, 1)
                    dve.wait_ge(rates, 2)
                    nc.vector.tensor_tensor(decay[:], a_log[:], decay[:], ALU.subtract)
                else:
                    nc.vector.tensor_scalar(decay[:], decay[:], -1.0, None, ALU.mult)
                with dve.Fori(0, NG) as i:
                    at = bass.ds(i * G, G)
                    dve.wait_ge(AC.sem, AC.at(i, "bc"))
                    nc.vector.tensor_tensor(rest[:], bc_ps[:], bc[:, at], ALU.subtract).then_inc(VE.sem, VE.step("rest"))
                    dve.wait_ge(AC.sem, AC.at(i, "bc_mid"))
                    dve.wait_ge(VE.sem, VE.at(i, "rest"))
                    nc.vector.tensor_tensor(bc[64:96, at], rest[64:96, :], mid[64:96, :], ALU.subtract)\
                        .then_inc(VE.sem, VE.step("bc_low"))
                    for h in range(H):
                        dve.wait_ge(AC.sem, AC.at(i, ("abs", h)))
                        nc.vector.tensor_scalar(pos[:, h, :], dt_ps[:, h, :], dt_b[:, h:h + 1], 0.0, ALU.add, ALU.max)\
                            .then_inc(VE.sem, VE.step(("pos", h)))
                        dve.wait_ge(VE.sem, VE.at(i, ("pos", h)))
                        dve.wait_ge(AC.sem, AC.at(i, ("ln", h)))
                        nc.vector.tensor_tensor(delta[:, h, bass.ds(i * G, G)], pos[:, h, :], mag[:, h, :], ALU.add)\
                            .then_inc(VE.sem, VE.step(("delta", h)))
                VE.done()

        with ExitStack() as ctx:
            sb, ps, sem = open_tools(ctx, nc)
            dA = sb(f"{name}_dA", [P, 2, H, 2, G])
            inp = sb(f"{name}_inp", [P, H, 2, G])
            hs = sb(f"{name}_hs", [P, 2, H, 2, G])
            cb = sb(f"{name}_cb", [P, 2, 2, G])
            du = sb(f"{name}_du", [P, H, G])
            y = delta
            b_ps = ps(f"{name}_bps", [P, 2, G])
            c_ps = ps(f"{name}_cps", [P, 2, G])
            y_ps = ps(f"{name}_yps", [P, H, G])
            o_ps = ps(f"{name}_ops", [P, G])
            CS, HS = range(CH), range(H)
            PE = Steps(ctx, nc, f"{name}_c_pe",
                       [("bcast", 0)] + [s for c in CS for s in ([("bcast", c + 1)] if c + 1 < CH else [])
                        + [("sum", c - 1, h) for h in HS if c]] + [("sum", CH - 1, h) for h in HS] + ["out"])
            AC = Steps(ctx, nc, f"{name}_c_act", [s for c in CS for s in [("decay", c, h) for h in HS] + [("c", c)]])
            VE = Steps(ctx, nc, f"{name}_c_dve", [s for c in CS for s in [("in", c, h) for h in HS] + [("scan", c, h) for h in HS]]
                       + [(s, h) for h in HS for s in ("skip", "gate")] + ["res"])
            PO = Steps(ctx, nc, f"{name}_c_pool", [("du", h) for h in HS] + [("hc", c, h) for c in CS for h in HS])
            zeros = sem(f"{name}_zeros")
            decays_begun = sem(f"{name}_decays_begun")
            block = ctx.enter_context(nc.Block())

            @block.gpsimd
            def _(pool):
                PO.credit(pool)
                nc.gpsimd.memset(dA[:], 0.0).then_inc(zeros, 1)
                with pool.Fori(0, NG) as i:
                    at = bass.ds(i * G, G)
                    for h in HS:
                        pool.wait_ge(VE.sem, VE.at(i, ("in", CH - 1, h), 1))
                        nc.gpsimd.tensor_tensor(du[:, h, :], delta[:, h, at], u[:, h, at], ALU.mult)\
                            .then_inc(PO.sem, PO.step(("du", h)))
                    for c in CS:
                        pool.wait_ge(AC.sem, AC.at(i, ("c", c)))
                        for h in HS:
                            pool.wait_ge(VE.sem, VE.at(i, ("scan", c, h)))
                            nc.gpsimd.tensor_tensor(hs[:, c % 2, h], hs[:, c % 2, h], cb[:, c % 2], ALU.mult)\
                                .then_inc(PO.sem, PO.step(("hc", c, h)))
                PO.done()

            @block.tensor
            def _(pe):
                PE.credit(pe)

                def bcast(i, c):
                    at = bass.ds(i * G, G)
                    for s in range(2):
                        n = 2 * c + s
                        if s == 0:
                            pe.wait_ge(VE.sem, VE.at(i, ("in", (c - 1) % CH, 1), 0 if c else 1))
                        nc.tensor.matmul(b_ps[:, s, :], sel[:, n, :], bc[:, at], start=True, stop=True)
                        if s == 0:
                            pe.wait_ge(AC.sem, AC.at(i, ("c", (c - 1) % CH), 0 if c else 1))
                        mm = nc.tensor.matmul(c_ps[:, s, :], sel[:, N + n, :], bc[:, at], start=True, stop=True)
                    mm.then_inc(PE.sem, PE.step(("bcast", c)))

                def add_up(i, c):
                    for h in HS:
                        pe.wait_ge(PO.sem, PO.at(i, ("hc", c, h)))
                        if c == 0:
                            pe.wait_ge(VE.sem, VE.at(i, ("skip", h), 1))
                        for s in range(2):
                            mm = nc.tensor.matmul(y_ps[:, h, :], C.ident[:], hs[:, c % 2, h, s, :],
                                                  start=c == 0 and s == 0, stop=c == CH - 1 and s == 1)
                        mm.then_inc(PE.sem, PE.step(("sum", c, h)))

                with pe.Fori(0, NG) as i:
                    bcast(i, 0)
                    for c in CS:
                        if c + 1 < CH:
                            bcast(i, c + 1)
                        if c:
                            add_up(i, c - 1)
                    add_up(i, CH - 1)
                    at = bass.ds(i * G, G)
                    pe.wait_ge(VE.sem, VE.at(i, "res", 1))
                    for h in HS:
                        pe.wait_ge(VE.sem, VE.at(i, ("gate", h)))
                        mm = nc.tensor.matmul(o_ps[:], out_w[:, h, :], y[:, h, at], start=h == 0, stop=h == H - 1)
                    mm.then_inc(PE.sem, PE.step("out"))
                PE.done()

            @block.scalar
            def _(act):
                AC.credit(act)
                act.wait_ge(zeros, 1)
                act.preload_act_table_set("natural_log_exp_and_others")
                with act.Fori(0, NG) as i:
                    for c in CS:
                        for h in HS:
                            act.wait_ge(VE.sem, VE.at(i, ("scan", (c - 2) % CH, h), 0 if c >= 2 else 1))
                            act.sem_inc(decays_begun, 1)
                            for s in range(2):
                                dl = delta[:, h, bass.ds(i * G, G)].rearrange("p (b t) -> p b t", b=NSEQ)[:, :, 1:]
                                o = dA[:, c % 2, h, s, :].rearrange("p (b t) -> p b t", b=NSEQ)[:, :, 1:]
                                a = nc.scalar.activation(o, dl, ACT.Exp, scale=decay[:, h, 2 * c + s:2 * c + s + 1])
                            a.then_inc(AC.sem, AC.step(("decay", c, h)))
                        act.wait_ge(PE.sem, PE.at(i, ("bcast", c)))
                        act.wait_ge(PO.sem, PO.at(i, ("hc", (c - 2) % CH, 1), 0 if c >= 2 else 1))
                        nc.scalar.activation(cb[:, c % 2], c_ps[:], ACT.Copy).then_inc(AC.sem, AC.step(("c", c)))
                AC.done()

            @block.vector
            def _(dve):
                VE.credit(dve)
                with dve.Fori(0, NG) as i:
                    for c in CS:
                        dve.wait_ge(PE.sem, PE.at(i, ("bcast", c)))
                        for h in HS:
                            if c == 0:
                                dve.wait_ge(PO.sem, PO.at(i, ("du", h)))
                            dve.wait_ge(VE.sem, VE.at(i, ("scan", (c - 1) % CH, h), 0 if c else 1))
                            nc.vector.tensor_tensor(inp[:, h], b_ps[:], du[:, h:h + 1, :].to_broadcast([P, 2, G]), ALU.mult)\
                                .then_inc(VE.sem, VE.step(("in", c, h)))
                        for h in HS:
                            dve.wait_ge(VE.sem, VE.at(i, ("in", c, h)))
                            dve.wait_ge(AC.sem, AC.at(i, ("decay", c, h)))
                            dve.wait_ge(PE.sem, PE.at(i, ("sum", (c - 2) % CH, h), 0 if c >= 2 else 1))
                            nc.vector.tensor_tensor_scan(hs[:, c % 2, h].rearrange("p s t -> p (s t)"),
                                                         dA[:, c % 2, h].rearrange("p s t -> p (s t)"),
                                                         inp[:, h].rearrange("p s t -> p (s t)"), 0.0, ALU.mult, ALU.add)\
                                .then_inc(VE.sem, VE.step(("scan", c, h)))
                    at = bass.ds(i * G, G)
                    for h in HS:
                        dve.wait_ge(PE.sem, PE.at(i, ("sum", CH - 1, h)))
                        dve.wait_ge(PE.sem, PE.at(i, "out", 1))
                        nc.vector.scalar_tensor_tensor(y[:, h, at], u[:, h, at], skip[:, h:h + 1], y_ps[:, h, :], ALU.mult, ALU.add)\
                            .then_inc(VE.sem, VE.step(("skip", h)))
                        dve.wait_ge(VE.sem, VE.at(i, ("skip", h)))
                        nc.vector.tensor_tensor(y[:, h, at], y[:, h, at], sz[:, h, at], ALU.mult)\
                            .then_inc(VE.sem, VE.step(("gate", h)))
                    dve.wait_ge(PE.sem, PE.at(i, "out"))
                    nc.vector.tensor_tensor(res[:, at], res[:, at], o_ps[:], ALU.add).then_inc(VE.sem, VE.step("res"))
                VE.done()


def mamba_layer(nc, x, z, w, C):
    with ExitStack() as stage:
        mamba(nc, "m2", z, x, w, C, selector(nc, stage, "m2", w, 8), 8, low_rank=True)


def mamba_stack(nc, x, z, w, C):
    with ExitStack() as stage:
        sb, ps, sem = open_tools(stage, nc)
        ln = sb("m3_ln", [P, 2, 4])
        load_tiles(nc, "m3", [(ln[:], w["m3_ln"])])
        sel = selector(nc, stage, "m3", w, 16)
        for l in range(4):
            mamba(nc, f"m3{l}", z, z, w, C, sel, 16)
            layernorm(nc, f"m3{l}_post", z, z, C, ln[:, 0, l:l + 1], ln[:, 1, l:l + 1])
        residual_add(nc, "m3", x, z)


def mamba_layout(a, w):
    def halves(v):
        return v.reshape(2, P, -1).transpose(1, 0, 2)

    def one(name, in_w, conv_w, conv_b, xp, dtw, dtb, alog, D, ow):
        w[f"{name}_in_w"] = in_w.reshape(P, 4, P)
        w[f"{name}_conv_w"] = halves(conv_w)
        w[f"{name}_col"] = np.stack([conv_b.reshape(2, P).T, dtb.reshape(2, P).T, D.reshape(2, P).T], 1)
        bc = np.concatenate([xp[:, 8:], np.zeros((256, 32 - (xp.shape[1] - 8)), np.float32)], 1)
        w[f"{name}_xp_w"] = halves(np.concatenate([xp[:, :8], bc, bc, bc], 1))
        w[f"{name}_dt_w"] = dtw.reshape(8, 2, P)
        w[f"{name}_a_log"] = halves(alog)
        w[f"{name}_out_w"] = halves(ow)

    q = lambda k: a["L2_attn_" + k]
    one("m2", q("in_proj_w").T, q("conv_w"), q("conv_b"), q("x_proj_w").T, q("dt_proj_w").T, q("dt_proj_b"),
        q("A_log"), q("D"), q("out_proj_w").T)
    w["m2_ut"] = q("U_param").T.reshape(8, 2, P)
    w["m2_v"] = q("V_param")
    w["m2_lrs"] = np.broadcast_to(q("low_rank_scale").reshape(1, 1), (P, 1))
    q = lambda k: a["L3_attn_" + k]
    for l in range(4):
        one(f"m3{l}", *[q(k)[l] for k in ("in_proj_w", "conv_w", "conv_b", "x_proj_w", "dt_proj_w", "dt_proj_b",
                                          "A_log", "D", "out_proj_w")])
    w["m3_ln"] = np.stack([q("ln_w").T, q("ln_b").T], 1)


def selector_tables():
    return {f"c_sel{k}": np.repeat(np.tile(np.eye(32, k, dtype=np.float32), (3, 1))[:, :, None], P, 2)
            for k in (16, 32)}


def mx_linear(nc, x, z, w, C):
    BLK, TOP = 32, 7.5
    MAGIC = 1.5 * 2 ** 23
    NB = G // BLK
    QUANT = ["amax", "scale", "rscale", "ratio", "square", "ge2", "ge4", "step", "magic",
             "shifted", "rounded", "excess", "tie", "lower", "fixed", "value"]
    with ExitStack() as ctx:
        sb, ps, sem = open_tools(ctx, nc)
        wq = sb("mx_wq", [P, P])
        w_t = sb("mx_wt", [P, P])
        bias = sb("mx_bias", [P, 1])
        zs = sb("mx_zs", [P, G])
        xd_t = sb("mx_xdt", [P, G])
        amax, scale, rscale = (sb(f"mx_{n}", [P, NB]) for n in ("amax", "scale", "rscale"))
        ratio, ge2, ge4, step, magic, val, exc = (sb(f"mx_{n}", [P, G]) for n in
                                                  ("ratio", "ge2", "ge4", "step", "magic", "val", "exc"))
        t_ps = ps("mx_tps", [P, G])
        f_ps = ps("mx_fps", [P, G])
        o_ps = ps("mx_ops", [P, G])
        w_ps = ps("mx_wps", [P, P])
        load_tiles(nc, "mx", [(wq[:], w["L1_ffn_weight"]), (bias[:], w["mx_bias"])])
        PE = Steps(ctx, nc, "mx_pe", ["turn", "back", "out"])
        AC = Steps(ctx, nc, "mx_act", ["stage", "xd"])
        VE = Steps(ctx, nc, "mx_dve", QUANT + ["res"])
        WQ = Steps(ctx, nc, "mx_wq_steps", QUANT)
        w_turned = sem("mx_w_turned")
        w_ready = sem("mx_w_ready")
        block = ctx.enter_context(nc.Block())

        def quantise(dve, S, i, src, out, n):
            b = n // BLK

            def blocks(t):
                return t[:, :n].rearrange("p (b k) -> p b k", k=BLK)

            def wide(t):
                return t[:, :b].rearrange("p (b k) -> p b k", k=1).to_broadcast([P, b, BLK])

            def after(name):
                dve.wait_ge(S.sem, S.at(i, name))

            v = nc.vector
            v.tensor_reduce(amax[:, :b], blocks(src), X, ALU.max, apply_absolute_value=True)\
                .then_inc(S.sem, S.step("amax"))
            after("amax")
            v.tensor_scalar(scale[:, :b], amax[:, :b], 1.0 / TOP, 1e-30, ALU.mult, ALU.max)\
                .then_inc(S.sem, S.step("scale"))
            after("scale")
            v.reciprocal(rscale[:, :b], scale[:, :b]).then_inc(S.sem, S.step("rscale"))
            after("rscale")
            v.tensor_tensor(blocks(ratio), blocks(src), wide(rscale), ALU.mult).then_inc(S.sem, S.step("ratio"))
            after("ratio")
            if S is VE:
                dve.wait_ge(PE.sem, PE.at(i, "back", 1))
            v.tensor_tensor(exc[:, :n], ratio[:, :n], ratio[:, :n], ALU.mult).then_inc(S.sem, S.step("square"))
            after("square")
            v.tensor_scalar(ge2[:, :n], exc[:, :n], 4.0, 0.125, ALU.is_ge, ALU.mult).then_inc(S.sem, S.step("ge2"))
            v.tensor_scalar(ge4[:, :n], exc[:, :n], 16.0, 0.25, ALU.is_ge, ALU.mult).then_inc(S.sem, S.step("ge4"))
            after("ge4")
            v.scalar_tensor_tensor(step[:, :n], ge2[:, :n], 0.125, ge4[:, :n], ALU.add, ALU.add)\
                .then_inc(S.sem, S.step("step"))
            after("step")
            v.tensor_scalar(magic[:, :n], step[:, :n], MAGIC, None, ALU.mult).then_inc(S.sem, S.step("magic"))
            after("magic")
            v.tensor_tensor(val[:, :n], ratio[:, :n], magic[:, :n], ALU.add).then_inc(S.sem, S.step("shifted"))
            after("shifted")
            v.tensor_tensor(val[:, :n], val[:, :n], magic[:, :n], ALU.subtract).then_inc(S.sem, S.step("rounded"))
            after("rounded")
            v.tensor_tensor(exc[:, :n], val[:, :n], ratio[:, :n], ALU.subtract).then_inc(S.sem, S.step("excess"))
            after("excess")
            v.scalar_tensor_tensor(exc[:, :n], exc[:, :n], 2.0, step[:, :n], ALU.mult, ALU.is_ge)\
                .then_inc(S.sem, S.step("tie"))
            after("tie")
            v.tensor_tensor(exc[:, :n], exc[:, :n], step[:, :n], ALU.mult).then_inc(S.sem, S.step("lower"))
            after("lower")
            v.tensor_tensor(val[:, :n], val[:, :n], exc[:, :n], ALU.subtract).then_inc(S.sem, S.step("fixed"))
            after("fixed")
            v.tensor_tensor(blocks(out), blocks(val), wide(scale), ALU.mult).then_inc(S.sem, S.step("value"))
            after("value")

        @block.tensor
        def _(pe):
            PE.credit(pe)
            pe.wait_ge(WQ.sem, WQ.at(0, "value"))
            nc.tensor.transpose(w_ps[:], exc[:, :P], C.ident[:]).then_inc(w_turned, 1)
            pe.wait_ge(w_ready, 1)
            with pe.Fori(0, NG) as i:
                pe.wait_ge(AC.sem, AC.at(i, "stage"))
                pe.wait_ge(VE.sem, VE.at(i, "ratio", 1))
                for t in range(G // P):
                    mm = nc.tensor.transpose(t_ps[:, t * P:(t + 1) * P], zs[:, t * P:(t + 1) * P], C.ident[:])
                mm.then_inc(PE.sem, PE.step("turn"))
                pe.wait_ge(VE.sem, VE.at(i, "value"))
                pe.wait_ge(AC.sem, AC.at(i, "xd", 1))
                for t in range(G // P):
                    mm = nc.tensor.transpose(f_ps[:, t * P:(t + 1) * P], exc[:, t * P:(t + 1) * P], C.ident[:])
                mm.then_inc(PE.sem, PE.step("back"))
                pe.wait_ge(AC.sem, AC.at(i, "xd"))
                pe.wait_ge(VE.sem, VE.at(i, "res", 1))
                nc.tensor.matmul(o_ps[:], w_t[:], xd_t[:], start=True, stop=True).then_inc(PE.sem, PE.step("out"))
            PE.done()

        @block.scalar
        def _(act):
            AC.credit(act)
            act.wait_ge(w_turned, 1)
            nc.scalar.activation(w_t[:], w_ps[:], ACT.Copy).then_inc(w_ready, 1)
            with act.Fori(0, NG) as i:
                act.wait_ge(PE.sem, PE.at(i, "turn", 1))
                nc.scalar.activation(zs[:], z[:, bass.ds(i * G, G)], ACT.Copy).then_inc(AC.sem, AC.step("stage"))
                act.wait_ge(PE.sem, PE.at(i, "back"))
                nc.scalar.activation(xd_t[:], f_ps[:], ACT.Copy).then_inc(AC.sem, AC.step("xd"))
            AC.done()

        @block.vector
        def _(dve):
            VE.credit(dve)
            WQ.credit(dve)
            quantise(dve, WQ, 0, wq, exc, P)
            WQ.done()
            dve.wait_ge(w_turned, 1)
            with dve.Fori(0, NG) as i:
                dve.wait_ge(PE.sem, PE.at(i, "turn"))
                quantise(dve, VE, i, t_ps, exc, G)
                dve.wait_ge(PE.sem, PE.at(i, "out"))
                at = bass.ds(i * G, G)
                nc.vector.scalar_tensor_tensor(x[:, at], o_ps[:], bias[:], x[:, at], ALU.add, ALU.add)\
                    .then_inc(VE.sem, VE.step("res"))
            VE.done()


def moe(nc, x, z, w, C):
    E = w["moe_router"].shape[1]
    F = w["moe_gate"].shape[2] // P
    NT = T // P
    with ExitStack() as stage:
        sb, ps, sem = open_tools(stage, nc)
        router = sb("moe_router", [P, E])
        gate_w = sb("moe_gate", [P, E, F * P])
        up_w = sb("moe_up", [P, E, F * P])
        down_w = sb("moe_down", [P, E, F, P])
        gu_b = sb("moe_gub", [P, 2, E, F])
        down_b = sb("moe_downb", [E, P])
        falling = sb("moe_falling", [P, NT, E])
        sel = sb("moe_sel", [E, E, P])
        prob_t = sb("moe_prob_t", [E, T])
        load_tiles(nc, "moe", [(router[:], w["moe_router"]), (gate_w[:], w["moe_gate"]), (up_w[:], w["moe_up"]),
                               (down_w[:], w["moe_down"]), (gu_b[:], w["moe_gub"]), (down_b[:], w["L2_ffn_down_b"]),
                               (falling[:], w["c_falling"]), (sel[:], w["c_sel8"])])
        prob = sb("moe_prob", [P, NT, E])

        with ExitStack() as ctx:
            sb, ps, sem = open_tools(ctx, nc)
            zs = sb("moe_zs", [P, 2, G])
            l_ps = ps("moe_lps", [P, 2, 512])
            PE = Steps(ctx, nc, "moe_r_pe", [("logits", j) for j in (0, 1)])
            AC = Steps(ctx, nc, "moe_r_act", [("logits", j) for j in (0, 1)])
            PO = Steps(ctx, nc, "moe_r_pool", [("stage", j) for j in (0, 1)])
            block = ctx.enter_context(nc.Block())

            @block.gpsimd
            def _(pool):
                PO.credit(pool)
                with pool.Fori(0, NG // 2) as i:
                    for j in (0, 1):
                        pool.wait_ge(PE.sem, PE.at(i, ("logits", j), 1))
                        nc.gpsimd.tensor_copy(zs[:, j, :], z[:, bass.ds(i * (2 * G) + j * G, G)])\
                            .then_inc(PO.sem, PO.step(("stage", j)))
                PO.done()

            @block.tensor
            def _(pe):
                PE.credit(pe)
                with pe.Fori(0, NG // 2) as i:
                    for j in (0, 1):
                        pe.wait_ge(PO.sem, PO.at(i, ("stage", j)))
                        pe.wait_ge(AC.sem, AC.at(i, ("logits", j), 1))
                        for t in range(G // P):
                            mm = nc.tensor.matmul(l_ps[:, j, t * E:(t + 1) * E], zs[:, j, t * P:(t + 1) * P], router[:],
                                                  start=True, stop=True)
                        mm.then_inc(PE.sem, PE.step(("logits", j)))
                PE.done()

            @block.scalar
            def _(act):
                AC.credit(act)
                with act.Fori(0, NG // 2) as i:
                    for j in (0, 1):
                        act.wait_ge(PE.sem, PE.at(i, ("logits", j)))
                        nc.scalar.activation(prob[:, bass.ds(i * (2 * G // P) + j * (G // P), G // P), :],
                                             l_ps[:, j, 0:G // P * E].rearrange("p (t e) -> p t e", e=E), ACT.Copy)\
                            .then_inc(AC.sem, AC.step(("logits", j)))
                AC.done()

        with ExitStack() as ctx:
            sb, ps, sem = open_tools(ctx, nc)
            one = sb("moe_one", [P, NT])
            left = sb("moe_left", [P, NT, E])
            rank = sb("moe_rank", [P, NT, E])
            pick = sb("moe_pick", [P, NT, E])
            mask = sb("moe_mask", [P, NT, E])
            t_ps = ps("moe_tps", [E, T])
            vstep = sem("moe_vstep")
            shifted = sem("moe_shifted")
            expd = sem("moe_exp")
            routed = sem("moe_routed")
            turned = sem("moe_turned")
            block = ctx.enter_context(nc.Block())

            @block.vector
            def _(dve):
                done = [0]

                def then(ins):
                    done[0] += 1
                    ins.then_inc(vstep, 1)
                    dve.wait_ge(vstep, done[0])

                def wide(t):
                    return t[:].rearrange("p (t e) -> p t e", e=1).to_broadcast([P, NT, E])

                v = nc.vector
                then(v.tensor_reduce(one[:], prob[:], X, ALU.max))
                v.tensor_tensor(prob[:], prob[:], wide(one), ALU.subtract).then_inc(shifted, 1)
                dve.wait_ge(expd, 1)
                then(v.tensor_reduce(one[:], prob[:], X, ALU.add))
                then(v.reciprocal(one[:], one[:]))
                then(v.tensor_tensor(prob[:], prob[:], wide(one), ALU.mult))
                then(v.tensor_copy(left[:], prob[:]))
                for k in range(2):
                    then(v.tensor_reduce(one[:], left[:], X, ALU.max))
                    then(v.tensor_tensor(rank[:], left[:], wide(one), ALU.is_equal))
                    then(v.tensor_tensor(rank[:], rank[:], falling[:], ALU.mult))
                    then(v.tensor_reduce(one[:], rank[:], X, ALU.max))
                    dst = mask if k == 0 else pick
                    then(v.tensor_tensor(dst[:], falling[:], wide(one), ALU.is_equal))
                    if k == 0:
                        then(v.scalar_tensor_tensor(left[:], mask[:], -2.0, left[:], ALU.mult, ALU.add))
                then(v.tensor_tensor(mask[:], mask[:], pick[:], ALU.add))
                then(v.tensor_tensor(prob[:], prob[:], mask[:], ALU.mult))
                then(v.tensor_reduce(one[:], prob[:], X, ALU.add))
                then(v.tensor_scalar(one[:], one[:], 1e-9, None, ALU.add))
                then(v.reciprocal(one[:], one[:]))
                v.tensor_tensor(prob[:], prob[:], wide(one), ALU.mult).then_inc(routed, 1)

            @block.scalar
            def _(act):
                act.wait_ge(shifted, 1)
                nc.scalar.activation(prob[:], prob[:], ACT.Exp).then_inc(expd, 1)
                for b in range(NG):
                    act.wait_ge(turned, b + 1)
                    nc.scalar.activation(prob_t[:, b * G:(b + 1) * G], t_ps[:, b * G:(b + 1) * G], ACT.Copy)

            @block.tensor
            def _(pe):
                pe.wait_ge(routed, 1)
                for t in range(NT):
                    mm = nc.tensor.transpose(t_ps[:, t * P:(t + 1) * P], prob[:, t, :], C.ident[:])
                    if t % (G // P) == G // P - 1:
                        mm.then_inc(turned, 1)

        with ExitStack() as ctx:
            sb, ps, sem = open_tools(ctx, nc)
            sg = sb("moe_sg", [P, 2, G])
            hid = sb("moe_hid", [P, 2, G])
            g_ps = ps("moe_gps", [P, 2, G])
            u_ps = ps("moe_ups", [P, 2, G])
            p_ps = ps("moe_pps", [P, 2, G])
            o_ps = ps("moe_ops", [P, G])
            U = range(E * F)
            n = len(U)
            PE = Steps(ctx, nc, "moe_pe", ["gateup0", "gateup1"] + [s for k in U for s in
                       (["gateup%d" % (k + 2)] if k + 2 < n else []) + ["down%d" % k]])
            AC = Steps(ctx, nc, "moe_act", ["silu%d" % k for k in U])
            VE = Steps(ctx, nc, "moe_dve", [s for k in U for s in ("hid%d" % k, "weigh%d" % k)] + ["res"])
            block = ctx.enter_context(nc.Block())

            @block.tensor
            def _(pe):
                PE.credit(pe)

                def gate_up(i, k):
                    e, f = divmod(k, F)
                    at = bass.ds(i * G, G)
                    pe.wait_ge(VE.sem, VE.at(i, "weigh%d" % ((k - 2) % n), 0 if k >= 2 else 1))
                    nc.tensor.matmul(g_ps[:, k % 2, :], gate_w[:, e, f * P:(f + 1) * P], z[:, at], start=True, stop=True)
                    if f == 0:
                        nc.tensor.matmul(p_ps[:, e % 2, :], sel[:, e, :], prob_t[:, at], start=True, stop=True)
                    nc.tensor.matmul(u_ps[:, k % 2, :], up_w[:, e, f * P:(f + 1) * P], z[:, at], start=True, stop=True)\
                        .then_inc(PE.sem, PE.step("gateup%d" % k))

                with pe.Fori(0, NG) as i:
                    at = bass.ds(i * G, G)
                    gate_up(i, 0)
                    gate_up(i, 1)
                    for k in U:
                        if k + 2 < n:
                            gate_up(i, k + 2)
                        pe.wait_ge(VE.sem, VE.at(i, "weigh%d" % k))
                        mm = nc.tensor.matmul(o_ps[:], down_w[:, k // F, k % F, :], hid[:, k % 2, :], start=k == 0, stop=False)
                        if k == n - 1:
                            mm = nc.tensor.matmul(o_ps[:], down_b[:], prob_t[:, at], start=False, stop=True)
                        mm.then_inc(PE.sem, PE.step("down%d" % k))
                PE.done()

            @block.scalar
            def _(act):
                AC.credit(act)
                act.preload_act_table(ACT.Silu)
                with act.Fori(0, NG) as i:
                    for k in U:
                        act.wait_ge(PE.sem, PE.at(i, "gateup%d" % k))
                        act.wait_ge(VE.sem, VE.at(i, "hid%d" % ((k - 2) % n), 0 if k >= 2 else 1))
                        nc.scalar.activation(sg[:, k % 2, :], g_ps[:, k % 2, :], ACT.Silu,
                                             bias=gu_b[:, 0, k // F, k % F:k % F + 1]).then_inc(AC.sem, AC.step("silu%d" % k))
                AC.done()

            @block.vector
            def _(dve):
                VE.credit(dve)
                with dve.Fori(0, NG) as i:
                    for k in U:
                        dve.wait_ge(AC.sem, AC.at(i, "silu%d" % k))
                        dve.wait_ge(PE.sem, PE.at(i, "down%d" % ((k - 2) % n), 0 if k >= 2 else 1))
                        nc.vector.scalar_tensor_tensor(hid[:, k % 2, :], u_ps[:, k % 2, :], gu_b[:, 1, k // F, k % F:k % F + 1],
                                                       sg[:, k % 2, :], ALU.add, ALU.mult)\
                            .then_inc(VE.sem, VE.step("hid%d" % k))
                        dve.wait_ge(VE.sem, VE.at(i, "hid%d" % k))
                        nc.vector.tensor_tensor(hid[:, k % 2, :], hid[:, k % 2, :], p_ps[:, (k // F) % 2, :], ALU.mult)\
                            .then_inc(VE.sem, VE.step("weigh%d" % k))
                    dve.wait_ge(PE.sem, PE.at(i, "down%d" % (n - 1)))
                    at = bass.ds(i * G, G)
                    nc.vector.tensor_tensor(x[:, at], x[:, at], o_ps[:], ALU.add).then_inc(VE.sem, VE.step("res"))
                VE.done()


def ffn_layout(a, w):
    w["mx_bias"] = a["L1_ffn_bias"].reshape(P, 1)
    q = lambda k: a["L2_ffn_" + k]
    w["moe_router"] = q("router_w").T
    w["moe_gate"] = q("gate_w").transpose(1, 0, 2)
    w["moe_up"] = q("up_w").transpose(1, 0, 2)
    w["moe_down"] = q("down_w").reshape(8, 2, P, P).transpose(2, 0, 1, 3)
    w["moe_gub"] = np.stack([q("gate_b").reshape(8, 2, P).transpose(2, 0, 1), q("up_b").reshape(8, 2, P).transpose(2, 0, 1)], 1)


def ffn_tables():
    return {"c_falling": np.broadcast_to(np.arange(8, 0, -1, dtype=np.float32), (P, T // P, 8)),
            "c_sel8": np.repeat(np.eye(8, dtype=np.float32)[:, :, None], P, 2)}


def attention(nc, name, src, res, w, C, heads, dh, scale, rotary):
    HPC = 4
    QC = 4
    step = max(dh, 32)
    VW = heads * dh
    OC = HPC * step // P
    HALF = G
    units = [(c, qt) for c in range(heads // HPC) for qt in range(2)]
    NU = len(units)
    NB = 4
    with ExitStack() as stage:
        sb, ps, sem = open_tools(stage, nc)
        qk_w = sb(f"{name}_qkw", [P, 2, QC, P])
        v_w = sb(f"{name}_vw", [P, VW])
        o_w = sb(f"{name}_ow", [P, QC, P])
        tab = sb(f"{name}_tab", [P, 1 if rotary else heads, 3 * P])
        pairs = [(qk_w[:], w[f"{name}_qkw"]), (v_w[:], w[f"{name}_vw"]), (o_w[:], w[f"{name}_ow"]),
                 (tab[:], w["c_band" if rotary else "c_alibi"])]
        if rotary:
            rot = sb(f"{name}_rot", [P, P])
            blk = sb(f"{name}_blk", [P, P])
            trig = sb(f"{name}_trig", [P, 2, 2, SEQ])
            qk_s = sb(f"{name}_qks", [P, 2])
            undo = sb(f"{name}_undo", [P, 1])
            pairs += [(rot[:], w["c_rot"]), (blk[:], w["c_blk"]), (trig[:], w["c_trig"]), (qk_s[:], w[f"{name}_qks"]),
                      (undo[:], w["c_undo"])]
        else:
            qk_b = sb(f"{name}_qkb", [P, 2, QC, 1])
            v_b = sb(f"{name}_vb", [1, VW])
            o_b = sb(f"{name}_ob", [P, 1])
            pairs += [(qk_b[:], w[f"{name}_qkb"]), (v_b[:], w[f"{name}_vb"]), (o_b[:], w[f"{name}_ob"])]
        load_tiles(nc, name, pairs)

        with ExitStack() as ctx:
            sb, ps, sem = open_tools(ctx, nc)
            zs = sb(f"{name}_zs", [P, SEQ])
            qk = sb(f"{name}_qk", [P, 4, HALF])
            v1 = sb(f"{name}_v1", [P, 2, heads, step])
            s_sb = sb(f"{name}_s", [P, NB, HPC * 2 * P])
            nmax = sb(f"{name}_nmax", [P, NB, HPC])
            den = sb(f"{name}_den", [P, NB, HPC])
            rden = sb(f"{name}_rden", [P, NB, HPC])
            pt = sb(f"{name}_pt", [P, 2, HPC * 2 * P])
            ot = sb(f"{name}_ot", [P, QC, SEQ])
            s_ps = [ps(f"{name}_sps0", [P, G]), ps(f"{name}_sps1", [P, 2 * G])]
            pt_ps = ps(f"{name}_ptps", [P, 2 * G])
            o_ps = ps(f"{name}_ops", [P, G])
            p_ps = [ps(f"{name}_pps{j}", [P, HALF]) for j in (0, 1)]
            if rotary:
                sq = sb(f"{name}_sq", [P, 4, HALF])
                raw = sb(f"{name}_raw", [P, 4, HALF])
                turn = sb(f"{name}_turn", [P, 4, HALF])
            H4, U = range(4), range(NU)

            def kind(what, names):
                return Steps(ctx, nc, f"{name}_{what}", names)

            proj, vproj, scores, turned, values, outs = (kind(k, r) for k, r in (
                ("proj", H4), ("vproj", [0]), ("scores", U), ("turned", U), ("values", U), ("outs", [0])))
            vcopied, expd, ocopied = kind("vcopied", [0]), kind("expd", U), kind("ocopied", U)
            qkdone, biased, maxed, inverted, ptcopied, added = (kind(k, r) for k, r in (
                ("qkdone", H4), ("biased", U), ("maxed", U), ("inverted", U), ("ptcopied", U), ("added", [0])))
            staged, normed = kind("staged", [0]), kind("normed", U)
            if rotary:
                norms, rots, squared, logs, rnorms, rawed, clipped, sined, cosed, summed = (kind(k, H4) for k in (
                    "norms", "rots", "squared", "logs", "rnorms", "rawed", "clipped", "sined", "cosed", "summed"))
            zeroed = sem(f"{name}_zeroed")
            block = ctx.enter_context(nc.Block())
            LAST = BATCH - 1

            def chunks(t):
                return t.rearrange("p (c t) -> p c t", t=SEQ)

            def sequences(eng, prepare, body):
                prepare(0)
                with eng.Fori(0, LAST) as i:
                    body(i, i + 1)
                body(LAST, None)

            @block.gpsimd
            def _(pool):
                for k in (staged, normed) + ((cosed, summed) if rotary else ()):
                    k.credit(pool)
                nc.gpsimd.memset(v1[:], 0.0).then_inc(zeroed, 1)

                def stage_z(b):
                    pool.wait_ge(vproj.sem, vproj.at(b, 0, 1))
                    nc.gpsimd.tensor_copy(zs[:], src[:, bass.ds(b * SEQ, SEQ)]).then_inc(staged.sem, staged.step(0))

                def cosine(b, k):
                    pool.wait_ge(rawed.sem, rawed.at(b, k))
                    nc.gpsimd.tensor_tensor(chunks(turn[:, k, :]), chunks(raw[:, k, :]),
                                            trig[:, k // 2, 0:1, :].to_broadcast([P, 2, SEQ]), ALU.mult)\
                        .then_inc(cosed.sem, cosed.step(k))

                def add_sine(b, k):
                    pool.wait_ge(cosed.sem, cosed.at(b, k))
                    pool.wait_ge(sined.sem, sined.at(b, k))
                    nc.gpsimd.tensor_tensor(turn[:, k, :], turn[:, k, :], raw[:, k, :], ALU.add)\
                        .then_inc(summed.sem, summed.step(k))

                def normalise(i, u):
                    c, qt = units[u]
                    nk = (qt + 1) * P
                    s = s_sb[:, u % NB, 0:HPC * nk].rearrange("p (h k) -> p h k", h=HPC)
                    pool.wait_ge(inverted.sem, inverted.at(i, u))
                    nc.gpsimd.tensor_tensor(s, s, rden[:, u % NB, :].rearrange("p (h k) -> p h k", k=1)
                                            .to_broadcast([P, HPC, nk]), ALU.mult).then_inc(normed.sem, normed.step(u))

                def prepare(b):
                    stage_z(b)
                    if rotary:
                        for k in (0, 2):
                            for f in (cosine, add_sine):
                                f(b, k)
                                f(b, k + 1)

                def body(i, b):
                    for u in U:
                        normalise(i, u)
                    if b is not None:
                        prepare(b)

                sequences(pool, prepare, body)

            @block.tensor
            def _(pe):
                for k in (proj, vproj, scores, turned, values, outs) + ((norms, rots) if rotary else ()):
                    k.credit(pe)

                def project(b, k):
                    if k < 2:
                        pe.wait_ge(vcopied.sem, vcopied.at(b, 0, 1))
                    elif rotary:
                        pe.wait_ge(sined.sem, sined.at(b, k - 2))
                    else:
                        pe.wait_ge(qkdone.sem, qkdone.at(b, k - 2))
                    for c in range(2):
                        mm = nc.tensor.matmul(p_ps[k % 2][:, c * SEQ:(c + 1) * SEQ], qk_w[:, k // 2, k % 2 * 2 + c, :],
                                              src[:, bass.ds(b * SEQ, SEQ)], start=True, stop=True)
                    mm.then_inc(proj.sem, proj.step(k))

                def norm(b, k):
                    pe.wait_ge(squared.sem, squared.at(b, k))
                    pe.wait_ge(rawed.sem, rawed.at(b, k))
                    nc.tensor.matmul(p_ps[k % 2][:], blk[:], sq[:, k, :], start=True, stop=True)\
                        .then_inc(norms.sem, norms.step(k))

                def rotate(b, k):
                    pe.wait_ge(clipped.sem, clipped.at(b, k))
                    nc.tensor.matmul(p_ps[k % 2][:], rot[:], raw[:, k, :], start=True, stop=True)\
                        .then_inc(rots.sem, rots.step(k))

                def make_v(b):
                    pe.wait_ge(staged.sem, staged.at(b, 0))
                    last = sined if rotary else qkdone
                    pe.wait_ge(last.sem, last.at(b, 3))
                    for kt in range(2):
                        mm = nc.tensor.matmul(p_ps[kt][:, 0:VW], zs[:, kt * P:(kt + 1) * P], v_w[:],
                                              start=True, stop=rotary)
                        if not rotary:
                            mm = nc.tensor.matmul(p_ps[kt][:, 0:VW], C.ones[:, 0:P], v_b[:], start=False, stop=True)
                    mm.then_inc(vproj.sem, vproj.step(0))

                def score(i, u):
                    c, qt = units[u]
                    nk = (qt + 1) * P
                    if u == 0:
                        pe.wait_ge(qkdone.sem, qkdone.at(i, 3))
                    pe.wait_ge(biased.sem, biased.at(i, (u - 2) % NU, 0 if u >= 2 else 1))
                    at = slice(c * step, c * step + dh)
                    for j in range(HPC):
                        jj, cc = divmod(j, 2)
                        mm = nc.tensor.matmul(s_ps[qt][:, j * nk:(j + 1) * nk],
                                              qk[at, jj, cc * SEQ + qt * P:cc * SEQ + (qt + 1) * P],
                                              qk[at, 2 + jj, cc * SEQ:cc * SEQ + nk], start=True, stop=True)
                    mm.then_inc(scores.sem, scores.step(u))

                def turn_unit(i, u):
                    c, qt = units[u]
                    pe.wait_ge(normed.sem, normed.at(i, u))
                    pe.wait_ge(ptcopied.sem, ptcopied.at(i, (u - 1) % NU, 0 if u else 1))
                    for k in range(HPC * (qt + 1)):
                        mm = nc.tensor.transpose(pt_ps[:, k * P:(k + 1) * P], s_sb[:, u % NB, k * P:(k + 1) * P], C.ident[:])
                    mm.then_inc(turned.sem, turned.step(u))

                def value(i, u):
                    c, qt = units[u]
                    if u == 0:
                        pe.wait_ge(vcopied.sem, vcopied.at(i, 0))
                        pe.wait_ge(added.sem, added.at(i, 0, 1))
                    else:
                        pe.wait_ge(ocopied.sem, ocopied.at(i, u - 1))
                    pe.wait_ge(ptcopied.sem, ptcopied.at(i, u))
                    for j in range(HPC):
                        row = j * step % P
                        o = o_ps[row:row + step, j * step // P * P:(j * step // P + 1) * P]
                        for kt in range(qt + 1):
                            mm = nc.tensor.matmul(o, v1[:, kt, c * HPC + j, :],
                                                  pt[:, u % 2, (j * (qt + 1) + kt) * P:(j * (qt + 1) + kt + 1) * P],
                                                  start=kt == 0, stop=kt == qt, tile_position=(0, row))
                    mm.then_inc(values.sem, values.step(u))

                def out(i):
                    pe.wait_ge(ocopied.sem, ocopied.at(i, NU - 1))
                    for f in range(QC):
                        mm = nc.tensor.matmul(o_ps[:, 0:SEQ], o_w[:, f, :], ot[:, f, :], start=f == 0, stop=f == QC - 1)
                    mm.then_inc(outs.sem, outs.step(0))

                def halves(b, k):
                    norm(b, k)
                    norm(b, k + 1)
                    rotate(b, k)
                    rotate(b, k + 1)

                def prepare(b):
                    for k in (0, 2):
                        project(b, k)
                        project(b, k + 1)
                        if rotary:
                            halves(b, k)
                    make_v(b)

                def body(i, b):
                    for u in U:
                        score(i, u)
                        if u >= 2:
                            turn_unit(i, u - 2)
                        if u >= 3:
                            value(i, u - 3)
                    if b is not None:
                        project(b, 0)
                    turn_unit(i, NU - 2)
                    if b is not None:
                        project(b, 1)
                    value(i, NU - 3)
                    if b is not None and rotary:
                        norm(b, 0)
                    turn_unit(i, NU - 1)
                    if b is not None and rotary:
                        norm(b, 1)
                    value(i, NU - 2)
                    if b is not None:
                        if rotary:
                            rotate(b, 0)
                            rotate(b, 1)
                        else:
                            project(b, 2)
                            project(b, 3)
                    value(i, NU - 1)
                    if b is not None and rotary:
                        project(b, 2)
                        project(b, 3)
                    out(i)
                    if b is not None:
                        if rotary:
                            halves(b, 2)
                        make_v(b)

                sequences(pe, prepare, body)

            @block.scalar
            def _(act):
                for k in (vcopied, expd, ocopied) + ((squared, logs, rnorms) if rotary else ()):
                    k.credit(act)
                act.preload_act_table_set("natural_log_exp_and_others")
                act.wait_ge(zeroed, 1)

                def square(b, k):
                    act.wait_ge(proj.sem, proj.at(b, k))
                    nc.scalar.activation(sq[:, k, :], p_ps[k % 2][:], ACT.Square).then_inc(squared.sem, squared.step(k))

                def rnorm(b, k):
                    act.wait_ge(clipped.sem, clipped.at(b, k))
                    nc.scalar.activation(sq[:, k, :], sq[:, k, :], ACT.Ln).then_inc(logs.sem, logs.step(k))
                    act.wait_ge(logs.sem, logs.at(b, k))
                    nc.scalar.activation(sq[:, k, :], sq[:, k, :], ACT.Exp, scale=-0.5, bias=undo[:])\
                        .then_inc(rnorms.sem, rnorms.step(k))

                def copy_v(b):
                    act.wait_ge(vproj.sem, vproj.at(b, 0))
                    for kt in range(2):
                        a = nc.scalar.activation(v1[:, kt, :, 0:dh], p_ps[kt][:, 0:VW].rearrange("p (h d) -> p h d", d=dh), ACT.Copy)
                    a.then_inc(vcopied.sem, vcopied.step(0))

                def exps(i, u):
                    c, qt = units[u]
                    nk = (qt + 1) * P
                    act.wait_ge(maxed.sem, maxed.at(i, u))
                    for j in range(HPC):
                        s = s_sb[:, u % NB, j * nk:(j + 1) * nk]
                        a = nc.scalar.activation(s, s, ACT.Exp, bias=nmax[:, u % NB, j:j + 1], accum_out=den[:, u % NB, j:j + 1])
                    a.then_inc(expd.sem, expd.step(u))

                def copy_o(i, u):
                    c, qt = units[u]
                    act.wait_ge(values.sem, values.at(i, u))
                    if u == 0:
                        act.wait_ge(outs.sem, outs.at(i, 0, 1))
                    nc.scalar.activation(ot[:, c * OC:(c + 1) * OC, qt * P:(qt + 1) * P],
                                         o_ps[:, 0:OC * P].rearrange("p (f q) -> p f q", f=OC), ACT.Copy)\
                        .then_inc(ocopied.sem, ocopied.step(u))

                def prepare(b):
                    if rotary:
                        for k in (0, 2):
                            for f in (square, rnorm):
                                f(b, k)
                                f(b, k + 1)
                    copy_v(b)

                def body(i, b):
                    for u in U:
                        exps(i, u)
                        if u >= 3:
                            copy_o(i, u - 3)
                    if b is not None and rotary:
                        square(b, 0)
                        square(b, 1)
                    copy_o(i, NU - 3)
                    if b is not None and rotary:
                        rnorm(b, 0)
                        rnorm(b, 1)
                    copy_o(i, NU - 2)
                    copy_o(i, NU - 1)
                    if b is not None:
                        if rotary:
                            for f in (square, rnorm):
                                f(b, 2)
                                f(b, 3)
                        copy_v(b)

                sequences(act, prepare, body)

            @block.vector
            def _(dve):
                for k in (qkdone, biased, maxed, inverted, ptcopied, added) + ((rawed, clipped, sined) if rotary else ()):
                    k.credit(dve)
                v = nc.vector

                def add_bias(b, k):
                    dve.wait_ge(proj.sem, proj.at(b, k))
                    v.tensor_tensor(chunks(qk[:, k, :]), chunks(p_ps[k % 2][:]),
                                    qk_b[:, k // 2, k % 2 * 2:k % 2 * 2 + 2].to_broadcast([P, 2, SEQ]), ALU.add)\
                        .then_inc(qkdone.sem, qkdone.step(k))

                def copy_raw(b, k):
                    dve.wait_ge(squared.sem, squared.at(b, k))
                    dve.wait_ge(summed.sem, summed.at(b, k, 1))
                    v.tensor_scalar(raw[:, k, :], p_ps[k % 2][:], qk_s[:, k // 2:k // 2 + 1], None, ALU.mult)\
                        .then_inc(rawed.sem, rawed.step(k))

                def clip(b, k):
                    dve.wait_ge(norms.sem, norms.at(b, k))
                    v.tensor_scalar(sq[:, k, :], p_ps[k % 2][:], 1e-24, 2.0 ** 24, ALU.max, ALU.mult)\
                        .then_inc(clipped.sem, clipped.step(k))

                def sine(b, k):
                    dve.wait_ge(rots.sem, rots.at(b, k))
                    dve.wait_ge(cosed.sem, cosed.at(b, k))
                    v.tensor_tensor(chunks(raw[:, k, :]), chunks(p_ps[k % 2][:]),
                                    trig[:, k // 2, 1:2, :].to_broadcast([P, 2, SEQ]), ALU.mult).then_inc(sined.sem, sined.step(k))

                def scale_qk(b, k):
                    dve.wait_ge(summed.sem, summed.at(b, k))
                    dve.wait_ge(rnorms.sem, rnorms.at(b, k))
                    v.tensor_tensor(qk[:, k, :], turn[:, k, :], sq[:, k, :], ALU.mult).then_inc(qkdone.sem, qkdone.step(k))

                def bias_scores(i, u):
                    c, qt = units[u]
                    nk = (qt + 1) * P
                    s = s_sb[:, u % NB, 0:HPC * nk].rearrange("p (h k) -> p h k", h=HPC)
                    t = (tab[:, 0:1] if rotary else tab[:, c * HPC:(c + 1) * HPC])[:, :, qt * P:qt * P + nk]
                    dve.wait_ge(scores.sem, scores.at(i, u))
                    dve.wait_ge(turned.sem, turned.at(i, (u - NB) % NU, 0 if u >= NB else 1))
                    v.scalar_tensor_tensor(s, s_ps[qt][:, 0:HPC * nk].rearrange("p (h k) -> p h k", h=HPC), scale,
                                           t.to_broadcast([P, HPC, nk]) if rotary else t, ALU.mult, ALU.add)\
                        .then_inc(biased.sem, biased.step(u))

                def maxima(i, u):
                    c, qt = units[u]
                    nk = (qt + 1) * P
                    dve.wait_ge(biased.sem, biased.at(i, u))
                    v.tensor_reduce(nmax[:, u % NB, :], s_sb[:, u % NB, 0:HPC * nk].rearrange("p (h k) -> p h k", h=HPC),
                                    X, ALU.max, negate=True).then_inc(maxed.sem, maxed.step(u))

                def invert(i, u):
                    dve.wait_ge(expd.sem, expd.at(i, u))
                    v.reciprocal(rden[:, u % NB, :], den[:, u % NB, :]).then_inc(inverted.sem, inverted.step(u))

                def copy_pt(i, u):
                    c, qt = units[u]
                    n = HPC * (qt + 1) * P
                    dve.wait_ge(turned.sem, turned.at(i, u))
                    dve.wait_ge(values.sem, values.at(i, (u - 2) % NU, 0 if u >= 2 else 1))
                    v.tensor_copy(pt[:, u % 2, 0:n], pt_ps[:, 0:n]).then_inc(ptcopied.sem, ptcopied.step(u))

                def add_out(i):
                    at = bass.ds(i * SEQ, SEQ)
                    dve.wait_ge(outs.sem, outs.at(i, 0))
                    if rotary:
                        ins = v.tensor_tensor(res[:, at], res[:, at], o_ps[:, 0:SEQ], ALU.add)
                    else:
                        ins = v.scalar_tensor_tensor(res[:, at], o_ps[:, 0:SEQ], o_b[:], res[:, at], ALU.add, ALU.add)
                    ins.then_inc(added.sem, added.step(0))

                def prepare(b):
                    for k in (0, 2):
                        for f in ((copy_raw, clip, sine, scale_qk) if rotary else (add_bias,)):
                            f(b, k)
                            f(b, k + 1)

                def body(i, b):
                    for u in U:
                        bias_scores(i, u)
                        if u:
                            invert(i, u - 1)
                        maxima(i, u)
                        if u >= 2:
                            copy_pt(i, u - 2)
                    invert(i, NU - 1)
                    if b is None:
                        copy_pt(i, NU - 2)
                        copy_pt(i, NU - 1)
                    elif rotary:
                        copy_raw(b, 0)
                        copy_pt(i, NU - 2)
                        copy_raw(b, 1)
                        clip(b, 0)
                        copy_pt(i, NU - 1)
                        clip(b, 1)
                        for f in (sine, scale_qk):
                            f(b, 0)
                            f(b, 1)
                        copy_raw(b, 2)
                        copy_raw(b, 3)
                    else:
                        add_bias(b, 0)
                        copy_pt(i, NU - 2)
                        add_bias(b, 1)
                        copy_pt(i, NU - 1)
                        add_bias(b, 2)
                        add_bias(b, 3)
                    add_out(i)
                    if b is not None and rotary:
                        for f in (clip, sine, scale_qk):
                            f(b, 2)
                            f(b, 3)

                sequences(dve, prepare, body)


def alibi_attention(nc, x, z, w, C):
    attention(nc, "a1", z, x, w, C, 16, 8, 8 ** -0.5, False)


def shift_tokens(nc, name, src, dst):
    with ExitStack() as ctx:
        block = ctx.enter_context(nc.Block())
        seqs = lambda t, lo: t[lo:lo + 64, :].rearrange("p (b t) -> p b t", b=BATCH)

        @block.scalar
        def _(act):
            nc.scalar.activation(dst[0:64, :], src[0:64, :], ACT.Copy)

        @block.vector
        def _(dve):
            nc.vector.tensor_copy(seqs(dst, 64)[:, :, 1:], seqs(src, 64)[:, :, :SEQ - 1])

        @block.gpsimd
        def _(pool):
            nc.gpsimd.memset(seqs(dst, 64)[:, :, 0:1], 0.0)


def local_transformer(nc, x, z, w, C):
    HID = w["l3_w1"].shape[2] // 2
    sizes = [min(P, HID - c) for c in range(0, HID, P)]
    HC = len(sizes)
    with ExitStack() as stage:
        sb, ps, sem = open_tools(stage, nc)
        h = sb("l3_h", [P, T])
        for l in range(2):
            shift_tokens(nc, f"l3{l}a", z, h)
            attention(nc, f"l3{l}", h, z, w, C, 8, 64, 1.0, True)
            shift_tokens(nc, f"l3{l}f", z, h)
            with ExitStack() as ctx:
                sb, ps, sem = open_tools(ctx, nc)
                w1 = sb(f"l3{l}_w1", [P, 2 * HID])
                w2 = sb(f"l3{l}_w2", [P, HC, P])
                b1 = sb(f"l3{l}_b1", [P, 2, HC])
                col = sb(f"l3{l}_col", [P, 3])
                pairs = [(w1[:], w["l3_w1"][l]), (col[:], w["l3_col"][l])]
                for c, k in enumerate(sizes):
                    pairs.append((w2[:k, c, :], w["l3_w2"][l, c * P:c * P + k, :]))
                    for a in range(2):
                        pairs.append((b1[:k, a, c:c + 1], w["l3_b1"][l, a * HID + c * P:a * HID + c * P + k, :]))
                load_tiles(nc, f"l3{l}_ff", pairs)
                layernorm(nc, f"l3{l}_ln", h, h, C, col[:, 0:1], col[:, 1:2])
                gated_ffn(nc, f"l3{l}_ff", z, h, w1[:, HID:], w1[:, :HID], w2, sizes, ACT.Gelu, C,
                          b1[:, 1, :], b1[:, 0, :], col[:, 2:3])
        residual_add(nc, "l3", x, z)


def attn_layout(a, w):
    q = lambda k: a["L1_attn_" + k]
    win, bin_ = q("w_in"), q("b_in").reshape(1, 384)

    def spread(m):
        r = m.shape[0]
        t = np.zeros((r, 4, 4, 32), m.dtype)
        t[:, :, :, :8] = m.reshape(r, 4, 4, 8).transpose(0, 2, 1, 3)
        return t.reshape(r, 4, P)

    w["a1_qkw"] = np.stack([spread(win[:, :128]), spread(win[:, 128:256])], 1)
    w["a1_qkb"] = np.stack([spread(bin_[:, :128])[0].T, spread(bin_[:, 128:256])[0].T], 1)[..., None]
    w["a1_vw"] = win[:, 256:]
    w["a1_vb"] = bin_[:, 256:]
    w["a1_ow"] = np.zeros((4, 32, 4, P), np.float32)
    w["a1_ow"][:, :8] = q("w_out").reshape(4, 4, 8, P).transpose(1, 2, 0, 3)
    w["a1_ow"] = w["a1_ow"].reshape(P, 4, P)
    w["a1_ob"] = q("b_out").reshape(P, 1)
    q = lambda k: a["L3_ffn_" + k]
    for l in range(2):
        m = q("wqkv")[l]
        w[f"l3{l}_qkw"] = m[:, :1024].reshape(P, 2, 2, 4, 64).transpose(0, 1, 3, 2, 4).reshape(P, 2, 4, P)
        w[f"l3{l}_vw"] = m[:, 1024:]
        w[f"l3{l}_ow"] = q("wo")[l].reshape(4, P, P).transpose(1, 0, 2)
        w[f"l3{l}_qks"] = np.stack([np.tile(q("q_scale")[l], 2), np.tile(q("k_scale")[l], 2)], 1)
    w["l3_w1"], w["l3_w2"] = q("w1"), q("w2")
    w["l3_b1"] = q("b1")[:, :, None]
    w["l3_col"] = np.stack([q("ln_g"), q("ln_b"), q("b2")], 2)


def attn_tables():
    f = np.float32
    i, j = np.arange(SEQ)[:, None], np.arange(SEQ)[None, :]

    def two_tiles(m):
        return np.moveaxis(np.concatenate([m[..., :P, :P], m[..., P:, :]], -1), -2, 0)

    slopes = np.array([2.0 ** (-0.5 * (h + 1)) for h in range(16)], f)
    alibi = np.where(j <= i, slopes[:, None, None] * (j - i).astype(f), f(MASKED)).astype(f)
    band = np.where((j <= i) & (i <= j + 64), f(0), f(MASKED)).astype(f)[None]
    half = np.arange(0, 64, 2, dtype=f)
    t = np.arange(SEQ, dtype=f)
    freqs = t[:, None] * (f(1) / f(10000) ** (half / f(64)))[None]
    freqs = np.concatenate([freqs, freqs], -1)
    base = (half + f(0.4 * 64)) / f(1.4 * 64)
    sc = base[None, :] ** ((t - SEQ // 2) / f(32))[:, None]
    sc = np.concatenate([sc, sc], -1)
    cos, sin = np.cos(freqs), np.sin(freqs)
    parts = [[f(8) * cos * sc, f(8) * sin * sc], [cos / sc, sin / sc]]
    trig = np.stack([np.stack([np.tile(m.T, (2, 1)) for m in r], 1) for r in parts], 1)
    rot = np.zeros((P, P), f)
    for b in (0, 64):
        for d in range(32):
            rot[b + 32 + d, b + d] = -1
            rot[b + d, b + 32 + d] = 1
    blk = np.kron(np.eye(2, dtype=f), np.ones((64, 64), f))
    return {"c_alibi": two_tiles(alibi), "c_band": two_tiles(band), "c_trig": trig.astype(f), "c_rot": rot, "c_blk": blk,
            "c_undo": np.full((P, 1), 12 * np.log(2.0), f)}


def permutation_scan(nc, x, z, w, C):
    NH, N = 4, 8
    NN = N * N
    NT = T // P
    M = NT * NH
    BH = BATCH * NH
    REC = N * (N + 1)
    STATE = N + 1
    md = nc.dram_tensor("p_records", (BATCH, NH, SEQ, REC), F32).ap()
    with ExitStack() as stage:
        sb, ps, sem = open_tools(stage, nc)
        soft = sb("p_soft", [P, M, NN])
        gates = sb("p_gates", [P, NT, 3, NH * N])

        with ExitStack() as mid:
            sb, ps, sem = open_tools(mid, nc)
            xn = sb("p_xn", [P, T])
            lnw = sb("p_ln", [P, 2])
            pw = sb("p_w", [P, 3 * NH * N + NH * NN])
            pb = sb("p_b", [1, 3 * NH * N + NH * NN])
            load_tiles(nc, "p", [(lnw[:], w["l0_ln"]), (pw[:], w["l0_w"]), (pb[:], w["l0_b"])])
            layernorm(nc, "p_ln", z, xn, C, lnw[:, 0:1], lnw[:, 1:2])
            with ExitStack() as ctx:
                sb, ps, sem = open_tools(ctx, nc)
                xs = sb("p_xs", [P, 2, G])
                TG = G // P
                NG3 = 3 * NH * N
                p_ps = ps("p_ps", [P, 2, TG, 512])
                PE = Steps(ctx, nc, "p_pe", [("proj", j) for j in (0, 1)])
                AC = Steps(ctx, nc, "p_act", [("copy", j) for j in (0, 1)])
                PO = Steps(ctx, nc, "p_pool", [("stage", j) for j in (0, 1)])
                block = ctx.enter_context(nc.Block())

                @block.gpsimd
                def _(pool):
                    PO.credit(pool)
                    with pool.Fori(0, NG // 2) as i:
                        for j in (0, 1):
                            pool.wait_ge(PE.sem, PE.at(i, ("proj", j), 1))
                            nc.gpsimd.tensor_copy(xs[:, j, :], xn[:, bass.ds(i * (2 * G) + j * G, G)])\
                                .then_inc(PO.sem, PO.step(("stage", j)))
                    PO.done()

                @block.tensor
                def _(pe):
                    PE.credit(pe)
                    with pe.Fori(0, NG // 2) as i:
                        for j in (0, 1):
                            pe.wait_ge(PO.sem, PO.at(i, ("stage", j)))
                            pe.wait_ge(AC.sem, AC.at(i, ("copy", j), 1))
                            for t in range(TG):
                                o = p_ps[:, j, t, 0:NG3 + NH * NN]
                                nc.tensor.matmul(o, xs[:, j, t * P:(t + 1) * P], pw[:], start=True, stop=False)
                                mm = nc.tensor.matmul(o, C.ones[:, 0:P], pb[:], start=False, stop=True)
                            mm.then_inc(PE.sem, PE.step(("proj", j)))
                    PE.done()

                @block.scalar
                def _(act):
                    AC.credit(act)
                    with act.Fori(0, NG // 2) as i:
                        for j in (0, 1):
                            act.wait_ge(PE.sem, PE.at(i, ("proj", j)))
                            nc.scalar.activation(gates[:, bass.ds(i * (2 * TG) + j * TG, TG), :, :].rearrange("p t a n -> p t (a n)"),
                                                 p_ps[:, j, :, 0:NG3], ACT.Copy)
                            nc.scalar.activation(soft[:, bass.ds(i * (2 * TG * NH) + j * (TG * NH), TG * NH), :]
                                                 .rearrange("p (t h) k -> p t (h k)", h=NH),
                                                 p_ps[:, j, :, NG3:NG3 + NH * NN], ACT.Copy)\
                                .then_inc(AC.sem, AC.step(("copy", j)))
                    AC.done()

        with ExitStack() as ctx:
            sb, ps, sem = open_tools(ctx, nc)
            MD = 80
            MG = M - MD
            vec = sb("p_vec", [P, M, N])
            rows = sb("p_rows", [P, M, N])
            used = sb("p_used", [P, M, N])
            taken = sb("p_taken", [P, M, N])
            one = sb("p_one", [P, M])
            sel = sb("p_sel", [P, N, M, N])
            falling = sb("p_falling", [P, N])
            rec = sb("p_rec", [P, M, REC])
            prod = rec[:].rearrange("p m r -> p (m r)")[:, 0:MD * NN].rearrange("p (m k) -> p m k", k=NN)
            prod_g = sb("p_prodg", [P, MG, NN])
            col = sb("p_col", [P, M, N])
            load_tiles(nc, "p2", [(falling[:], w["c_fall"])])
            vstep = sem("p_vstep")
            centred = sem("p_centred")
            expd = sem("p_expd")
            sigd = sem("p_sigd")
            picked = sem("p_picked")
            multiplied = sem("p_multiplied")
            summed = sem("p_summed")
            recorded = sem("p_recorded")
            stored = sem("p_stored")
            block = ctx.enter_context(nc.Block())
            by_row = lambda t: t[:].rearrange("p m (i j) -> p m i j", i=N)
            by_col = lambda t: t[:].rearrange("p m (i j) -> p m j i", i=N)
            wide = lambda t: t.rearrange("p m (i k) -> p m i k", k=1).to_broadcast([P, M, N, N])
            wide1 = lambda t: t[:].rearrange("p (m k) -> p m k", k=1).to_broadcast([P, M, N])
            fall = falling[:].rearrange("p (m i) -> p m i", m=1).to_broadcast([P, M, N])

            @block.gpsimd
            def _(pool):
                for k in range(N):
                    pool.wait_ge(picked, k + 1)
                    if k:
                        pool.wait_ge(summed, k)
                    nc.gpsimd.tensor_tensor(prod_g[:].rearrange("p m (i j) -> p m i j", i=N),
                                            soft[:, MD:, :].rearrange("p m (i j) -> p m i j", i=N),
                                            sel[:, k, MD:, :].rearrange("p m (i k) -> p m i k", k=1).to_broadcast([P, MG, N, N]),
                                            ALU.mult).then_inc(multiplied, 1)

            @block.scalar
            def _(act):
                nc.scalar.activation(gates[:, :, 0:2, :], gates[:, :, 0:2, :], ACT.Sigmoid).then_inc(sigd, 1)
                act.wait_ge(centred, 1)
                nc.scalar.activation(soft[:], soft[:], ACT.Exp).then_inc(expd, 1)

            @block.vector
            def _(dve):
                v = nc.vector
                done = [0]

                def then(ins):
                    done[0] += 1
                    ins.then_inc(vstep, 1)
                    dve.wait_ge(vstep, done[0])

                then(v.tensor_reduce(vec[:], by_row(soft), X, ALU.max))
                then(v.tensor_tensor(by_row(soft), by_row(soft), wide(vec[:]), ALU.subtract))
                then(v.tensor_reduce(vec[:], by_col(soft), X, ALU.max))
                v.tensor_tensor(by_col(soft), by_col(soft), wide(vec[:]), ALU.subtract).then_inc(centred, 1)
                dve.wait_ge(expd, 1)
                for _ in range(5):
                    for view in (by_row, by_col):
                        then(v.tensor_reduce(vec[:], view(soft), X, ALU.add))
                        then(v.reciprocal(vec[:], vec[:]))
                        then(v.tensor_tensor(view(soft), view(soft), wide(vec[:]), ALU.mult))

                then(v.tensor_reduce(vec[:], by_row(soft), X, ALU.max))
                for k in range(N):
                    then(v.tensor_reduce(one[:], vec[:], X, ALU.max))
                    then(v.tensor_tensor(rows[:], vec[:], wide1(one), ALU.is_equal))
                    then(v.tensor_tensor(rows[:], rows[:], fall, ALU.mult))
                    then(v.tensor_reduce(one[:], rows[:], X, ALU.max))
                    then(v.tensor_tensor(sel[:, k], fall, wide1(one), ALU.is_equal))
                    v.scalar_tensor_tensor(vec[:], sel[:, k], -4.0, vec[:], ALU.mult, ALU.add).then_inc(picked, 1)
                    dve.wait_ge(picked, k + 1)

                then(v.memset(used[:], 0.0))
                for k in range(N):
                    sk = sel[:, k, :MD, :].rearrange("p m (i k) -> p m i k", k=1).to_broadcast([P, MD, N, N])
                    then(v.tensor_tensor(prod.rearrange("p m (i j) -> p m i j", i=N),
                                         soft[:, :MD, :].rearrange("p m (i j) -> p m i j", i=N), sk, ALU.mult))
                    then(v.tensor_reduce(rows[:, :MD, :], prod.rearrange("p m (i j) -> p m j i", i=N), X, ALU.add))
                    dve.wait_ge(multiplied, k + 1)
                    v.tensor_reduce(rows[:, MD:, :], prod_g[:].rearrange("p m (i j) -> p m j i", i=N), X, ALU.add)\
                        .then_inc(summed, 1)
                    dve.wait_ge(summed, k + 1)
                    then(v.tensor_tensor(rows[:], rows[:], used[:], ALU.add))
                    then(v.tensor_reduce(one[:], rows[:], X, ALU.max))
                    then(v.tensor_tensor(rows[:], rows[:], wide1(one), ALU.is_equal))
                    then(v.tensor_tensor(rows[:], rows[:], fall, ALU.mult))
                    then(v.tensor_reduce(one[:], rows[:], X, ALU.max))
                    then(v.tensor_tensor(taken[:], fall, wide1(one), ALU.is_equal))
                    then(v.scalar_tensor_tensor(used[:], taken[:], -4.0, used[:], ALU.mult, ALU.add))
                    if k == 0:
                        then(v.tensor_tensor(col[:], sel[:, k], wide1(one), ALU.mult))
                    else:
                        then(v.tensor_tensor(taken[:], sel[:, k], wide1(one), ALU.mult))
                        then(v.tensor_tensor(col[:], col[:], taken[:], ALU.add))

                dve.wait_ge(sigd, 1)
                gv = lambda a: gates[:, :, a, :].rearrange("p t (h i) -> p t h i", h=NH)
                vt = lambda t: t[:].rearrange("p (t h) i -> p t h i", h=NH)
                then(v.tensor_scalar(vt(vec), gv(0), 2.0, -1.0, ALU.mult, ALU.add))
                then(v.tensor_tensor(vt(vec), vt(vec), gv(1), ALU.mult))
                then(v.tensor_scalar(vt(rows), gv(1), -1.0, 1.0, ALU.mult, ALU.add))
                then(v.tensor_tensor(vt(rows), vt(rows), gv(2), ALU.mult))
                body = rec[:].rearrange("p m (i q) -> p m i q", i=N)[:, :, :, 0:N]
                tail = rec[:].rearrange("p m (i q) -> p m i q", i=N)[:, :, :, N]
                fall_j = falling[:].rearrange("p (m i j) -> p m i j", m=1, i=1).to_broadcast([P, M, N, N])
                then(v.tensor_tensor(body, fall_j, wide(col[:]), ALU.is_equal))
                then(v.tensor_tensor(body, body, by_row(soft), ALU.add))
                then(v.tensor_tensor(body, body, by_row(soft), ALU.subtract))
                then(v.tensor_tensor(body, body, wide(vec[:]), ALU.mult))
                v.tensor_copy(tail, rows[:]).then_inc(recorded, 1)

            def store(eng, tiles):
                eng.wait_ge(recorded, 1)
                for t in tiles:
                    b, s = t // 2, t % 2 * P
                    eng.dma_start(md[b, :, s:s + P, :].rearrange("h s r -> s h r"), rec[:, t * NH:(t + 1) * NH, :])\
                        .then_inc(stored, 16)
                eng.wait_ge(stored, 16 * NT)

            @block.sync
            def _(sp):
                store(sp, range(NT))

    with ExitStack() as stage:
        sb, ps, sem = open_tools(stage, nc)
        SL = P // N
        NSH = SEQ // SL
        state = sb("p_state", [BH, SEQ + 1, STATE])
        ow = sb("p_ow", [P, SL, NH, P])
        ob = sb("p_ob", [P, 1])
        with ExitStack() as ctx:
            sb, ps, sem = open_tools(ctx, nc)
            steps = sb("p_steps", [BH, SEQ, REC])
            prod = sb("p_prod", [BH, REC])
            LOADS = 8
            UN = 8
            loaded = [sem(f"p_loaded{q}") for q in range(LOADS)]
            oload = sem("p_oload")
            VE = Steps(ctx, nc, "p_dve", [(s, k) for k in range(UN) for s in ("mult", "sum")])
            start = sem("p_start")
            block = ctx.enter_context(nc.Block())
            mdv = md.rearrange("b h s r -> (b h) s r")

            @block.sync
            def _(sp):
                for q in range(LOADS):
                    at = slice(q * SEQ // LOADS, (q + 1) * SEQ // LOADS)
                    sp.dma_start(steps[:, at, :], mdv[:, at, :]).then_inc(loaded[q], 16)
                sp.dma_start(ow[:], w["l0_ow"]).then_inc(oload, 16)
                sp.dma_start(ob[:], w["l0_ob"]).then_inc(oload, 16)
                sp.wait_ge(oload, 32)

            @block.vector
            def _(dve):
                VE.credit(dve)
                v = nc.vector
                v.memset(state[:], 1.0).then_inc(start, 1)
                dve.wait_ge(start, 1)
                v.memset(state[:, 0, 0:N], 0.0).then_inc(start, 1)
                dve.wait_ge(start, 2)
                for q in range(LOADS):
                    per = SEQ // LOADS // UN
                    dve.wait_ge(loaded[q], 16)
                    with dve.Fori(q * per, (q + 1) * per) as i:
                        for k in range(UN):
                            if k:
                                dve.wait_ge(VE.sem, VE.at(i, ("sum", k - 1)))
                            else:
                                dve.wait_ge(VE.sem, VE.at(i, ("sum", UN - 1), 1))
                            v.tensor_tensor(prod[:].rearrange("p (o i q) -> p o i q", o=1, i=N),
                                            steps[:, bass.ds(i * UN + k, 1), :].rearrange("p s (i q) -> p s i q", i=N),
                                            state[:, bass.ds(i * UN + k, 1), :].rearrange("p s (o q) -> p s o q", o=1)
                                            .to_broadcast([BH, 1, N, STATE]), ALU.mult)\
                                .then_inc(VE.sem, VE.step(("mult", k)))
                            dve.wait_ge(VE.sem, VE.at(i, ("mult", k)))
                            v.tensor_reduce(state[:, bass.ds(i * UN + k + 1, 1), 0:N],
                                            prod[:].rearrange("p (o i q) -> p o i q", o=1, i=N), X, ALU.add)\
                                .then_inc(VE.sem, VE.step(("sum", k)))
                    VE.done()
                    VE.said = 0

        with ExitStack() as ctx:
            sb, ps, sem = open_tools(ctx, nc)
            packed = sb("p_packed", [BH, SEQ * N])
            turned = sb("p_turned", [P, NH, BATCH, NSH])
            t_ps = ps("p_tps", [P, NSH, BH])
            o_ps = ps("p_ops", [P, 4, 512])
            s_packed = sem("p_s_packed")
            s_turned = sem("p_s_turned")
            s_copied = sem("p_s_copied")
            s_proj = sem("p_s_proj")
            s_added = sem("p_s_added")
            s_pre = sem("p_s_pre")
            block = ctx.enter_context(nc.Block())

            @block.scalar
            def _(act):
                nc.scalar.activation(packed[:].rearrange("p (s n) -> p s n", n=N), state[:, 1:, 0:N], ACT.Copy)\
                    .then_inc(s_packed, 1)
                act.wait_ge(s_turned, 1)
                for h in range(NH):
                    a = nc.scalar.activation(turned[:, h].rearrange("p b s -> p s b"),
                                             t_ps[:].rearrange("p s (b h) -> p h s b", h=NH)[:, h], ACT.Copy)
                a.then_inc(s_copied, 1)

            @block.tensor
            def _(pe):
                pe.wait_ge(s_packed, 1)
                for s in range(NSH):
                    mm = nc.tensor.transpose(t_ps[:, s, :], packed[:, s * P:(s + 1) * P], C.ident[0:BH, 0:BH])
                mm.then_inc(s_turned, 1)
                pe.wait_ge(s_copied, 1)
                for l in range(SL):
                    if l >= 4:
                        pe.wait_ge(s_added, l - 3)
                    for h in range(NH):
                        mm = nc.tensor.matmul(o_ps[:, l % 4, 0:BATCH * NSH], ow[:, l, h, :],
                                              turned[:, h].rearrange("p b s -> p (b s)"), start=h == 0, stop=h == NH - 1)
                    mm.then_inc(s_proj, 1)

            @block.vector
            def _(dve):
                nc.vector.scalar_tensor_tensor(x[:], z[:], ob[:], x[:], ALU.add, ALU.add).then_inc(s_pre, 1)
                dve.wait_ge(s_pre, 1)
                xv = x[:].rearrange("p (b s l) -> p b s l", b=BATCH, l=SL)
                for l in range(SL):
                    dve.wait_ge(s_proj, l + 1)
                    nc.vector.tensor_tensor(xv[:, :, :, l], xv[:, :, :, l],
                                            o_ps[:, l % 4, 0:BATCH * NSH].rearrange("p (b s) -> p b s", b=BATCH), ALU.add)\
                        .then_inc(s_added, 1)


def perm_layout(a, w):
    q = lambda k: a["L0_attn_" + k]
    w["l0_ln"] = np.stack([q("ln_w"), q("ln_b")], 1)
    w["l0_w"] = np.concatenate([q("sign_W"), q("gate_W"), q("in_W"), q("perm_W")], 1)
    w["l0_b"] = np.concatenate([q("sign_b"), q("gate_b"), q("in_b"), q("perm_b")])[None]
    ow = np.zeros((16, 8, 16, 4, P), np.float32)
    for l in range(16):
        ow[l, :, l] = q("out_W").reshape(4, 8, P).transpose(1, 0, 2)
    w["l0_ow"] = ow.reshape(P, 16, 4, P)
    w["l0_ob"] = q("out_b").reshape(P, 1)


def perm_tables():
    return {"c_fall": np.broadcast_to(np.arange(8, 0, -1, dtype=np.float32), (P, 8))}


def more_layout(a, w):
    perm_layout(a, w)
    attn_layout(a, w)
    ffn_layout(a, w)
    mamba_layout(a, w)


def shape_tables():
    return {**selector_tables(), **ffn_tables(), **attn_tables(), **perm_tables()}


STAGE = {"L0_attn": permutation_scan, "L0_ffn": int8_swiglu, "L1_attn": alibi_attention, "L1_ffn": mx_linear,
         "L2_attn": mamba_layer, "L2_ffn": moe, "L3_attn": mamba_stack, "L3_ffn": local_transformer}
ALL_STAGES = tuple(STAGE)


class Tables:
    pass


def transformer_program(nc, w, out, stages=ALL_STAGES):
    with ExitStack() as ctx:
        sb, ps, sem = open_tools(ctx, nc)
        C = Tables()
        C.mean = sb("c_mean", [P, P])
        C.ident = sb("c_ident", [P, P])
        C.eps = sb("c_eps", [P, 1])
        C.one = sb("c_one", [P, 1])
        C.warm = sb("c_warm", [P, 2])
        C.ones = sb("c_ones", [1, G])
        x = sb("x", [P, T])
        z = sb("z", [P, T])
        load_tiles(nc, "start", [(x[:], w["x"]), (C.mean[:], w["c_mean"]), (C.ident[:], w["c_ident"]),
                                 (C.eps[:], w["c_eps"]), (C.one[:], w["c_one"]), (C.ones[:], w["c_ones"])])
        for s in stages:
            layernorm(nc, f"{s}_ln", x, z, C)
            STAGE[s](nc, x, z, w, C)
        with ExitStack() as end:
            stored = end.enter_context(semaphore(nc, "stored"))
            block = end.enter_context(nc.Block())

            @block.sync
            def _(sp):
                sp.dma_start(out, x[:]).then_inc(stored, 16)
                sp.wait_ge(stored, 16)


def lay_out(inputs):
    a = {k: np.asarray(v) for k, v in inputs.items()}
    w = {"x": a["L0_attn_x"].reshape(T, P).T}
    for k, v in a.items():
        if k != "L0_attn_x":
            w[k] = v
    for k in ("L0_ffn_w_gate", "L0_ffn_w_up", "L0_ffn_w_down"):
        w[k] = a[k].T
    more_layout(a, w)
    w["c_mean"] = np.full((P, P), 1.0 / P, np.float32)
    w["c_ident"] = np.eye(P, dtype=np.float32)
    w["c_eps"] = np.full((P, 1), EPS, np.float32)
    w["c_one"] = np.full((P, 1), 1.0, np.float32)
    w["c_ones"] = np.full((1, G), 1.0, np.float32)
    w.update(shape_tables())
    return {k: np.ascontiguousarray(v) for k, v in w.items()}


def build(nc, w, stages=None):
    args = {k: nc.dram_tensor(f"in_{k}", v.shape, mybir.dt.from_np(v.dtype), kind="ExternalInput").ap()
            for k, v in w.items()}
    out = nc.dram_tensor("out", (P, T), F32, kind="ExternalOutput").ap()
    transformer_program(nc, args, out, stages or ALL_STAGES)
    return {f"in_{k}": v for k, v in w.items()}


def kernel(**inputs):
    import concourse.bacc as bacc
    from concourse.bass_utils import run_bass_kernel_spmd

    nc = bacc.Bacc("TRN2", target_bir_lowering=False, num_devices=1)
    arrays = build(nc, lay_out(inputs))
    r = run_bass_kernel_spmd(nc, [arrays], core_ids=[0])
    return np.ascontiguousarray(r.results[0]["out"].T).reshape(BATCH, SEQ, P)
```

```python
from contextlib import ExitStack, contextmanager

import numpy as np
import concourse.bass as bass
from concourse import mybir

F32 = mybir.dt.float32
I32 = mybir.dt.int32
BF16 = mybir.dt.bfloat16
ALU = mybir.AluOpType
ACT = mybir.ActivationFunctionType
X = mybir.AxisListType.X

P = 128
BATCH, SEQ = 16, 256
T = BATCH * SEQ
G = 512
NG = T // G
EPS = 1e-5
MASKED = -1e30


@contextmanager
def semaphore(nc, name):
    s = nc.alloc_semaphore(name)
    yield s
    nc.gpsimd.sem_clear(s)
    nc.release_semaphore(s)


class Steps:

    LEAD = 2

    def __init__(self, ctx, nc, name, steps):
        self.sem = ctx.enter_context(semaphore(nc, name))
        self.names = {s: n for n, s in enumerate(steps)}
        assert len(self.names) == len(steps)
        self.n = len(steps)
        self.order = list(steps)
        self.said = 0

    def credit(self, eng):
        eng.sem_inc(self.sem, self.LEAD * self.n)

    def step(self, name):
        assert self.order[self.said % self.n] == name, (self.order[self.said % self.n], name)
        self.said += 1
        return 1

    def done(self):
        assert self.said % self.n == 0, (self.said, self.n)

    def at(self, i, name, back=0):
        assert 0 <= back <= self.LEAD
        return i * self.n + (self.LEAD - back) * self.n + self.names[name] + 1


def open_tools(ctx, nc, block_name=""):
    def sb(name, shape, dt=F32):
        return ctx.enter_context(nc.sbuf_tensor(name, shape, dt))

    def ps(name, shape, dt=F32):
        return ctx.enter_context(nc.psum_tensor(name, shape, dt))

    def sem(name):
        return ctx.enter_context(semaphore(nc, name))

    return sb, ps, sem


def load_tiles(nc, name, pairs):
    with ExitStack() as ctx:
        loaded = ctx.enter_context(semaphore(nc, f"{name}_loaded"))
        block = ctx.enter_context(nc.Block())

        @block.sync
        def _(sp):
            for dst, src in pairs[0::2]:
                sp.dma_start(dst, src).then_inc(loaded, 16)
            sp.wait_ge(loaded, 16 * len(pairs))

        @block.scalar
        def _(act):
            for dst, src in pairs[1::2]:
                act.dma_start(dst, src).then_inc(loaded, 16)


def layernorm(nc, name, src, dst, C, gain=None, shift=None, loads=()):
    with ExitStack() as ctx:
        sb, ps, sem = open_tools(ctx, nc)
        sq = sb(f"{name}_sq", [P, 2, G])
        rstd = sb(f"{name}_rstd", [P, 2, G])
        cen_ps = ps(f"{name}_cen", [P, 4, G])
        var_ps = ps(f"{name}_var", [P, 2, G])
        two = (0, 1)
        four = [(a, j) for a in two for j in two]
        centered = Steps(ctx, nc, f"{name}_centered", four)
        varied = Steps(ctx, nc, f"{name}_varied", four)
        squared = Steps(ctx, nc, f"{name}_squared", four)
        logged = Steps(ctx, nc, f"{name}_logged", four)
        inverted = Steps(ctx, nc, f"{name}_inverted", four)
        copied = Steps(ctx, nc, f"{name}_copied", four)
        scaled = Steps(ctx, nc, f"{name}_scaled", four)
        loaded = sem(f"{name}_loaded")
        block = ctx.enter_context(nc.Block())

        @block.sync
        def _(sp):
            for d, s in loads:
                sp.dma_start(d, s).then_inc(loaded, 16)
            if loads:
                sp.wait_ge(loaded, 16 * len(loads))

        def at(i, a, j):
            return bass.ds(i * (4 * G) + (2 * a + j) * G, G)

        def steps(eng, head, body):
            def whole(i, nxt):
                body(i, 0, i, 1)
                body(i, 1, nxt, 0)
            head(0, 0)
            with eng.Fori(0, NG // 4 - 1) as i:
                whole(i, i + 1)
            whole(NG // 4 - 1, None)

        @block.tensor
        def _(pe):
            centered.credit(pe)
            varied.credit(pe)

            def center(i, a):
                for j in two:
                    pe.wait_ge(copied.sem, copied.at(i, (a, j), 1))
                    nc.tensor.matmul(cen_ps[:, 2 * a + j, :], C.center[:], src[:, at(i, a, j)], start=True, stop=True)\
                        .then_inc(centered.sem, centered.step((a, j)))

            def half(i, a, ni, na):
                if ni is not None:
                    center(ni, na)
                for j in two:
                    pe.wait_ge(squared.sem, squared.at(i, (a, j)))
                    pe.wait_ge(logged.sem, logged.at(i, (1 - a, j), 0 if a else 1))
                    nc.tensor.matmul(var_ps[:, j, :], C.mean[:], sq[:, j, :], start=True, stop=True)\
                        .then_inc(varied.sem, varied.step((a, j)))

            steps(pe, center, half)

        @block.scalar
        def _(act):
            for k in (squared, logged, inverted):
                k.credit(act)
            act.preload_act_table_set("natural_log_exp_and_others")

            def square(i, a):
                for j in two:
                    act.wait_ge(copied.sem, copied.at(i, (a, j)))
                    act.wait_ge(varied.sem, varied.at(i, (1 - a, j), 0 if a else 1))
                    nc.scalar.activation(sq[:, j, :], dst[:, at(i, a, j)], ACT.Square)\
                        .then_inc(squared.sem, squared.step((a, j)))

            def half(i, a, ni, na):
                for j in two:
                    act.wait_ge(varied.sem, varied.at(i, (a, j)))
                    act.wait_ge(scaled.sem, scaled.at(i, (1 - a, j), 0 if a else 1))
                    nc.scalar.activation(rstd[:, j, :], var_ps[:, j, :], ACT.Ln, bias=C.eps[:])\
                        .then_inc(logged.sem, logged.step((a, j)))
                if ni is not None:
                    square(ni, na)
                for j in two:
                    act.wait_ge(logged.sem, logged.at(i, (a, j)))
                    nc.scalar.activation(rstd[:, j, :], rstd[:, j, :], ACT.Exp, scale=-0.5)\
                        .then_inc(inverted.sem, inverted.step((a, j)))

            steps(act, square, half)

        @block.vector
        def _(dve):
            copied.credit(dve)
            scaled.credit(dve)

            def copy(i, a):
                for j in two:
                    dve.wait_ge(centered.sem, centered.at(i, (a, j)))
                    nc.vector.tensor_copy(dst[:, at(i, a, j)], cen_ps[:, 2 * a + j, :]).then_inc(copied.sem, copied.step((a, j)))

            def half(i, a, ni, na):
                if ni is not None:
                    copy(ni, na)
                for j in two:
                    dve.wait_ge(inverted.sem, inverted.at(i, (a, j)))
                    dve.wait_ge(copied.sem, copied.at(i, (a, j)))
                    nc.vector.tensor_tensor(dst[:, at(i, a, j)], dst[:, at(i, a, j)], rstd[:, j, :], ALU.mult)\
                        .then_inc(scaled.sem, scaled.step((a, j)))
                if gain is not None:
                    for j in two:
                        dve.wait_ge(scaled.sem, scaled.at(i, (a, j)))
                        nc.vector.tensor_scalar(dst[:, at(i, a, j)], dst[:, at(i, a, j)], gain, shift, ALU.mult, ALU.add)

            steps(dve, copy, half)


def residual_add(nc, name, x, y):
    with ExitStack() as ctx:
        block = ctx.enter_context(nc.Block())

        @block.vector
        def _(dve):
            nc.vector.tensor_tensor(x[:, 0:T * 5 // 8], x[:, 0:T * 5 // 8], y[:, 0:T * 5 // 8], ALU.add)

        @block.gpsimd
        def _(pool):
            nc.gpsimd.tensor_tensor(x[:, T * 5 // 8:T], x[:, T * 5 // 8:T], y[:, T * 5 // 8:T], ALU.add)


def gated_ffn(nc, name, res, src, gate_w, up_w, down_w, sizes, func, C, gate_b=None, up_b=None, down_b=None):
    with ExitStack() as ctx:
        sb, ps, sem = open_tools(ctx, nc)
        HC = len(sizes)
        hid = sb(f"{name}_hid", [P, 2, G])
        sg = sb(f"{name}_sg", [P, 2, G])
        gate_ps = ps(f"{name}_gate", [P, 2, G])
        up_ps = ps(f"{name}_up", [P, 2, G])
        out_ps = ps(f"{name}_out", [P, G])
        U = range(2 * HC)
        n = len(U)
        PE = Steps(ctx, nc, f"{name}_pe", ["gateup0", "gateup1"] + [s for u in U for s in
                   (["gateup%d" % (u + 2)] if u + 2 in U else []) + ["down%d" % u]])
        AC = Steps(ctx, nc, f"{name}_act", ["func%d" % u for u in U])
        VE = Steps(ctx, nc, f"{name}_dve", [s for u in U for s in ["hid%d" % u] + (["out%d" % u] if u % HC == HC - 1 else [])])
        block = ctx.enter_context(nc.Block())

        @block.tensor
        def _(pe):
            PE.credit(pe)

            def gate_up(i, u):
                g, c = divmod(u, HC)
                k = sizes[c]
                at = bass.ds(i * (2 * G) + g * G, G)
                pe.wait_ge(VE.sem, VE.at(i, "hid%d" % ((u - 2) % n), 0 if u >= 2 else 1))
                nc.tensor.matmul(gate_ps[:k, u % 2, :], gate_w[:, c * P:c * P + k], src[:, at], start=True, stop=True)
                nc.tensor.matmul(up_ps[:k, u % 2, :], up_w[:, c * P:c * P + k], src[:, at], start=True, stop=True)\
                    .then_inc(PE.sem, PE.step("gateup%d" % u))

            with pe.Fori(0, NG // 2) as i:
                gate_up(i, 0)
                gate_up(i, 1)
                for u in U:
                    if u + 2 in U:
                        gate_up(i, u + 2)
                    c = u % HC
                    k = sizes[c]
                    pe.wait_ge(VE.sem, VE.at(i, "hid%d" % u))
                    if c == 0:
                        pe.wait_ge(VE.sem, VE.at(i, "out%d" % ((u - 1) % n), 0 if u else 1))
                    nc.tensor.matmul(out_ps[:], down_w[:k, c, :], hid[:k, u % 2, :],
                                     start=c == 0, stop=c == HC - 1).then_inc(PE.sem, PE.step("down%d" % u))
            PE.done()

        @block.scalar
        def _(act):
            AC.credit(act)
            act.preload_act_table(func)
            with act.Fori(0, NG // 2) as i:
                for u in U:
                    k = sizes[u % HC]
                    act.wait_ge(PE.sem, PE.at(i, "gateup%d" % u))
                    act.wait_ge(VE.sem, VE.at(i, "hid%d" % ((u - 2) % n), 0 if u >= 2 else 1))
                    bias = {} if gate_b is None else {"bias": gate_b[:k, u % HC:u % HC + 1]}
                    nc.scalar.activation(sg[:k, u % 2, :], gate_ps[:k, u % 2, :], func, **bias)\
                        .then_inc(AC.sem, AC.step("func%d" % u))
            AC.done()

        @block.vector
        def _(dve):
            VE.credit(dve)
            with dve.Fori(0, NG // 2) as i:
                for u in U:
                    g, c = divmod(u, HC)
                    k = sizes[c]
                    dve.wait_ge(AC.sem, AC.at(i, "func%d" % u))
                    dve.wait_ge(PE.sem, PE.at(i, "down%d" % ((u - 2) % n), 0 if u >= 2 else 1))
                    h, up, s = hid[:k, u % 2, :], up_ps[:k, u % 2, :], sg[:k, u % 2, :]
                    if up_b is None:
                        ins = nc.vector.tensor_tensor(h, up, s, ALU.mult)
                    else:
                        ins = nc.vector.scalar_tensor_tensor(h, up, up_b[:k, c:c + 1], s, ALU.add, ALU.mult)
                    ins.then_inc(VE.sem, VE.step("hid%d" % u))
                    if c == HC - 1:
                        at = bass.ds(i * (2 * G) + g * G, G)
                        dve.wait_ge(PE.sem, PE.at(i, "down%d" % u))
                        if down_b is None:
                            ins = nc.vector.tensor_tensor(res[:, at], res[:, at], out_ps[:], ALU.add)
                        else:
                            ins = nc.vector.scalar_tensor_tensor(res[:, at], out_ps[:], down_b, res[:, at], ALU.add, ALU.add)
                        ins.then_inc(VE.sem, VE.step("out%d" % u))
            VE.done()


def int8_swiglu(nc, x, z, w, C):
    with ExitStack() as stage:
        sb, ps, sem = open_tools(stage, nc)
        HC = w["L0_ffn_w_gate"].shape[1] // P
        wi = sb("q_wi", [P, 3, HC * P], I32)
        wf = sb("q_wf", [P, 3, HC * P])
        layernorm(nc, "L0_ffn_ln", x, z, C, loads=[(wi[:, 0, :], w["L0_ffn_w_gate"]), (wi[:, 1, :], w["L0_ffn_w_up"]),
                                                   (wi[:, 2, :].rearrange("p (c n) -> p c n", c=HC),
                                                    w["L0_ffn_w_down"].rearrange("(c p) n -> p c n", p=P))])
        with ExitStack() as ctx:
            block = ctx.enter_context(nc.Block())

            @block.scalar
            def _(act):
                nc.scalar.activation(wf[:], wi[:], ACT.Copy, scale=1.0 / 127.0)

        gated_ffn(nc, "q", x, z, wf[:, 0, :], wf[:, 1, :], wf[:, 2, :].rearrange("p (c n) -> p c n", c=HC),
                  [P] * HC, ACT.Silu, C)


def selector(nc, stage, name, w, N):
    sel = stage.enter_context(nc.sbuf_tensor(f"{name}_sel", [96, 2 * N, P], BF16))
    with ExitStack() as ctx:
        wide = ctx.enter_context(nc.sbuf_tensor(f"{name}_sel32", [96, 2 * N, P], F32))
        load_tiles(nc, f"{name}_sel", [(wide[:], w[f"c_sel{2 * N}"])])
        block = ctx.enter_context(nc.Block())

        @block.vector
        def _(dve):
            nc.vector.tensor_copy(sel[:], wide[:])
    return sel


def mamba(nc, name, src, res, w, C, sel, N, norm, low_rank=False):
    H = 2
    R = 8
    NSEQ = G // SEQ
    CH = N // 2
    KN = 2 * N
    with ExitStack() as stage:
        sb, ps, sem = open_tools(stage, nc)
        in_w = sb(f"{name}_in_w", [P, 2 * H, P])
        conv_w = sb(f"{name}_conv_w", [P, H, 4])
        col = sb(f"{name}_col", [P, 3, H])
        conv_b, dt_b, skip = col[:, 0, :], col[:, 1, :], col[:, 2, :]
        xp_w = sb(f"{name}_xp_w", [P, H, 96 + R])
        dt_w = sb(f"{name}_dt_w", [R, H, P])
        a_log = sb(f"{name}_a_log", [P, H, N])
        decay = sb(f"{name}_decay", [P, H, N])
        out_w = sb(f"{name}_out_w", [P, H, P])
        skip_w = sb(f"{name}_skip_w", [P, H, P])
        u = sb(f"{name}_u", [P, H, T])
        sz = sb(f"{name}_sz", [P, H, T])
        delta = sb(f"{name}_delta", [P, H, T])
        bc = sb(f"{name}_bc", [96, T], BF16)
        pairs = [(in_w[:], w[f"{name}_in_w"]), (conv_w[:], w[f"{name}_conv_w"]), (col[:], w[f"{name}_col"]),
                 (xp_w[:], w[f"{name}_xp_w"]), (dt_w[:], w[f"{name}_dt_w"]), (a_log[:], w[f"{name}_a_log"]),
                 (out_w[:], w[f"{name}_out_w"])]
        if low_rank:
            u_t = sb(f"{name}_ut", [R, H, P])
            v_w = sb(f"{name}_v", [R, N])
            lrs = sb(f"{name}_lrs", [P, 1])
            pairs += [(u_t[:], w[f"{name}_ut"]), (v_w[:], w[f"{name}_v"]), (lrs[:], w[f"{name}_lrs"])]
        norm(pairs)

        with ExitStack() as ctx:
            sb, ps, sem = open_tools(ctx, nc)
            conv = sb(f"{name}_conv", [P, 2, G])
            prod = sb(f"{name}_prod", [P, 2, 4, G])
            in_ps = ps(f"{name}_inps", [P, 2, 2 * H, G])
            two, TAPS = (0, 1), (3, 2, 1, 0)
            PE = Steps(ctx, nc, f"{name}_a_pe", [("in", j, c) for j in two for c in (1, 0, 2, 3)])
            AC = Steps(ctx, nc, f"{name}_a_act", [("prod", 0), ("silu", 0, 2), ("silu", 0, 3), ("prod", 1), ("silu", 0, 0),
                                                  ("silu", 0, 1), ("silu", 1, 2), ("silu", 1, 3), ("silu", 1, 0), ("silu", 1, 1)])
            VE = Steps(ctx, nc, f"{name}_a_dve", [("tap", j, k) for j in two for k in range(4)])
            PO = Steps(ctx, nc, f"{name}_a_pool", [("add", j, k) for j in two for k in (1, 2, 3)])
            block = ctx.enter_context(nc.Block())

            def by_sequence(t):
                return t.rearrange("p (b t) -> p b t", b=NSEQ)

            @block.tensor
            def _(pe):
                PE.credit(pe)
                with pe.Fori(0, NG // 2) as i:
                    for j in two:
                        for c in (1, 0, 2, 3):
                            if c == 0:
                                pe.wait_ge(VE.sem, VE.at(i, ("tap", j, 3), 1))
                            elif c == 1:
                                pe.wait_ge(AC.sem, AC.at(i, ("prod", j), 1))
                            else:
                                pe.wait_ge(AC.sem, AC.at(i, ("silu", j, c), 1))
                            nc.tensor.matmul(in_ps[:, j, c, :], in_w[:, c, :], src[:, bass.ds(i * (2 * G) + j * G, G)],
                                             start=True, stop=True).then_inc(PE.sem, PE.step(("in", j, c)))
                PE.done()

            @block.vector
            def _(dve):
                VE.credit(dve)
                for h in range(H):
                    nc.vector.tensor_scalar(skip_w[:, h, :], C.ident[:], skip[:, h:h + 1], None, ALU.mult)
                with dve.Fori(0, NG // 2) as i:
                    for j in two:
                        xin, acc = by_sequence(in_ps[:, j, 0, :]), by_sequence(conv[:, j, :])
                        dve.wait_ge(PE.sem, PE.at(i, ("in", j, 0)))
                        dve.wait_ge(AC.sem, AC.at(i, ("silu", j, 0), 1))
                        nc.vector.tensor_scalar(acc, xin, conv_w[:, 0, 3:4], None, ALU.mult)\
                            .then_inc(VE.sem, VE.step(("tap", j, 0)))
                        for k in range(1, 4):
                            dve.wait_ge(VE.sem, VE.at(i, ("tap", j, k - 1)))
                            nc.vector.scalar_tensor_tensor(acc[:, :, k:], xin[:, :, :SEQ - k], conv_w[:, 0, 3 - k:4 - k],
                                                           acc[:, :, k:], ALU.mult, ALU.add)\
                                .then_inc(VE.sem, VE.step(("tap", j, k)))
                VE.done()

            @block.gpsimd
            def _(pool):
                PO.credit(pool)
                with pool.Fori(0, NG // 2) as i:
                    for j in two:
                        pool.wait_ge(AC.sem, AC.at(i, ("prod", j)))
                        acc = by_sequence(prod[:, j, 0, :])
                        for k in range(1, 4):
                            if k > 1:
                                pool.wait_ge(PO.sem, PO.at(i, ("add", j, k - 1)))
                            nc.gpsimd.tensor_tensor(acc[:, :, k:], acc[:, :, k:], by_sequence(prod[:, j, k, :])[:, :, :SEQ - k],
                                                    ALU.add).then_inc(PO.sem, PO.step(("add", j, k)))
                PO.done()

            @block.scalar
            def _(act):
                AC.credit(act)
                act.preload_act_table(ACT.Silu)

                def products(i, j):
                    act.wait_ge(PE.sem, PE.at(i, ("in", j, 1)))
                    act.wait_ge(AC.sem, AC.at(i, ("silu", j, 1), 1))
                    for k in range(4):
                        a = nc.scalar.activation(prod[:, j, k, :], in_ps[:, j, 1, :], ACT.Copy, scale=conv_w[:, 1, 3 - k:4 - k])
                    a.then_inc(AC.sem, AC.step(("prod", j)))

                def silu_z(i, j):
                    for c in (2, 3):
                        act.wait_ge(PE.sem, PE.at(i, ("in", j, c)))
                        nc.scalar.activation(sz[:, c - H, bass.ds(i * (2 * G) + j * G, G)], in_ps[:, j, c, :], ACT.Silu)\
                            .then_inc(AC.sem, AC.step(("silu", j, c)))

                def silu_u(i, j):
                    for h in range(H):
                        if h == 0:
                            act.wait_ge(VE.sem, VE.at(i, ("tap", j, 3)))
                        else:
                            act.wait_ge(PO.sem, PO.at(i, ("add", j, 3)))
                        nc.scalar.activation(u[:, h, bass.ds(i * (2 * G) + j * G, G)], prod[:, j, 0, :] if h else conv[:, j, :],
                                             ACT.Silu, bias=conv_b[:, h:h + 1]).then_inc(AC.sem, AC.step(("silu", j, h)))

                with act.Fori(0, NG // 2) as i:
                    products(i, 0)
                    silu_z(i, 0)
                    products(i, 1)
                    silu_u(i, 0)
                    silu_z(i, 1)
                    silu_u(i, 1)
                AC.done()

        with ExitStack() as ctx:
            sb, ps, sem = open_tools(ctx, nc)
            dt_low = sb(f"{name}_dt_low", [R, 2, G])
            mag = sb(f"{name}_mag", [P, 2, H, G])
            pos = sb(f"{name}_pos", [P, 2, H, G])
            rest = sb(f"{name}_rest", [96, 2, G])
            mid = sb(f"{name}_mid", [96, 2, G], BF16)
            x_ps = ps(f"{name}_xps", [96 + R, 2, G])
            dt_ps = ps(f"{name}_dtps", [P, 2, H, G])
            two = (0, 1)
            PE = Steps(ctx, nc, f"{name}_b_pe", [("x", j) for j in two] + [("dt", j, h) for j in two for h in range(H)])
            AC = Steps(ctx, nc, f"{name}_b_act", [("high", j) for j in two]
                       + [s for j in two for s in [("abs", j, 0), ("abs", j, 1), ("exp", j)]] + [("ln", j) for j in two])
            VE = Steps(ctx, nc, f"{name}_b_dve", [(s, j) for j in two for s in ("low", "rest", "mid", "mid_bc")]
                       + [("pos", j, h) for j in two for h in range(H)])
            PO = Steps(ctx, nc, f"{name}_b_pool", [("last", j) for j in two] + [("delta", j) for j in two])
            rank_done = sem(f"{name}_rank")
            rates = sem(f"{name}_rates")
            block = ctx.enter_context(nc.Block())

            @block.tensor
            def _(pe):
                PE.credit(pe)
                if low_rank:
                    for h in range(H):
                        mm = nc.tensor.matmul(dt_ps[:, 0, h, 0:N], u_t[:, h, :], v_w[:], start=True, stop=True)
                    mm.then_inc(rank_done, 1)
                    pe.wait_ge(rates, 2)
                with pe.Fori(0, NG // 2) as i:
                    for j in two:
                        pe.wait_ge(VE.sem, VE.at(i, ("rest", j), 1))
                        for h in range(H):
                            mm = nc.tensor.matmul(x_ps[:, j, :], xp_w[:, h, :], u[:, h, bass.ds(i * (2 * G) + j * G, G)],
                                                  start=h == 0, stop=h == H - 1)
                        mm.then_inc(PE.sem, PE.step(("x", j)))
                    for j in two:
                        pe.wait_ge(VE.sem, VE.at(i, ("low", j)))
                        for h in range(H):
                            pe.wait_ge(VE.sem, VE.at(i, ("pos", j, h), 1))
                            nc.tensor.matmul(dt_ps[:, j, h, :], dt_w[:, h, :], dt_low[:, j, :], start=True, stop=True)\
                                .then_inc(PE.sem, PE.step(("dt", j, h)))
                PE.done()

            @block.scalar
            def _(act):
                AC.credit(act)
                act.preload_act_table_set("natural_log_exp_and_others")
                nc.scalar.activation(decay[:], a_log[:], ACT.Exp).then_inc(rates, 1)
                with act.Fori(0, NG // 2) as i:
                    for j in two:
                        act.wait_ge(PE.sem, PE.at(i, ("x", j)))
                        nc.scalar.activation(bc[:, bass.ds(i * (2 * G) + j * G, G)], x_ps[0:96, j, :], ACT.Copy)\
                            .then_inc(AC.sem, AC.step(("high", j)))
                    for j in two:
                        act.wait_ge(PO.sem, PO.at(i, ("delta", j), 1))
                        for h in range(H):
                            act.wait_ge(PE.sem, PE.at(i, ("dt", j, h)))
                            nc.scalar.activation(mag[:, j, h, :], dt_ps[:, j, h, :], ACT.Abs, bias=dt_b[:, h:h + 1])\
                                .then_inc(AC.sem, AC.step(("abs", j, h)))
                        act.wait_ge(AC.sem, AC.at(i, ("abs", j, 1)))
                        nc.scalar.activation(mag[:, j], mag[:, j], ACT.Exp, scale=-1.0).then_inc(AC.sem, AC.step(("exp", j)))
                    for j in two:
                        act.wait_ge(AC.sem, AC.at(i, ("exp", j)))
                        nc.scalar.activation(mag[:, j], mag[:, j], ACT.Ln, bias=C.one[:]).then_inc(AC.sem, AC.step(("ln", j)))
                AC.done()

            @block.vector
            def _(dve):
                VE.credit(dve)
                dve.wait_ge(rates, 1)
                if low_rank:
                    dve.wait_ge(rank_done, 1)
                    nc.vector.tensor_scalar(a_log[:], dt_ps[:, 0, :, 0:N], lrs[:], float(R) ** -0.5, ALU.mult, ALU.mult)\
                        .then_inc(rates, 1)
                    dve.wait_ge(rates, 2)
                    nc.vector.tensor_tensor(decay[:], a_log[:], decay[:], ALU.subtract)
                else:
                    nc.vector.tensor_scalar(decay[:], decay[:], -1.0, None, ALU.mult)
                with dve.Fori(0, NG // 2) as i:
                    for j in two:
                        dve.wait_ge(AC.sem, AC.at(i, ("high", j)))
                        dve.wait_ge(PE.sem, PE.at(i, ("dt", j, 1), 1))
                        nc.vector.tensor_copy(dt_low[:, j, :], x_ps[96:96 + R, j, :]).then_inc(VE.sem, VE.step(("low", j)))
                        dve.wait_ge(PO.sem, PO.at(i, ("last", j), 1))
                        nc.vector.tensor_tensor(rest[:, j, :], x_ps[0:96, j, :], bc[:, bass.ds(i * (2 * G) + j * G, G)],
                                                ALU.subtract).then_inc(VE.sem, VE.step(("rest", j)))
                        dve.wait_ge(VE.sem, VE.at(i, ("rest", j)))
                        nc.vector.tensor_copy(mid[:, j, :], rest[:, j, :]).then_inc(VE.sem, VE.step(("mid", j)))
                        dve.wait_ge(VE.sem, VE.at(i, ("mid", j)))
                        nc.vector.tensor_copy(bc[32:64, bass.ds(i * (2 * G) + j * G, G)], mid[32:64, j, :])\
                            .then_inc(VE.sem, VE.step(("mid_bc", j)))
                    for j in two:
                        dve.wait_ge(PO.sem, PO.at(i, ("delta", j), 1))
                        for h in range(H):
                            dve.wait_ge(AC.sem, AC.at(i, ("abs", j, h)))
                            nc.vector.tensor_scalar(pos[:, j, h, :], dt_ps[:, j, h, :], dt_b[:, h:h + 1], 0.0, ALU.add, ALU.max)\
                                .then_inc(VE.sem, VE.step(("pos", j, h)))
                VE.done()

            @block.gpsimd
            def _(pool):
                PO.credit(pool)
                with pool.Fori(0, NG // 2) as i:
                    for j in two:
                        at = bass.ds(i * (2 * G) + j * G, G)
                        pool.wait_ge(VE.sem, VE.at(i, ("mid", j)))
                        pool.wait_ge(PO.sem, PO.at(i, ("last", 0)) if j else PO.at(i, ("delta", 1), 1))
                        nc.gpsimd.tensor_tensor(bc[64:96, at], rest[64:96, j, :], mid[64:96, j, :], ALU.subtract)\
                            .then_inc(PO.sem, PO.step(("last", j)))
                    for j in two:
                        if j == 0:
                            pool.wait_ge(PO.sem, PO.at(i, ("last", 1)))
                        pool.wait_ge(VE.sem, VE.at(i, ("pos", j, 1)))
                        pool.wait_ge(AC.sem, AC.at(i, ("ln", j)))
                        nc.gpsimd.tensor_tensor(delta[:, :, bass.ds(i * (2 * G) + j * G, G)], pos[:, j], mag[:, j], ALU.add)\
                            .then_inc(PO.sem, PO.step(("delta", j)))
                PO.done()

        with ExitStack() as ctx:
            sb, ps, sem = open_tools(ctx, nc)
            dA = sb(f"{name}_dA", [P, 2, H, 2, G])
            inp = sb(f"{name}_inp", [P, H, 2, G])
            hs = sb(f"{name}_hs", [P, 2, H, 2, G])
            cb = sb(f"{name}_cb", [P, 2, 2, G])
            du = sb(f"{name}_du", [P, H, G])
            y = delta
            b_ps = ps(f"{name}_bps", [P, 2, G])
            c_ps = ps(f"{name}_cps", [P, 2, G])
            y_ps = ps(f"{name}_yps", [P, H, G])
            o_ps = ps(f"{name}_ops", [P, G])
            CS, HS = range(CH), range(H)
            half_steps = [(c, h) for c in CS for h in HS]
            bcasts = Steps(ctx, nc, f"{name}_bcasts", CS)
            sums = Steps(ctx, nc, f"{name}_sums", half_steps)
            outs = Steps(ctx, nc, f"{name}_outs", ["out"])
            decays = Steps(ctx, nc, f"{name}_decays", half_steps)
            c_copied = Steps(ctx, nc, f"{name}_c_copied", CS)
            inputs = Steps(ctx, nc, f"{name}_inputs", half_steps)
            scans = Steps(ctx, nc, f"{name}_scans", half_steps)
            gates = Steps(ctx, nc, f"{name}_gates", HS)
            added = Steps(ctx, nc, f"{name}_added", ["res"])
            dus = Steps(ctx, nc, f"{name}_dus", HS)
            weighed = Steps(ctx, nc, f"{name}_weighed", half_steps)
            zeros = sem(f"{name}_zeros")
            decays_begun = sem(f"{name}_decays_begun")
            block = ctx.enter_context(nc.Block())

            def groups(eng, head, body):
                head(0)
                with eng.Fori(0, NG - 1) as i:
                    body(i, i + 1)
                body(NG - 1, None)

            @block.gpsimd
            def _(pool):
                dus.credit(pool)
                weighed.credit(pool)
                nc.gpsimd.memset(dA[:].rearrange("p a h s (b t) -> p (a h s b) t", b=NSEQ)[:, :, 0:1], 0.0).then_inc(zeros, 1)

                def multiply_du(i):
                    at = bass.ds(i * G, G)
                    for h in HS:
                        pool.wait_ge(inputs.sem, inputs.at(i, (CH - 1, h), 1))
                        nc.gpsimd.tensor_tensor(du[:, h, :], delta[:, h, at], u[:, h, at], ALU.mult)\
                            .then_inc(dus.sem, dus.step(h))

                def group(i, nxt):
                    for c in CS:
                        if c == CH - 1 and nxt is not None:
                            multiply_du(nxt)
                        pool.wait_ge(c_copied.sem, c_copied.at(i, c))
                        for h in HS:
                            pool.wait_ge(scans.sem, scans.at(i, (c, h)))
                            nc.gpsimd.tensor_tensor(hs[:, c % 2, h], hs[:, c % 2, h], cb[:, c % 2], ALU.mult)\
                                .then_inc(weighed.sem, weighed.step((c, h)))

                groups(pool, multiply_du, group)

            @block.tensor
            def _(pe):
                for k in (bcasts, sums, outs):
                    k.credit(pe)

                def bcast(i, c):
                    at = bass.ds(i * G, G)
                    back = 0 if c else 1
                    for s in range(2):
                        n = 2 * c + s
                        if s == 0:
                            pe.wait_ge(inputs.sem, inputs.at(i, ((c - 1) % CH, 1), back))
                        nc.tensor.matmul(b_ps[:, s, :], sel[:, n, :], bc[:, at], start=True, stop=True)
                        if s == 0:
                            pe.wait_ge(c_copied.sem, c_copied.at(i, (c - 1) % CH, back))
                        mm = nc.tensor.matmul(c_ps[:, s, :], sel[:, N + n, :], bc[:, at], start=True, stop=True)
                    mm.then_inc(bcasts.sem, bcasts.step(c))

                def add_up(i, c):
                    for h in HS:
                        if c == 0:
                            pe.wait_ge(gates.sem, gates.at(i, h, 1))
                            nc.tensor.matmul(y_ps[:, h, :], skip_w[:, h, :], u[:, h, bass.ds(i * G, G)],
                                             start=True, stop=False)
                        pe.wait_ge(weighed.sem, weighed.at(i, (c, h)))
                        for s in range(2):
                            mm = nc.tensor.matmul(y_ps[:, h, :], C.ident[:], hs[:, c % 2, h, s, :],
                                                  start=False, stop=c == CH - 1 and s == 1)
                        mm.then_inc(sums.sem, sums.step((c, h)))

                def head(i):
                    bcast(i, 0)
                    bcast(i, 1)
                    bcast(i, 2)
                    add_up(i, 0)

                def group(i, nxt):
                    for c in range(2, CH - 1):
                        bcast(i, c + 1)
                        add_up(i, c - 1)
                    if nxt is not None:
                        bcast(nxt, 0)
                    add_up(i, CH - 2)
                    if nxt is not None:
                        bcast(nxt, 1)
                    add_up(i, CH - 1)
                    if nxt is not None:
                        bcast(nxt, 2)
                    pe.wait_ge(added.sem, added.at(i, "res", 1))
                    for h in HS:
                        pe.wait_ge(gates.sem, gates.at(i, h))
                        mm = nc.tensor.matmul(o_ps[:], out_w[:, h, :], y[:, h, bass.ds(i * G, G)],
                                              start=h == 0, stop=h == H - 1)
                    mm.then_inc(outs.sem, outs.step("out"))
                    if nxt is not None:
                        add_up(nxt, 0)

                groups(pe, head, group)

            @block.scalar
            def _(act):
                decays.credit(act)
                c_copied.credit(act)
                act.wait_ge(zeros, 1)
                act.preload_act_table_set("natural_log_exp_and_others")
                with act.Fori(0, NG) as i:
                    for c in CS:
                        back = 0 if c >= 2 else 1
                        for h in HS:
                            act.wait_ge(scans.sem, scans.at(i, ((c - 2) % CH, h), back))
                            act.sem_inc(decays_begun, 1)
                            for s in range(2):
                                dl = delta[:, h, bass.ds(i * G, G)].rearrange("p (b t) -> p b t", b=NSEQ)[:, :, 1:]
                                o = dA[:, c % 2, h, s, :].rearrange("p (b t) -> p b t", b=NSEQ)[:, :, 1:]
                                a = nc.scalar.activation(o, dl, ACT.Exp, scale=decay[:, h, 2 * c + s:2 * c + s + 1])
                            a.then_inc(decays.sem, decays.step((c, h)))
                        act.wait_ge(bcasts.sem, bcasts.at(i, c))
                        act.wait_ge(weighed.sem, weighed.at(i, ((c - 2) % CH, 1), back))
                        nc.scalar.activation(cb[:, c % 2], c_ps[:], ACT.Copy).then_inc(c_copied.sem, c_copied.step(c))

            @block.vector
            def _(dve):
                for k in (inputs, scans, gates, added):
                    k.credit(dve)

                def feed(i, c):
                    dve.wait_ge(bcasts.sem, bcasts.at(i, c))
                    for h in HS:
                        if c == 0:
                            dve.wait_ge(dus.sem, dus.at(i, h))
                        dve.wait_ge(scans.sem, scans.at(i, ((c - 1) % CH, h), 0 if c else 1))
                        nc.vector.tensor_tensor(inp[:, h], b_ps[:], du[:, h:h + 1, :].to_broadcast([P, 2, G]), ALU.mult)\
                            .then_inc(inputs.sem, inputs.step((c, h)))

                def scan(i, c):
                    for h in HS:
                        dve.wait_ge(inputs.sem, inputs.at(i, (c, h)))
                        dve.wait_ge(decays.sem, decays.at(i, (c, h)))
                        dve.wait_ge(sums.sem, sums.at(i, ((c - 2) % CH, h), 0 if c >= 2 else 1))
                        nc.vector.tensor_tensor_scan(hs[:, c % 2, h].rearrange("p s t -> p (s t)"),
                                                     dA[:, c % 2, h].rearrange("p s t -> p (s t)"),
                                                     inp[:, h].rearrange("p s t -> p (s t)"), 0.0, ALU.mult, ALU.add)\
                            .then_inc(scans.sem, scans.step((c, h)))

                def head(i):
                    feed(i, 0)
                    scan(i, 0)
                    feed(i, 1)

                def first_head(i):
                    head(i)
                    scan(i, 1)

                def group(i, nxt):
                    for c in range(2, CH):
                        feed(i, c)
                        scan(i, c)
                    if nxt is not None:
                        head(nxt)
                    at = bass.ds(i * G, G)
                    dve.wait_ge(outs.sem, outs.at(i, "out", 1))
                    for h in HS:
                        dve.wait_ge(sums.sem, sums.at(i, (CH - 1, h)))
                        nc.vector.tensor_tensor(y[:, h, at], y_ps[:, h, :], sz[:, h, at], ALU.mult)\
                            .then_inc(gates.sem, gates.step(h))
                    if nxt is not None:
                        scan(nxt, 1)
                    dve.wait_ge(outs.sem, outs.at(i, "out"))
                    nc.vector.tensor_tensor(res[:, at], res[:, at], o_ps[:], ALU.add).then_inc(added.sem, added.step("res"))

                groups(dve, first_head, group)


def mamba_layer(nc, x, z, w, C):
    with ExitStack() as stage:
        mamba(nc, "m2", z, x, w, C, selector(nc, stage, "m2", w, 8), 8,
              lambda loads: layernorm(nc, "L2_attn_ln", x, z, C, loads=loads), low_rank=True)


def mamba_stack(nc, x, z, w, C):
    with ExitStack() as stage:
        sb, ps, sem = open_tools(stage, nc)
        ln = sb("m3_ln", [P, 2, 4])
        load_tiles(nc, "m3", [(ln[:], w["m3_ln"])])
        sel = selector(nc, stage, "m3", w, 16)

        def norm(l):
            if l == 0:
                return lambda loads: layernorm(nc, "L3_attn_ln", x, z, C, loads=loads)
            return lambda loads: layernorm(nc, f"m3{l - 1}_post", z, z, C, ln[:, 0, l - 1:l], ln[:, 1, l - 1:l], loads=loads)

        for l in range(4):
            mamba(nc, f"m3{l}", z, z, w, C, sel, 16, norm(l))
        norm(4)(())
        residual_add(nc, "m3", x, z)


def mamba_layout(a, w):
    def halves(v):
        return v.reshape(2, P, -1).transpose(1, 0, 2)

    def one(name, in_w, conv_w, conv_b, xp, dtw, dtb, alog, D, ow):
        w[f"{name}_in_w"] = in_w.reshape(P, 4, P)
        w[f"{name}_conv_w"] = halves(conv_w)
        w[f"{name}_col"] = np.stack([conv_b.reshape(2, P).T, dtb.reshape(2, P).T, D.reshape(2, P).T], 1)
        bc = np.concatenate([xp[:, 8:], np.zeros((256, 32 - (xp.shape[1] - 8)), np.float32)], 1)
        w[f"{name}_xp_w"] = halves(np.concatenate([bc, bc, bc, xp[:, :8]], 1))
        w[f"{name}_dt_w"] = dtw.reshape(8, 2, P)
        w[f"{name}_a_log"] = halves(alog)
        w[f"{name}_out_w"] = halves(ow)

    q = lambda k: a["L2_attn_" + k]
    one("m2", q("in_proj_w").T, q("conv_w"), q("conv_b"), q("x_proj_w").T, q("dt_proj_w").T, q("dt_proj_b"),
        q("A_log"), q("D"), q("out_proj_w").T)
    w["m2_ut"] = q("U_param").T.reshape(8, 2, P)
    w["m2_v"] = q("V_param")
    w["m2_lrs"] = np.broadcast_to(q("low_rank_scale").reshape(1, 1), (P, 1))
    q = lambda k: a["L3_attn_" + k]
    for l in range(4):
        one(f"m3{l}", *[q(k)[l] for k in ("in_proj_w", "conv_w", "conv_b", "x_proj_w", "dt_proj_w", "dt_proj_b",
                                          "A_log", "D", "out_proj_w")])
    w["m3_ln"] = np.stack([q("ln_w").T, q("ln_b").T], 1)


def selector_tables():
    return {f"c_sel{k}": np.repeat(np.tile(np.eye(32, k, dtype=np.float32), (3, 1))[:, :, None], P, 2)
            for k in (16, 32)}


def mx_linear(nc, x, z, w, C):
    BLK, TOP = 32, 7.5
    MAGIC = 1.5 * 2 ** 23
    NB = G // BLK
    two = (0, 1)
    QUANT = ["amax", "scale", "rscale", "ratio", "square", "ge2", "ge4", "step",
             "shifted", "rounded", "excess", "tie", "lower", "fixed", "value"]
    with ExitStack() as ctx:
        sb, ps, sem = open_tools(ctx, nc)
        wq = sb("mx_wq", [P, 1, P])
        w_t = sb("mx_wt", [P, P])
        bias = sb("mx_bias", [P, 1])
        zs = sb("mx_zs", [P, 2, G])
        xd_t = sb("mx_xdt", [P, 2, G])
        res = sb("mx_res", [P, 2, G])
        amax, scale, rscale = (sb(f"mx_{n}", [P, 2, NB]) for n in ("amax", "scale", "rscale"))
        ratio, ge2, ge4, step, val, exc = (sb(f"mx_{n}", [P, 2, G]) for n in
                                           ("ratio", "ge2", "ge4", "step", "val", "exc"))
        layernorm(nc, "L1_ffn_ln", x, z, C, loads=[(wq[:, 0, :], w["L1_ffn_weight"]), (bias[:], w["mx_bias"])])
        t_ps = ps("mx_tps", [P, 2, G])
        f_ps = ps("mx_fps", [P, 2, G])
        o_ps = ps("mx_ops", [P, 2, G])
        w_ps = ps("mx_wps", [P, P])
        PE = Steps(ctx, nc, "mx_pe", [(s, j) for s in ("back", "out") for j in two])
        turns = Steps(ctx, nc, "mx_turns", two)
        AC = Steps(ctx, nc, "mx_act", [(s, j) for s in ("xd", "bias") for j in two])
        stages = Steps(ctx, nc, "mx_stages", two)
        VE = Steps(ctx, nc, "mx_dve", [(s, j) for s in QUANT for j in two])
        PO = Steps(ctx, nc, "mx_pool", [("res", j) for j in two])
        WQ = Steps(ctx, nc, "mx_wq_steps", [(s, 0) for s in QUANT])
        w_turned = sem("mx_w_turned")
        w_ready = sem("mx_w_ready")
        block = ctx.enter_context(nc.Block())

        def quantise(dve, S, i, src, n, js):
            b = n // BLK

            def blocks(t, j):
                return t[:, j, :n].rearrange("p (b k) -> p b k", k=BLK)

            def wide(t, j):
                return t[:, j, :b].rearrange("p (b k) -> p b k", k=1).to_broadcast([P, b, BLK])

            def each(name, after, make):
                for j in js:
                    if after is not None:
                        dve.wait_ge(S.sem, S.at(i, (after, j)))
                    make(j).then_inc(S.sem, S.step((name, j)))

            def first(j):
                if S is VE:
                    dve.wait_ge(turns.sem, turns.at(i, j))
                return v.tensor_reduce(amax[:, j, :b], blocks(src, j), X, ALU.max, apply_absolute_value=True)

            def square(j):
                if S is VE:
                    dve.wait_ge(PE.sem, PE.at(i, ("back", j), 1))
                return v.tensor_tensor(exc[:, j, :n], ratio[:, j, :n], ratio[:, j, :n], ALU.mult)

            v = nc.vector
            each("amax", None, first)
            each("scale", "amax", lambda j: v.tensor_scalar(scale[:, j, :b], amax[:, j, :b], 1.0 / TOP, 1e-30, ALU.mult, ALU.max))
            each("rscale", "scale", lambda j: v.reciprocal(rscale[:, j, :b], scale[:, j, :b]))
            each("ratio", "rscale", lambda j: v.tensor_tensor(blocks(ratio, j), blocks(src, j), wide(rscale, j), ALU.mult))
            each("square", "ratio", square)
            each("ge2", "square", lambda j: v.tensor_scalar(ge2[:, j, :n], exc[:, j, :n], 4.0, 0.125, ALU.is_ge, ALU.mult))
            each("ge4", None, lambda j: v.tensor_scalar(ge4[:, j, :n], exc[:, j, :n], 16.0, 0.25, ALU.is_ge, ALU.mult))
            each("step", "ge4", lambda j: v.scalar_tensor_tensor(step[:, j, :n], ge2[:, j, :n], 0.125, ge4[:, j, :n],
                                                                 ALU.add, ALU.add))
            each("shifted", "step", lambda j: v.scalar_tensor_tensor(val[:, j, :n], step[:, j, :n], MAGIC, ratio[:, j, :n],
                                                                     ALU.mult, ALU.add))
            each("rounded", "shifted", lambda j: v.scalar_tensor_tensor(val[:, j, :n], step[:, j, :n], -MAGIC, val[:, j, :n],
                                                                        ALU.mult, ALU.add))
            each("excess", "rounded", lambda j: v.tensor_tensor(exc[:, j, :n], val[:, j, :n], ratio[:, j, :n], ALU.subtract))
            each("tie", "excess", lambda j: v.scalar_tensor_tensor(exc[:, j, :n], exc[:, j, :n], 2.0, step[:, j, :n],
                                                                   ALU.mult, ALU.is_ge))
            each("lower", "tie", lambda j: v.tensor_tensor(exc[:, j, :n], exc[:, j, :n], step[:, j, :n], ALU.mult))
            each("fixed", "lower", lambda j: v.tensor_tensor(val[:, j, :n], val[:, j, :n], exc[:, j, :n], ALU.subtract))
            each("value", "fixed", lambda j: v.tensor_tensor(blocks(exc, j), blocks(val, j), wide(scale, j), ALU.mult))

        def ahead(eng, begin, finish):
            begin(0)
            with eng.Fori(0, NG // 2 - 1) as i:
                begin(i + 1)
                finish(i)
            finish(NG // 2 - 1)

        @block.tensor
        def _(pe):
            PE.credit(pe)
            pe.wait_ge(WQ.sem, WQ.at(0, ("value", 0)))
            nc.tensor.transpose(w_ps[:], exc[:, 0, :P], C.ident[:]).then_inc(w_turned, 1)
            pe.wait_ge(w_ready, 1)
            turns.credit(pe)

            def turn(i):
                for j in two:
                    pe.wait_ge(stages.sem, stages.at(i, j))
                    pe.wait_ge(VE.sem, VE.at(i, ("ratio", j), 1))
                    for t in range(G // P):
                        mm = nc.tensor.transpose(t_ps[:, j, t * P:(t + 1) * P], zs[:, j, t * P:(t + 1) * P], C.ident[:])
                    mm.then_inc(turns.sem, turns.step(j))

            def back_and_out(i):
                for j in two:
                    pe.wait_ge(VE.sem, VE.at(i, ("value", j)))
                    pe.wait_ge(AC.sem, AC.at(i, ("xd", j), 1))
                    for t in range(G // P):
                        mm = nc.tensor.transpose(f_ps[:, j, t * P:(t + 1) * P], exc[:, j, t * P:(t + 1) * P], C.ident[:])
                    mm.then_inc(PE.sem, PE.step(("back", j)))
                for j in two:
                    pe.wait_ge(AC.sem, AC.at(i, ("xd", j)))
                    pe.wait_ge(AC.sem, AC.at(i, ("bias", j), 1))
                    nc.tensor.matmul(o_ps[:, j, :], w_t[:], xd_t[:, j, :], start=True, stop=True)\
                        .then_inc(PE.sem, PE.step(("out", j)))

            ahead(pe, turn, back_and_out)

        @block.scalar
        def _(act):
            AC.credit(act)
            act.wait_ge(w_turned, 1)
            nc.scalar.activation(w_t[:], w_ps[:], ACT.Copy).then_inc(w_ready, 1)
            stages.credit(act)

            def stage(i):
                for j in two:
                    act.wait_ge(turns.sem, turns.at(i, j, 1))
                    nc.scalar.activation(zs[:, j, :], z[:, bass.ds(i * (2 * G) + j * G, G)], ACT.Copy)\
                        .then_inc(stages.sem, stages.step(j))

            def finish(i):
                for j in two:
                    act.wait_ge(PE.sem, PE.at(i, ("back", j)))
                    nc.scalar.activation(xd_t[:, j, :], f_ps[:, j, :], ACT.Copy).then_inc(AC.sem, AC.step(("xd", j)))
                for j in two:
                    act.wait_ge(PE.sem, PE.at(i, ("out", j)))
                    act.wait_ge(PO.sem, PO.at(i, ("res", j), 1))
                    nc.scalar.activation(res[:, j, :], o_ps[:, j, :], ACT.Identity, bias=bias[:])\
                        .then_inc(AC.sem, AC.step(("bias", j)))

            ahead(act, stage, finish)

        @block.vector
        def _(dve):
            VE.credit(dve)
            WQ.credit(dve)
            quantise(dve, WQ, 0, wq, P, (0,))
            WQ.done()
            dve.wait_ge(w_turned, 1)
            with dve.Fori(0, NG // 2) as i:
                quantise(dve, VE, i, t_ps, G, two)
            VE.done()

        @block.gpsimd
        def _(pool):
            PO.credit(pool)
            with pool.Fori(0, NG // 2) as i:
                for j in two:
                    at = bass.ds(i * (2 * G) + j * G, G)
                    pool.wait_ge(AC.sem, AC.at(i, ("bias", j)))
                    nc.gpsimd.tensor_tensor(x[:, at], x[:, at], res[:, j, :], ALU.add).then_inc(PO.sem, PO.step(("res", j)))
            PO.done()


def moe(nc, x, z, w, C):
    E = w["moe_router"].shape[1]
    F = w["moe_gate"].shape[2] // P
    NT = T // P
    with ExitStack() as stage:
        sb, ps, sem = open_tools(stage, nc)
        router = sb("moe_router", [P, E])
        gate_w = sb("moe_gate", [P, E, F * P])
        up_w = sb("moe_up", [P, E, F * P])
        down_w = sb("moe_down", [P, E, F, P])
        gu_b = sb("moe_gub", [P, 2, E, F])
        down_b = sb("moe_downb", [E, P])
        falling = sb("moe_falling", [P, NT, E])
        sel = selector(nc, stage, "moe", w, 8)
        parts = sb("moe_parts", [96, T], BF16)
        prob_t = sb("moe_prob_t", [E, T])
        layernorm(nc, "L2_ffn_ln", x, z, C, loads=[(router[:], w["moe_router"]), (gate_w[:], w["moe_gate"]), (up_w[:], w["moe_up"]),
                               (down_w[:], w["moe_down"]), (gu_b[:], w["moe_gub"]), (down_b[:], w["L2_ffn_down_b"]),
                               (falling[:], w["c_falling"])])
        prob = sb("moe_prob", [P, NT, E])

        with ExitStack() as ctx:
            sb, ps, sem = open_tools(ctx, nc)
            zs = sb("moe_zs", [P, 2, G])
            l_ps = ps("moe_lps", [P, 2, 512])
            PE = Steps(ctx, nc, "moe_r_pe", [("logits", j) for j in (0, 1)])
            AC = Steps(ctx, nc, "moe_r_act", [("logits", j) for j in (0, 1)])
            PO = Steps(ctx, nc, "moe_r_pool", [("stage", j) for j in (0, 1)])
            block = ctx.enter_context(nc.Block())

            @block.gpsimd
            def _(pool):
                PO.credit(pool)
                with pool.Fori(0, NG // 2) as i:
                    for j in (0, 1):
                        pool.wait_ge(PE.sem, PE.at(i, ("logits", j), 1))
                        nc.gpsimd.tensor_copy(zs[:, j, :], z[:, bass.ds(i * (2 * G) + j * G, G)])\
                            .then_inc(PO.sem, PO.step(("stage", j)))
                PO.done()

            @block.tensor
            def _(pe):
                PE.credit(pe)
                with pe.Fori(0, NG // 2) as i:
                    for j in (0, 1):
                        pe.wait_ge(PO.sem, PO.at(i, ("stage", j)))
                        pe.wait_ge(AC.sem, AC.at(i, ("logits", j), 1))
                        for t in range(G // P):
                            mm = nc.tensor.matmul(l_ps[:, j, t * E:(t + 1) * E], zs[:, j, t * P:(t + 1) * P], router[:],
                                                  start=True, stop=True)
                        mm.then_inc(PE.sem, PE.step(("logits", j)))
                PE.done()

            @block.scalar
            def _(act):
                AC.credit(act)
                with act.Fori(0, NG // 2) as i:
                    for j in (0, 1):
                        act.wait_ge(PE.sem, PE.at(i, ("logits", j)))
                        nc.scalar.activation(prob[:, bass.ds(i * (2 * G // P) + j * (G // P), G // P), :],
                                             l_ps[:, j, 0:G // P * E].rearrange("p (t e) -> p t e", e=E), ACT.Copy)\
                            .then_inc(AC.sem, AC.step(("logits", j)))
                AC.done()

        with ExitStack() as ctx:
            sb, ps, sem = open_tools(ctx, nc)
            one = sb("moe_one", [P, NT])
            left = sb("moe_left", [P, NT, E])
            rank = sb("moe_rank", [P, NT, E])
            pick = sb("moe_pick", [P, NT, E])
            mask = sb("moe_mask", [P, NT, E])
            thrice = sb("moe_thrice", [P, NT, 96])
            rest = sb("moe_rest", [96, G])
            mid = sb("moe_mid", [96, G], BF16)
            t_ps = ps("moe_tps", [96, T])
            high = sem("moe_high")
            cleared = sem("moe_cleared")
            vstep = sem("moe_vstep")
            shifted = sem("moe_shifted")
            expd = sem("moe_exp")
            routed = sem("moe_routed")
            turned = sem("moe_turned")
            block = ctx.enter_context(nc.Block())

            @block.vector
            def _(dve):
                done = [0]

                def then(ins):
                    done[0] += 1
                    ins.then_inc(vstep, 1)
                    dve.wait_ge(vstep, done[0])

                def wide(t):
                    return t[:].rearrange("p (t e) -> p t e", e=1).to_broadcast([P, NT, E])

                v = nc.vector
                then(v.tensor_reduce(one[:], prob[:], X, ALU.max))
                v.tensor_tensor(prob[:], prob[:], wide(one), ALU.subtract).then_inc(shifted, 1)
                dve.wait_ge(expd, 1)
                then(v.tensor_reduce(one[:], prob[:], X, ALU.add))
                then(v.reciprocal(one[:], one[:]))
                then(v.tensor_tensor(prob[:], prob[:], wide(one), ALU.mult))
                then(v.tensor_copy(left[:], prob[:]))
                for k in range(2):
                    then(v.tensor_reduce(one[:], left[:], X, ALU.max))
                    then(v.tensor_tensor(rank[:], left[:], wide(one), ALU.is_equal))
                    then(v.tensor_tensor(rank[:], rank[:], falling[:], ALU.mult))
                    then(v.tensor_reduce(one[:], rank[:], X, ALU.max))
                    dst = mask if k == 0 else pick
                    then(v.tensor_tensor(dst[:], falling[:], wide(one), ALU.is_equal))
                    if k == 0:
                        then(v.scalar_tensor_tensor(left[:], mask[:], -2.0, left[:], ALU.mult, ALU.add))
                then(v.tensor_tensor(mask[:], mask[:], pick[:], ALU.add))
                then(v.tensor_tensor(prob[:], prob[:], mask[:], ALU.mult))
                then(v.tensor_reduce(one[:], prob[:], X, ALU.add))
                then(v.tensor_scalar(one[:], one[:], 1e-9, None, ALU.add))
                then(v.reciprocal(one[:], one[:]))
                dve.wait_ge(cleared, 1)
                for s in range(3):
                    v.tensor_tensor(thrice[:, :, 32 * s:32 * s + E], prob[:], wide(one), ALU.mult).then_inc(routed, 1)
                for b in range(NG):
                    at = slice(b * G, (b + 1) * G)
                    dve.wait_ge(high, b + 1)
                    then(v.tensor_tensor(rest[:], t_ps[:, at], parts[:, at], ALU.subtract))
                    then(v.tensor_copy(mid[:], rest[:]))
                    then(v.tensor_copy(parts[32:64, at], mid[32:64, :]))
                    then(v.tensor_tensor(parts[64:96, at], rest[64:96, :], mid[64:96, :], ALU.subtract))

            @block.gpsimd
            def _(pool):
                nc.gpsimd.memset(thrice[:], 0.0).then_inc(cleared, 1)

            @block.scalar
            def _(act):
                act.wait_ge(shifted, 1)
                nc.scalar.activation(prob[:], prob[:], ACT.Exp).then_inc(expd, 1)
                for b in range(NG):
                    act.wait_ge(turned, b + 1)
                    nc.scalar.activation(prob_t[:, b * G:(b + 1) * G], t_ps[0:E, b * G:(b + 1) * G], ACT.Copy)
                    nc.scalar.activation(parts[:, b * G:(b + 1) * G], t_ps[:, b * G:(b + 1) * G], ACT.Copy).then_inc(high, 1)

            @block.tensor
            def _(pe):
                pe.wait_ge(routed, 3)
                for t in range(NT):
                    mm = nc.tensor.transpose(t_ps[:, t * P:(t + 1) * P], thrice[:, t, :], C.ident[:])
                    if t % (G // P) == G // P - 1:
                        mm.then_inc(turned, 1)

        with ExitStack() as ctx:
            sb, ps, sem = open_tools(ctx, nc)
            sg = sb("moe_sg", [P, 2, G])
            hid = sb("moe_hid", [P, 2, G])
            g_ps = ps("moe_gps", [P, 2, G])
            u_ps = ps("moe_ups", [P, 2, G])
            p_ps = ps("moe_pps", [P, 2, G])
            o_ps = ps("moe_ops", [P, G])
            U = range(E * F)
            n = len(U)
            PE = Steps(ctx, nc, "moe_pe", ["gateup0", "gateup1"] + [s for k in U for s in
                       (["gateup%d" % (k + 2)] if k + 2 < n else []) + ["down%d" % k]])
            AC = Steps(ctx, nc, "moe_act", ["silu%d" % k for k in U])
            VE = Steps(ctx, nc, "moe_dve", [s for k in U for s in ("hid%d" % k, "weigh%d" % k)] + ["res"])
            block = ctx.enter_context(nc.Block())

            @block.tensor
            def _(pe):
                PE.credit(pe)

                def gate_up(i, k):
                    e, f = divmod(k, F)
                    at = bass.ds(i * G, G)
                    pe.wait_ge(VE.sem, VE.at(i, "weigh%d" % ((k - 2) % n), 0 if k >= 2 else 1))
                    nc.tensor.matmul(g_ps[:, k % 2, :], gate_w[:, e, f * P:(f + 1) * P], z[:, at], start=True, stop=True)
                    if f == 0:
                        nc.tensor.matmul(p_ps[:, e % 2, :], sel[:, e, :], parts[:, at], start=True, stop=True)
                    nc.tensor.matmul(u_ps[:, k % 2, :], up_w[:, e, f * P:(f + 1) * P], z[:, at], start=True, stop=True)\
                        .then_inc(PE.sem, PE.step("gateup%d" % k))

                with pe.Fori(0, NG) as i:
                    at = bass.ds(i * G, G)
                    gate_up(i, 0)
                    gate_up(i, 1)
                    for k in U:
                        if k + 2 < n:
                            gate_up(i, k + 2)
                        pe.wait_ge(VE.sem, VE.at(i, "weigh%d" % k))
                        mm = nc.tensor.matmul(o_ps[:], down_w[:, k // F, k % F, :], hid[:, k % 2, :], start=k == 0, stop=False)
                        if k == n - 1:
                            mm = nc.tensor.matmul(o_ps[:], down_b[:], prob_t[:, at], start=False, stop=True)
                        mm.then_inc(PE.sem, PE.step("down%d" % k))
                PE.done()

            @block.scalar
            def _(act):
                AC.credit(act)
                act.preload_act_table(ACT.Silu)
                with act.Fori(0, NG) as i:
                    for k in U:
                        act.wait_ge(PE.sem, PE.at(i, "gateup%d" % k))
                        act.wait_ge(VE.sem, VE.at(i, "hid%d" % ((k - 2) % n), 0 if k >= 2 else 1))
                        nc.scalar.activation(sg[:, k % 2, :], g_ps[:, k % 2, :], ACT.Silu,
                                             bias=gu_b[:, 0, k // F, k % F:k % F + 1]).then_inc(AC.sem, AC.step("silu%d" % k))
                AC.done()

            @block.vector
            def _(dve):
                VE.credit(dve)
                with dve.Fori(0, NG) as i:
                    for k in U:
                        dve.wait_ge(AC.sem, AC.at(i, "silu%d" % k))
                        dve.wait_ge(PE.sem, PE.at(i, "down%d" % ((k - 2) % n), 0 if k >= 2 else 1))
                        nc.vector.scalar_tensor_tensor(hid[:, k % 2, :], u_ps[:, k % 2, :], gu_b[:, 1, k // F, k % F:k % F + 1],
                                                       sg[:, k % 2, :], ALU.add, ALU.mult)\
                            .then_inc(VE.sem, VE.step("hid%d" % k))
                        dve.wait_ge(VE.sem, VE.at(i, "hid%d" % k))
                        nc.vector.tensor_tensor(hid[:, k % 2, :], hid[:, k % 2, :], p_ps[:, (k // F) % 2, :], ALU.mult)\
                            .then_inc(VE.sem, VE.step("weigh%d" % k))
                    dve.wait_ge(PE.sem, PE.at(i, "down%d" % (n - 1)))
                    at = bass.ds(i * G, G)
                    nc.vector.tensor_tensor(x[:, at], x[:, at], o_ps[:], ALU.add).then_inc(VE.sem, VE.step("res"))
                VE.done()


def ffn_layout(a, w):
    w["mx_bias"] = a["L1_ffn_bias"].reshape(P, 1)
    q = lambda k: a["L2_ffn_" + k]
    w["moe_router"] = q("router_w").T
    w["moe_gate"] = q("gate_w").transpose(1, 0, 2)
    w["moe_up"] = q("up_w").transpose(1, 0, 2)
    w["moe_down"] = q("down_w").reshape(8, 2, P, P).transpose(2, 0, 1, 3)
    w["moe_gub"] = np.stack([q("gate_b").reshape(8, 2, P).transpose(2, 0, 1), q("up_b").reshape(8, 2, P).transpose(2, 0, 1)], 1)


def ffn_tables():
    return {"c_falling": np.broadcast_to(np.arange(8, 0, -1, dtype=np.float32), (P, T // P, 8))}


def attention(nc, name, src, res, w, C, heads, dh, scale, rotary, norm_of=None):
    HPC = 4
    QC = 4
    step = max(dh, 32)
    VW = heads * dh
    OC = HPC * step // P
    HALF = G
    units = [(c, qt) for c in range(heads // HPC) for qt in range(2)]
    NU = len(units)
    NB = 4
    with ExitStack() as stage:
        sb, ps, sem = open_tools(stage, nc)
        qk_w = sb(f"{name}_qkw", [P, 2, QC, P])
        v_w = sb(f"{name}_vw", [P, VW])
        o_w = sb(f"{name}_ow", [P, QC, P])
        tab = sb(f"{name}_tab", [P, 1 if rotary else heads, 3 * P])
        pairs = [(qk_w[:], w[f"{name}_qkw"]), (v_w[:], w[f"{name}_vw"]), (o_w[:], w[f"{name}_ow"]),
                 (tab[:], w["c_band" if rotary else "c_alibi"])]
        if rotary:
            rot = sb(f"{name}_rot", [P, P])
            blk = sb(f"{name}_blk", [P, P])
            trig = sb(f"{name}_trig", [P, 2, 2, SEQ])
            qk_s = sb(f"{name}_qks", [P, 2])
            undo = sb(f"{name}_undo", [P, 1])
            pairs += [(rot[:], w["c_rot"]), (blk[:], w["c_blk"]), (trig[:], w["c_trig"]), (qk_s[:], w[f"{name}_qks"]),
                      (undo[:], w["c_undo"])]
        else:
            qk_b = sb(f"{name}_qkb", [P, 2, QC, 1])
            v_b = sb(f"{name}_vb", [1, VW])
            o_b = sb(f"{name}_ob", [P, 1])
            pairs += [(qk_b[:], w[f"{name}_qkb"]), (v_b[:], w[f"{name}_vb"]), (o_b[:], w[f"{name}_ob"])]
        if norm_of is None:
            load_tiles(nc, name, pairs)
        else:
            layernorm(nc, f"{name}_norm", norm_of, src, C, loads=pairs)

        with ExitStack() as ctx:
            sb, ps, sem = open_tools(ctx, nc)
            zs = sb(f"{name}_zs", [P, SEQ])
            qk = sb(f"{name}_qk", [P, 4, HALF])
            v1 = sb(f"{name}_v1", [P, 2, heads, step])
            s_sb = sb(f"{name}_s", [P, NB, HPC * 2 * P])
            nmax = sb(f"{name}_nmax", [P, NB, HPC])
            den = sb(f"{name}_den", [P, NB, HPC])
            rden = sb(f"{name}_rden", [P, NB, HPC])
            pt = sb(f"{name}_pt", [P, 2, HPC * 2 * P])
            ot = sb(f"{name}_ot", [P, QC, SEQ])
            s_ps = [ps(f"{name}_sps0", [P, G]), ps(f"{name}_sps1", [P, 2 * G])]
            pt_ps = ps(f"{name}_ptps", [P, 2 * G])
            o_ps = ps(f"{name}_ops", [P, G])
            p_ps = [ps(f"{name}_pps{j}", [P, HALF]) for j in (0, 1)]
            if rotary:
                sq = sb(f"{name}_sq", [P, 4, HALF])
                raw = sb(f"{name}_raw", [P, 4, HALF])
                turn = sb(f"{name}_turn", [P, 4, HALF])
            H4, U = range(4), range(NU)

            def kind(what, names):
                return Steps(ctx, nc, f"{name}_{what}", names)

            proj, vproj, scores, turned, values, outs = (kind(k, r) for k, r in (
                ("proj", H4), ("vproj", [0]), ("scores", U), ("turned", U), ("values", U), ("outs", [0])))
            vcopied, expd, ocopied = kind("vcopied", [0]), kind("expd", U), kind("ocopied", U)
            qkdone, biased, maxed, inverted, ptcopied, added = (kind(k, r) for k, r in (
                ("qkdone", H4), ("biased", U), ("maxed", U), ("inverted", U), ("ptcopied", U), ("added", [0])))
            staged, normed = kind("staged", [0]), kind("normed", U)
            if rotary:
                norms, rots, squared, logs, rnorms, rawed, clipped, sined, cosed, summed = (kind(k, H4) for k in (
                    "norms", "rots", "squared", "logs", "rnorms", "rawed", "clipped", "sined", "cosed", "summed"))
            zeroed = sem(f"{name}_zeroed")
            block = ctx.enter_context(nc.Block())
            LAST = BATCH - 1

            def chunks(t):
                return t.rearrange("p (c t) -> p c t", t=SEQ)

            def sequences(eng, prepare, body):
                prepare(0)
                with eng.Fori(0, LAST) as i:
                    body(i, i + 1)
                body(LAST, None)

            @block.gpsimd
            def _(pool):
                for k in (staged, normed) + ((cosed, summed) if rotary else ()):
                    k.credit(pool)
                nc.gpsimd.memset(v1[:], 0.0).then_inc(zeroed, 1)

                def stage_z(b):
                    pool.wait_ge(vproj.sem, vproj.at(b, 0, 1))
                    nc.gpsimd.tensor_copy(zs[:], src[:, bass.ds(b * SEQ, SEQ)]).then_inc(staged.sem, staged.step(0))

                def cosine(b, k):
                    pool.wait_ge(rawed.sem, rawed.at(b, k))
                    nc.gpsimd.tensor_tensor(chunks(turn[:, k, :]), chunks(raw[:, k, :]),
                                            trig[:, k // 2, 0:1, :].to_broadcast([P, 2, SEQ]), ALU.mult)\
                        .then_inc(cosed.sem, cosed.step(k))

                def add_sine(b, k):
                    pool.wait_ge(cosed.sem, cosed.at(b, k))
                    pool.wait_ge(sined.sem, sined.at(b, k))
                    nc.gpsimd.tensor_tensor(turn[:, k, :], turn[:, k, :], raw[:, k, :], ALU.add)\
                        .then_inc(summed.sem, summed.step(k))

                def normalise(i, u):
                    c, qt = units[u]
                    nk = (qt + 1) * P
                    s = s_sb[:, u % NB, 0:HPC * nk].rearrange("p (h k) -> p h k", h=HPC)
                    pool.wait_ge(inverted.sem, inverted.at(i, u))
                    nc.gpsimd.tensor_tensor(s, s, rden[:, u % NB, :].rearrange("p (h k) -> p h k", k=1)
                                            .to_broadcast([P, HPC, nk]), ALU.mult).then_inc(normed.sem, normed.step(u))

                def prepare(b):
                    stage_z(b)
                    if rotary:
                        for k in (0, 2):
                            for f in (cosine, add_sine):
                                f(b, k)
                                f(b, k + 1)

                def body(i, b):
                    for u in U:
                        normalise(i, u)
                    if b is not None:
                        prepare(b)

                sequences(pool, prepare, body)

            @block.tensor
            def _(pe):
                for k in (proj, vproj, scores, turned, values, outs) + ((norms, rots) if rotary else ()):
                    k.credit(pe)

                def project(b, k):
                    if k < 2:
                        pe.wait_ge(vcopied.sem, vcopied.at(b, 0, 1))
                    elif rotary:
                        pe.wait_ge(sined.sem, sined.at(b, k - 2))
                    else:
                        pe.wait_ge(qkdone.sem, qkdone.at(b, k - 2))
                    for c in range(2):
                        mm = nc.tensor.matmul(p_ps[k % 2][:, c * SEQ:(c + 1) * SEQ], qk_w[:, k // 2, k % 2 * 2 + c, :],
                                              src[:, bass.ds(b * SEQ, SEQ)], start=True, stop=True)
                    mm.then_inc(proj.sem, proj.step(k))

                def norm(b, k):
                    pe.wait_ge(squared.sem, squared.at(b, k))
                    pe.wait_ge(rawed.sem, rawed.at(b, k))
                    nc.tensor.matmul(p_ps[k % 2][:], blk[:], sq[:, k, :], start=True, stop=True)\
                        .then_inc(norms.sem, norms.step(k))

                def rotate(b, k):
                    pe.wait_ge(clipped.sem, clipped.at(b, k))
                    nc.tensor.matmul(p_ps[k % 2][:], rot[:], raw[:, k, :], start=True, stop=True)\
                        .then_inc(rots.sem, rots.step(k))

                def make_v(b):
                    pe.wait_ge(staged.sem, staged.at(b, 0))
                    last = sined if rotary else qkdone
                    pe.wait_ge(last.sem, last.at(b, 3))
                    for kt in range(2):
                        mm = nc.tensor.matmul(p_ps[kt][:, 0:VW], zs[:, kt * P:(kt + 1) * P], v_w[:],
                                              start=True, stop=rotary)
                        if not rotary:
                            mm = nc.tensor.matmul(p_ps[kt][:, 0:VW], C.ones[:, 0:P], v_b[:], start=False, stop=True)
                    mm.then_inc(vproj.sem, vproj.step(0))

                def score(i, u):
                    c, qt = units[u]
                    nk = (qt + 1) * P
                    if u == 0:
                        pe.wait_ge(qkdone.sem, qkdone.at(i, 3))
                    pe.wait_ge(biased.sem, biased.at(i, (u - 2) % NU, 0 if u >= 2 else 1))
                    at = slice(c * step, c * step + dh)
                    for j in range(HPC):
                        jj, cc = divmod(j, 2)
                        mm = nc.tensor.matmul(s_ps[qt][:, j * nk:(j + 1) * nk],
                                              qk[at, jj, cc * SEQ + qt * P:cc * SEQ + (qt + 1) * P],
                                              qk[at, 2 + jj, cc * SEQ:cc * SEQ + nk], start=True, stop=True)
                    mm.then_inc(scores.sem, scores.step(u))

                def turn_unit(i, u):
                    c, qt = units[u]
                    pe.wait_ge(normed.sem, normed.at(i, u))
                    pe.wait_ge(ptcopied.sem, ptcopied.at(i, (u - 1) % NU, 0 if u else 1))
                    for k in range(HPC * (qt + 1)):
                        mm = nc.tensor.transpose(pt_ps[:, k * P:(k + 1) * P], s_sb[:, u % NB, k * P:(k + 1) * P], C.ident[:])
                    mm.then_inc(turned.sem, turned.step(u))

                def value(i, u):
                    c, qt = units[u]
                    if u == 0:
                        pe.wait_ge(vcopied.sem, vcopied.at(i, 0))
                        pe.wait_ge(added.sem, added.at(i, 0, 1))
                    else:
                        pe.wait_ge(ocopied.sem, ocopied.at(i, u - 1))
                    pe.wait_ge(ptcopied.sem, ptcopied.at(i, u))
                    for j in range(HPC):
                        row = j * step % P
                        o = o_ps[row:row + step, j * step // P * P:(j * step // P + 1) * P]
                        for kt in range(qt + 1):
                            mm = nc.tensor.matmul(o, v1[:, kt, c * HPC + j, :],
                                                  pt[:, u % 2, (j * (qt + 1) + kt) * P:(j * (qt + 1) + kt + 1) * P],
                                                  start=kt == 0, stop=kt == qt, tile_position=(0, row))
                    mm.then_inc(values.sem, values.step(u))

                def out(i):
                    pe.wait_ge(ocopied.sem, ocopied.at(i, NU - 1))
                    for f in range(QC):
                        mm = nc.tensor.matmul(o_ps[:, 0:SEQ], o_w[:, f, :], ot[:, f, :], start=f == 0, stop=f == QC - 1)
                    mm.then_inc(outs.sem, outs.step(0))

                def halves(b, k):
                    norm(b, k)
                    norm(b, k + 1)
                    rotate(b, k)
                    rotate(b, k + 1)

                def prepare(b):
                    for k in (0, 2):
                        project(b, k)
                        project(b, k + 1)
                        if rotary:
                            halves(b, k)
                    make_v(b)

                def body(i, b):
                    for u in U:
                        score(i, u)
                        if u >= 2:
                            turn_unit(i, u - 2)
                        if u >= 3:
                            value(i, u - 3)
                    if b is not None:
                        project(b, 0)
                    turn_unit(i, NU - 2)
                    if b is not None:
                        project(b, 1)
                    value(i, NU - 3)
                    if b is not None and rotary:
                        norm(b, 0)
                    turn_unit(i, NU - 1)
                    if b is not None and rotary:
                        norm(b, 1)
                    value(i, NU - 2)
                    if b is not None:
                        if rotary:
                            rotate(b, 0)
                            rotate(b, 1)
                        else:
                            project(b, 2)
                            project(b, 3)
                    value(i, NU - 1)
                    if b is not None and rotary:
                        project(b, 2)
                        project(b, 3)
                    out(i)
                    if b is not None:
                        if rotary:
                            halves(b, 2)
                        make_v(b)

                sequences(pe, prepare, body)

            @block.scalar
            def _(act):
                for k in (vcopied, expd, ocopied) + ((squared, logs, rnorms) if rotary else ()):
                    k.credit(act)
                act.preload_act_table_set("natural_log_exp_and_others")
                act.wait_ge(zeroed, 1)

                def square(b, k):
                    act.wait_ge(proj.sem, proj.at(b, k))
                    nc.scalar.activation(sq[:, k, :], p_ps[k % 2][:], ACT.Square).then_inc(squared.sem, squared.step(k))

                def rnorm(b, k):
                    act.wait_ge(clipped.sem, clipped.at(b, k))
                    nc.scalar.activation(sq[:, k, :], sq[:, k, :], ACT.Ln).then_inc(logs.sem, logs.step(k))
                    act.wait_ge(logs.sem, logs.at(b, k))
                    nc.scalar.activation(sq[:, k, :], sq[:, k, :], ACT.Exp, scale=-0.5, bias=undo[:])\
                        .then_inc(rnorms.sem, rnorms.step(k))

                def copy_v(b):
                    act.wait_ge(vproj.sem, vproj.at(b, 0))
                    for kt in range(2):
                        a = nc.scalar.activation(v1[:, kt, :, 0:dh], p_ps[kt][:, 0:VW].rearrange("p (h d) -> p h d", d=dh), ACT.Copy)
                    a.then_inc(vcopied.sem, vcopied.step(0))

                def exps(i, u):
                    c, qt = units[u]
                    nk = (qt + 1) * P
                    act.wait_ge(maxed.sem, maxed.at(i, u))
                    for j in range(HPC):
                        s = s_sb[:, u % NB, j * nk:(j + 1) * nk]
                        a = nc.scalar.activation(s, s, ACT.Exp, bias=nmax[:, u % NB, j:j + 1], accum_out=den[:, u % NB, j:j + 1])
                    a.then_inc(expd.sem, expd.step(u))

                def copy_o(i, u):
                    c, qt = units[u]
                    act.wait_ge(values.sem, values.at(i, u))
                    if u == 0:
                        act.wait_ge(outs.sem, outs.at(i, 0, 1))
                    nc.scalar.activation(ot[:, c * OC:(c + 1) * OC, qt * P:(qt + 1) * P],
                                         o_ps[:, 0:OC * P].rearrange("p (f q) -> p f q", f=OC), ACT.Copy)\
                        .then_inc(ocopied.sem, ocopied.step(u))

                def prepare(b):
                    if rotary:
                        for k in (0, 2):
                            for f in (square, rnorm):
                                f(b, k)
                                f(b, k + 1)
                    copy_v(b)

                def body(i, b):
                    for u in U:
                        exps(i, u)
                        if u >= 3:
                            copy_o(i, u - 3)
                    if b is not None and rotary:
                        square(b, 0)
                        square(b, 1)
                    copy_o(i, NU - 3)
                    if b is not None and rotary:
                        rnorm(b, 0)
                        rnorm(b, 1)
                    copy_o(i, NU - 2)
                    copy_o(i, NU - 1)
                    if b is not None:
                        if rotary:
                            for f in (square, rnorm):
                                f(b, 2)
                                f(b, 3)
                        copy_v(b)

                sequences(act, prepare, body)

            @block.vector
            def _(dve):
                for k in (qkdone, biased, maxed, inverted, ptcopied, added) + ((rawed, clipped, sined) if rotary else ()):
                    k.credit(dve)
                v = nc.vector

                def add_bias(b, k):
                    dve.wait_ge(proj.sem, proj.at(b, k))
                    v.tensor_tensor(chunks(qk[:, k, :]), chunks(p_ps[k % 2][:]),
                                    qk_b[:, k // 2, k % 2 * 2:k % 2 * 2 + 2].to_broadcast([P, 2, SEQ]), ALU.add)\
                        .then_inc(qkdone.sem, qkdone.step(k))

                def copy_raw(b, k):
                    dve.wait_ge(squared.sem, squared.at(b, k))
                    dve.wait_ge(summed.sem, summed.at(b, k, 1))
                    v.tensor_scalar(raw[:, k, :], p_ps[k % 2][:], qk_s[:, k // 2:k // 2 + 1], None, ALU.mult)\
                        .then_inc(rawed.sem, rawed.step(k))

                def clip(b, k):
                    dve.wait_ge(norms.sem, norms.at(b, k))
                    v.tensor_scalar(sq[:, k, :], p_ps[k % 2][:], 1e-24, 2.0 ** 24, ALU.max, ALU.mult)\
                        .then_inc(clipped.sem, clipped.step(k))

                def sine(b, k):
                    dve.wait_ge(rots.sem, rots.at(b, k))
                    dve.wait_ge(cosed.sem, cosed.at(b, k))
                    v.tensor_tensor(chunks(raw[:, k, :]), chunks(p_ps[k % 2][:]),
                                    trig[:, k // 2, 1:2, :].to_broadcast([P, 2, SEQ]), ALU.mult).then_inc(sined.sem, sined.step(k))

                def scale_qk(b, k):
                    dve.wait_ge(summed.sem, summed.at(b, k))
                    dve.wait_ge(rnorms.sem, rnorms.at(b, k))
                    v.tensor_tensor(qk[:, k, :], turn[:, k, :], sq[:, k, :], ALU.mult).then_inc(qkdone.sem, qkdone.step(k))

                def bias_scores(i, u):
                    c, qt = units[u]
                    nk = (qt + 1) * P
                    s = s_sb[:, u % NB, 0:HPC * nk].rearrange("p (h k) -> p h k", h=HPC)
                    t = (tab[:, 0:1] if rotary else tab[:, c * HPC:(c + 1) * HPC])[:, :, qt * P:qt * P + nk]
                    dve.wait_ge(scores.sem, scores.at(i, u))
                    dve.wait_ge(turned.sem, turned.at(i, (u - NB) % NU, 0 if u >= NB else 1))
                    v.scalar_tensor_tensor(s, s_ps[qt][:, 0:HPC * nk].rearrange("p (h k) -> p h k", h=HPC), scale,
                                           t.to_broadcast([P, HPC, nk]) if rotary else t, ALU.mult, ALU.add)\
                        .then_inc(biased.sem, biased.step(u))

                def maxima(i, u):
                    c, qt = units[u]
                    nk = (qt + 1) * P
                    dve.wait_ge(biased.sem, biased.at(i, u))
                    v.tensor_reduce(nmax[:, u % NB, :], s_sb[:, u % NB, 0:HPC * nk].rearrange("p (h k) -> p h k", h=HPC),
                                    X, ALU.max, negate=True).then_inc(maxed.sem, maxed.step(u))

                def invert(i, u):
                    dve.wait_ge(expd.sem, expd.at(i, u))
                    v.reciprocal(rden[:, u % NB, :], den[:, u % NB, :]).then_inc(inverted.sem, inverted.step(u))

                def copy_pt(i, u):
                    c, qt = units[u]
                    n = HPC * (qt + 1) * P
                    dve.wait_ge(turned.sem, turned.at(i, u))
                    dve.wait_ge(values.sem, values.at(i, (u - 2) % NU, 0 if u >= 2 else 1))
                    v.tensor_copy(pt[:, u % 2, 0:n], pt_ps[:, 0:n]).then_inc(ptcopied.sem, ptcopied.step(u))

                def add_out(i):
                    at = bass.ds(i * SEQ, SEQ)
                    dve.wait_ge(outs.sem, outs.at(i, 0))
                    if rotary:
                        ins = v.tensor_tensor(res[:, at], res[:, at], o_ps[:, 0:SEQ], ALU.add)
                    else:
                        ins = v.scalar_tensor_tensor(res[:, at], o_ps[:, 0:SEQ], o_b[:], res[:, at], ALU.add, ALU.add)
                    ins.then_inc(added.sem, added.step(0))

                def prepare(b):
                    for k in (0, 2):
                        for f in ((copy_raw, clip, sine, scale_qk) if rotary else (add_bias,)):
                            f(b, k)
                            f(b, k + 1)

                def body(i, b):
                    for u in U:
                        bias_scores(i, u)
                        if u:
                            invert(i, u - 1)
                        maxima(i, u)
                        if u >= 2:
                            copy_pt(i, u - 2)
                    invert(i, NU - 1)
                    if b is None:
                        copy_pt(i, NU - 2)
                        copy_pt(i, NU - 1)
                    elif rotary:
                        copy_raw(b, 0)
                        copy_pt(i, NU - 2)
                        copy_raw(b, 1)
                        clip(b, 0)
                        copy_pt(i, NU - 1)
                        clip(b, 1)
                        for f in (sine, scale_qk):
                            f(b, 0)
                            f(b, 1)
                        copy_raw(b, 2)
                        copy_raw(b, 3)
                    else:
                        add_bias(b, 0)
                        copy_pt(i, NU - 2)
                        add_bias(b, 1)
                        copy_pt(i, NU - 1)
                        add_bias(b, 2)
                        add_bias(b, 3)
                    add_out(i)
                    if b is not None and rotary:
                        for f in (clip, sine, scale_qk):
                            f(b, 2)
                            f(b, 3)

                sequences(dve, prepare, body)


def alibi_attention(nc, x, z, w, C):
    attention(nc, "a1", z, x, w, C, 16, 8, 8 ** -0.5, False, norm_of=x)


def shift_tokens(nc, name, src, dst):
    with ExitStack() as ctx:
        block = ctx.enter_context(nc.Block())
        seqs = lambda t, lo: t[lo:lo + 64, :].rearrange("p (b t) -> p b t", b=BATCH)

        @block.scalar
        def _(act):
            nc.scalar.activation(dst[0:64, :], src[0:64, :], ACT.Copy)

        @block.vector
        def _(dve):
            nc.vector.tensor_copy(seqs(dst, 64)[:, :, 1:], seqs(src, 64)[:, :, :SEQ - 1])

        @block.gpsimd
        def _(pool):
            nc.gpsimd.memset(seqs(dst, 64)[:, :, 0:1], 0.0)


def local_transformer(nc, x, z, w, C):
    HID = w["l3_w1"].shape[2] // 2
    sizes = [min(P, HID - c) for c in range(0, HID, P)]
    HC = len(sizes)
    with ExitStack() as stage:
        sb, ps, sem = open_tools(stage, nc)
        h = sb("l3_h", [P, T])
        layernorm(nc, "L3_ffn_ln", x, z, C)
        for l in range(2):
            shift_tokens(nc, f"l3{l}a", z, h)
            attention(nc, f"l3{l}", h, z, w, C, 8, 64, 1.0, True)
            shift_tokens(nc, f"l3{l}f", z, h)
            with ExitStack() as ctx:
                sb, ps, sem = open_tools(ctx, nc)
                w1 = sb(f"l3{l}_w1", [P, 2 * HID])
                w2 = sb(f"l3{l}_w2", [P, HC, P])
                b1 = sb(f"l3{l}_b1", [P, 2, HC])
                col = sb(f"l3{l}_col", [P, 3])
                pairs = [(w1[:], w["l3_w1"][l])]
                for c, k in enumerate(sizes):
                    pairs.append((w2[:k, c, :], w["l3_w2"][l, c * P:c * P + k, :]))
                    for a in range(2):
                        pairs.append((b1[:k, a, c:c + 1], w["l3_b1"][l, a * HID + c * P:a * HID + c * P + k, :]))
                load_tiles(nc, f"l3{l}_col", [(col[:], w["l3_col"][l])])
                layernorm(nc, f"l3{l}_ln", h, h, C, col[:, 0:1], col[:, 1:2], loads=pairs)
                gated_ffn(nc, f"l3{l}_ff", z, h, w1[:, HID:], w1[:, :HID], w2, sizes, ACT.Gelu, C,
                          b1[:, 1, :], b1[:, 0, :], col[:, 2:3])
        residual_add(nc, "l3", x, z)


def attn_layout(a, w):
    q = lambda k: a["L1_attn_" + k]
    win, bin_ = q("w_in"), q("b_in").reshape(1, 384)

    def spread(m):
        r = m.shape[0]
        t = np.zeros((r, 4, 4, 32), m.dtype)
        t[:, :, :, :8] = m.reshape(r, 4, 4, 8).transpose(0, 2, 1, 3)
        return t.reshape(r, 4, P)

    w["a1_qkw"] = np.stack([spread(win[:, :128]), spread(win[:, 128:256])], 1)
    w["a1_qkb"] = np.stack([spread(bin_[:, :128])[0].T, spread(bin_[:, 128:256])[0].T], 1)[..., None]
    w["a1_vw"] = win[:, 256:]
    w["a1_vb"] = bin_[:, 256:]
    w["a1_ow"] = np.zeros((4, 32, 4, P), np.float32)
    w["a1_ow"][:, :8] = q("w_out").reshape(4, 4, 8, P).transpose(1, 2, 0, 3)
    w["a1_ow"] = w["a1_ow"].reshape(P, 4, P)
    w["a1_ob"] = q("b_out").reshape(P, 1)
    q = lambda k: a["L3_ffn_" + k]
    for l in range(2):
        m = q("wqkv")[l]
        w[f"l3{l}_qkw"] = m[:, :1024].reshape(P, 2, 2, 4, 64).transpose(0, 1, 3, 2, 4).reshape(P, 2, 4, P)
        w[f"l3{l}_vw"] = m[:, 1024:]
        w[f"l3{l}_ow"] = q("wo")[l].reshape(4, P, P).transpose(1, 0, 2)
        w[f"l3{l}_qks"] = np.stack([np.tile(q("q_scale")[l], 2), np.tile(q("k_scale")[l], 2)], 1)
    w["l3_w1"], w["l3_w2"] = q("w1"), q("w2")
    w["l3_b1"] = q("b1")[:, :, None]
    w["l3_col"] = np.stack([q("ln_g"), q("ln_b"), q("b2")], 2)


def attn_tables():
    f = np.float32
    i, j = np.arange(SEQ)[:, None], np.arange(SEQ)[None, :]

    def two_tiles(m):
        return np.moveaxis(np.concatenate([m[..., :P, :P], m[..., P:, :]], -1), -2, 0)

    slopes = np.array([2.0 ** (-0.5 * (h + 1)) for h in range(16)], f)
    alibi = np.where(j <= i, slopes[:, None, None] * (j - i).astype(f), f(MASKED)).astype(f)
    band = np.where((j <= i) & (i <= j + 64), f(0), f(MASKED)).astype(f)[None]
    half = np.arange(0, 64, 2, dtype=f)
    t = np.arange(SEQ, dtype=f)
    freqs = t[:, None] * (f(1) / f(10000) ** (half / f(64)))[None]
    freqs = np.concatenate([freqs, freqs], -1)
    base = (half + f(0.4 * 64)) / f(1.4 * 64)
    sc = base[None, :] ** ((t - SEQ // 2) / f(32))[:, None]
    sc = np.concatenate([sc, sc], -1)
    cos, sin = np.cos(freqs), np.sin(freqs)
    parts = [[f(8) * cos * sc, f(8) * sin * sc], [cos / sc, sin / sc]]
    trig = np.stack([np.stack([np.tile(m.T, (2, 1)) for m in r], 1) for r in parts], 1)
    rot = np.zeros((P, P), f)
    for b in (0, 64):
        for d in range(32):
            rot[b + 32 + d, b + d] = -1
            rot[b + d, b + 32 + d] = 1
    blk = np.kron(np.eye(2, dtype=f), np.ones((64, 64), f))
    return {"c_alibi": two_tiles(alibi), "c_band": two_tiles(band), "c_trig": trig.astype(f), "c_rot": rot, "c_blk": blk,
            "c_undo": np.full((P, 1), 12 * np.log(2.0), f)}


def permutation_scan(nc, x, z, w, C):
    NH, N = 4, 8
    NN = N * N
    NT = T // P
    M = NT * NH
    BH = BATCH * NH
    REC = N * (N + 1)
    STATE = N + 1
    md = nc.dram_tensor("p_records", (BATCH, NH, SEQ, REC), F32).ap()
    with ExitStack() as stage:
        sb, ps, sem = open_tools(stage, nc)
        soft = sb("p_soft", [P, M, NN])
        gates = sb("p_gates", [P, NT, 3, NH * N])

        with ExitStack() as mid:
            sb, ps, sem = open_tools(mid, nc)
            xn = sb("p_xn", [P, T])
            lnw = sb("p_ln", [P, 2])
            pw = sb("p_w", [P, 3 * NH * N + NH * NN])
            pb = sb("p_b", [P, 3 * NH * N + NH * NN])
            layernorm(nc, "L0_attn_ln", x, z, C, loads=[(lnw[:], w["l0_ln"]), (pw[:], w["l0_w"]), (pb[:], w["l0_b"])])
            layernorm(nc, "p_ln", z, xn, C, lnw[:, 0:1], lnw[:, 1:2])
            with ExitStack() as ctx:
                sb, ps, sem = open_tools(ctx, nc)
                xs = sb("p_xs", [P, 2, G])
                TG = G // P
                NG3 = 3 * NH * N
                p_ps = ps("p_ps", [P, 2, TG, 512])
                PE = Steps(ctx, nc, "p_pe", [("proj", j) for j in (0, 1)])
                VE = Steps(ctx, nc, "p_dve", [("bias", j) for j in (0, 1)])
                PO = Steps(ctx, nc, "p_pool", [("stage", j) for j in (0, 1)])
                block = ctx.enter_context(nc.Block())

                @block.gpsimd
                def _(pool):
                    PO.credit(pool)
                    with pool.Fori(0, NG // 2) as i:
                        for j in (0, 1):
                            pool.wait_ge(PE.sem, PE.at(i, ("proj", j), 1))
                            nc.gpsimd.tensor_copy(xs[:, j, :], xn[:, bass.ds(i * (2 * G) + j * G, G)])\
                                .then_inc(PO.sem, PO.step(("stage", j)))
                    PO.done()

                @block.tensor
                def _(pe):
                    PE.credit(pe)
                    with pe.Fori(0, NG // 2) as i:
                        for j in (0, 1):
                            pe.wait_ge(PO.sem, PO.at(i, ("stage", j)))
                            pe.wait_ge(VE.sem, VE.at(i, ("bias", j), 1))
                            for t in range(TG):
                                mm = nc.tensor.matmul(p_ps[:, j, t, 0:NG3 + NH * NN], xs[:, j, t * P:(t + 1) * P], pw[:],
                                                      start=True, stop=True)
                            mm.then_inc(PE.sem, PE.step(("proj", j)))
                    PE.done()

                @block.vector
                def _(dve):
                    VE.credit(dve)

                    def bias(lo, hi):
                        return pb[:, lo:hi].rearrange("p (t n) -> p t n", t=1).to_broadcast([P, TG, hi - lo])

                    with dve.Fori(0, NG // 2) as i:
                        for j in (0, 1):
                            dve.wait_ge(PE.sem, PE.at(i, ("proj", j)))
                            nc.vector.tensor_tensor(gates[:, bass.ds(i * (2 * TG) + j * TG, TG), :, :].rearrange("p t a n -> p t (a n)"),
                                                    p_ps[:, j, :, 0:NG3], bias(0, NG3), ALU.add)
                            nc.vector.tensor_tensor(soft[:, bass.ds(i * (2 * TG * NH) + j * (TG * NH), TG * NH), :]
                                                    .rearrange("p (t h) k -> p t (h k)", h=NH),
                                                    p_ps[:, j, :, NG3:NG3 + NH * NN], bias(NG3, NG3 + NH * NN), ALU.add)\
                                .then_inc(VE.sem, VE.step(("bias", j)))
                    VE.done()

        with ExitStack() as ctx:
            sb, ps, sem = open_tools(ctx, nc)
            MV = 56
            vec = sb("p_vec", [P, M, N])
            rows = sb("p_rows", [P, M, N])
            used = sb("p_used", [P, M, N])
            taken = sb("p_taken", [P, M, N])
            one = sb("p_one", [P, M])
            sel = sb("p_sel", [P, N, M, N])
            falling = sb("p_falling", [P, N])
            rec = sb("p_rec", [P, M, REC])
            prod = [sb("p_prod0", [P, M, NN])[:],
                    rec[:].rearrange("p m r -> p (m r)")[:, 0:M * NN].rearrange("p (m k) -> p m k", k=NN)]
            col = sb("p_col", [P, M, N])
            load_tiles(nc, "p2", [(falling[:], w["c_fall"])])
            vstep = sem("p_vstep")
            centred = sem("p_centred")
            expd = sem("p_expd")
            sigd = sem("p_sigd")
            picked = sem("p_picked")
            multiplied = sem("p_multiplied")
            inverted = sem("p_inverted")
            scaled = sem("p_scaled")
            summed = sem("p_summed")
            recorded = sem("p_recorded")
            stored = sem("p_stored")
            block = ctx.enter_context(nc.Block())
            by_row = lambda t: t[:].rearrange("p m (i j) -> p m i j", i=N)
            by_col = lambda t: t[:].rearrange("p m (i j) -> p m j i", i=N)
            wide = lambda t: t.rearrange("p m (i k) -> p m i k", k=1).to_broadcast([P, M, N, N])
            part = lambda v, lo, hi: v[:, lo:hi]
            wide1 = lambda t: t[:].rearrange("p (m k) -> p m k", k=1).to_broadcast([P, M, N])
            fall = falling[:].rearrange("p (m i) -> p m i", m=1).to_broadcast([P, M, N])

            @block.gpsimd
            def _(pool):
                for n in range(10):
                    view = part(by_col(soft) if n % 2 else by_row(soft), MV, M)
                    pool.wait_ge(inverted, n + 1)
                    nc.gpsimd.tensor_tensor(view, view, part(wide(vec[:]), MV, M), ALU.mult).then_inc(scaled, 1)
                for k in range(N):
                    pool.wait_ge(picked, k + 1)
                    if k >= 2:
                        pool.wait_ge(summed, k - 1)
                    nc.gpsimd.tensor_tensor(prod[k % 2].rearrange("p m (i j) -> p m i j", i=N), by_row(soft),
                                            wide(sel[:, k]), ALU.mult).then_inc(multiplied, 1)

            @block.scalar
            def _(act):
                nc.scalar.activation(gates[:, :, 0:2, :], gates[:, :, 0:2, :], ACT.Sigmoid).then_inc(sigd, 1)
                act.wait_ge(centred, 1)
                nc.scalar.activation(soft[:], soft[:], ACT.Exp).then_inc(expd, 1)

            @block.vector
            def _(dve):
                v = nc.vector
                done = [0]

                def then(ins):
                    done[0] += 1
                    ins.then_inc(vstep, 1)
                    dve.wait_ge(vstep, done[0])

                then(v.tensor_reduce(vec[:], by_row(soft), X, ALU.max))
                then(v.tensor_tensor(by_row(soft), by_row(soft), wide(vec[:]), ALU.subtract))
                then(v.tensor_reduce(vec[:], by_col(soft), X, ALU.max))
                v.tensor_tensor(by_col(soft), by_col(soft), wide(vec[:]), ALU.subtract).then_inc(centred, 1)
                dve.wait_ge(expd, 1)
                for n in range(10):
                    view = by_col(soft) if n % 2 else by_row(soft)
                    v.tensor_reduce(vec[:, :MV, :], part(view, 0, MV), X, ALU.add)
                    if n:
                        dve.wait_ge(scaled, n)
                    then(v.tensor_reduce(vec[:, MV:, :], part(view, MV, M), X, ALU.add))
                    v.reciprocal(vec[:, MV:, :], vec[:, MV:, :]).then_inc(inverted, 1)
                    then(v.reciprocal(vec[:, :MV, :], vec[:, :MV, :]))
                    then(v.tensor_tensor(part(view, 0, MV), part(view, 0, MV), part(wide(vec[:]), 0, MV), ALU.mult))
                dve.wait_ge(scaled, 10)

                then(v.tensor_reduce(vec[:], by_row(soft), X, ALU.max))
                for k in range(N):
                    then(v.tensor_reduce(one[:], vec[:], X, ALU.max))
                    then(v.tensor_tensor(rows[:], vec[:], wide1(one), ALU.is_equal))
                    then(v.tensor_tensor(rows[:], rows[:], fall, ALU.mult))
                    then(v.tensor_reduce(one[:], rows[:], X, ALU.max))
                    then(v.tensor_tensor(sel[:, k], fall, wide1(one), ALU.is_equal))
                    v.scalar_tensor_tensor(vec[:], sel[:, k], -4.0, vec[:], ALU.mult, ALU.add).then_inc(picked, 1)
                    dve.wait_ge(picked, k + 1)

                then(v.memset(used[:], 0.0))
                for k in range(N):
                    dve.wait_ge(multiplied, k + 1)
                    v.tensor_reduce(rows[:], prod[k % 2].rearrange("p m (i j) -> p m j i", i=N), X, ALU.add)\
                        .then_inc(summed, 1)
                    dve.wait_ge(summed, k + 1)
                    then(v.tensor_tensor(rows[:], rows[:], used[:], ALU.add))
                    then(v.tensor_reduce(one[:], rows[:], X, ALU.max))
                    then(v.tensor_tensor(rows[:], rows[:], wide1(one), ALU.is_equal))
                    then(v.tensor_tensor(rows[:], rows[:], fall, ALU.mult))
                    then(v.tensor_reduce(one[:], rows[:], X, ALU.max))
                    then(v.tensor_tensor(taken[:], fall, wide1(one), ALU.is_equal))
                    then(v.scalar_tensor_tensor(used[:], taken[:], -4.0, used[:], ALU.mult, ALU.add))
                    if k == 0:
                        then(v.tensor_tensor(col[:], sel[:, k], wide1(one), ALU.mult))
                    else:
                        then(v.tensor_tensor(taken[:], sel[:, k], wide1(one), ALU.mult))
                        then(v.tensor_tensor(col[:], col[:], taken[:], ALU.add))

                dve.wait_ge(sigd, 1)
                gv = lambda a: gates[:, :, a, :].rearrange("p t (h i) -> p t h i", h=NH)
                vt = lambda t: t[:].rearrange("p (t h) i -> p t h i", h=NH)
                then(v.tensor_scalar(vt(vec), gv(0), 2.0, -1.0, ALU.mult, ALU.add))
                then(v.tensor_tensor(vt(vec), vt(vec), gv(1), ALU.mult))
                then(v.tensor_scalar(vt(rows), gv(1), -1.0, 1.0, ALU.mult, ALU.add))
                then(v.tensor_tensor(vt(rows), vt(rows), gv(2), ALU.mult))
                body = rec[:].rearrange("p m (i q) -> p m i q", i=N)[:, :, :, 0:N]
                tail = rec[:].rearrange("p m (i q) -> p m i q", i=N)[:, :, :, N]
                fall_j = falling[:].rearrange("p (m i j) -> p m i j", m=1, i=1).to_broadcast([P, M, N, N])
                then(v.tensor_tensor(body, fall_j, wide(col[:]), ALU.is_equal))
                then(v.tensor_tensor(body, body, by_row(soft), ALU.add))
                then(v.tensor_tensor(body, body, by_row(soft), ALU.subtract))
                then(v.tensor_tensor(body, body, wide(vec[:]), ALU.mult))
                v.tensor_copy(tail, rows[:]).then_inc(recorded, 1)

            def store(eng, tiles):
                eng.wait_ge(recorded, 1)
                for t in tiles:
                    b, s = t // 2, t % 2 * P
                    eng.dma_start(md[b, :, s:s + P, :].rearrange("h s r -> s h r"), rec[:, t * NH:(t + 1) * NH, :])\
                        .then_inc(stored, 16)
                eng.wait_ge(stored, 16 * NT)

            @block.sync
            def _(sp):
                store(sp, range(NT))

    with ExitStack() as stage:
        sb, ps, sem = open_tools(stage, nc)
        SL = P // N
        NSH = SEQ // SL
        state = sb("p_state", [BH, SEQ + 1, STATE])
        ow = sb("p_ow", [P, SL, NH, P])
        ob = sb("p_ob", [P, 1])
        with ExitStack() as ctx:
            sb, ps, sem = open_tools(ctx, nc)
            steps = sb("p_steps", [BH, SEQ, REC])
            prod = sb("p_prod", [BH, REC])
            LOADS = 8
            UN = 8
            loaded = [sem(f"p_loaded{q}") for q in range(LOADS)]
            oload = sem("p_oload")
            VE = Steps(ctx, nc, "p_dve", [(s, k) for k in range(UN) for s in ("mult", "sum")])
            start = sem("p_start")
            block = ctx.enter_context(nc.Block())
            mdv = md.rearrange("b h s r -> (b h) s r")

            @block.sync
            def _(sp):
                for q in range(LOADS):
                    at = slice(q * SEQ // LOADS, (q + 1) * SEQ // LOADS)
                    sp.dma_start(steps[:, at, :], mdv[:, at, :]).then_inc(loaded[q], 16)
                sp.dma_start(ow[:], w["l0_ow"]).then_inc(oload, 16)
                sp.dma_start(ob[:], w["l0_ob"]).then_inc(oload, 16)
                sp.wait_ge(oload, 32)

            @block.vector
            def _(dve):
                VE.credit(dve)
                v = nc.vector
                v.memset(state[:], 1.0).then_inc(start, 1)
                dve.wait_ge(start, 1)
                v.memset(state[:, 0, 0:N], 0.0).then_inc(start, 1)
                dve.wait_ge(start, 2)
                for q in range(LOADS):
                    per = SEQ // LOADS // UN
                    dve.wait_ge(loaded[q], 16)
                    with dve.Fori(q * per, (q + 1) * per) as i:
                        for k in range(UN):
                            if k:
                                dve.wait_ge(VE.sem, VE.at(i, ("sum", k - 1)))
                            else:
                                dve.wait_ge(VE.sem, VE.at(i, ("sum", UN - 1), 1))
                            v.tensor_tensor(prod[:].rearrange("p (o i q) -> p o i q", o=1, i=N),
                                            steps[:, bass.ds(i * UN + k, 1), :].rearrange("p s (i q) -> p s i q", i=N),
                                            state[:, bass.ds(i * UN + k, 1), :].rearrange("p s (o q) -> p s o q", o=1)
                                            .to_broadcast([BH, 1, N, STATE]), ALU.mult)\
                                .then_inc(VE.sem, VE.step(("mult", k)))
                            dve.wait_ge(VE.sem, VE.at(i, ("mult", k)))
                            v.tensor_reduce(state[:, bass.ds(i * UN + k + 1, 1), 0:N],
                                            prod[:].rearrange("p (o i q) -> p o i q", o=1, i=N), X, ALU.add)\
                                .then_inc(VE.sem, VE.step(("sum", k)))
                    VE.done()
                    VE.said = 0

        with ExitStack() as ctx:
            sb, ps, sem = open_tools(ctx, nc)
            packed = sb("p_packed", [BH, SEQ * N])
            turned = sb("p_turned", [P, NH, BATCH, NSH])
            t_ps = ps("p_tps", [P, NSH, BH])
            o_ps = ps("p_ops", [P, 4, 512])
            s_packed = sem("p_s_packed")
            s_turned = sem("p_s_turned")
            s_copied = sem("p_s_copied")
            s_proj = sem("p_s_proj")
            s_added = sem("p_s_added")
            s_pre = sem("p_s_pre")
            block = ctx.enter_context(nc.Block())

            @block.scalar
            def _(act):
                nc.scalar.activation(packed[:].rearrange("p (s n) -> p s n", n=N), state[:, 1:, 0:N], ACT.Copy)\
                    .then_inc(s_packed, 1)
                act.wait_ge(s_turned, 1)
                for h in range(NH):
                    a = nc.scalar.activation(turned[:, h].rearrange("p b s -> p s b"),
                                             t_ps[:].rearrange("p s (b h) -> p h s b", h=NH)[:, h], ACT.Copy)
                a.then_inc(s_copied, 1)

            @block.tensor
            def _(pe):
                pe.wait_ge(s_packed, 1)
                for s in range(NSH):
                    mm = nc.tensor.transpose(t_ps[:, s, :], packed[:, s * P:(s + 1) * P], C.ident[0:BH, 0:BH])
                mm.then_inc(s_turned, 1)
                pe.wait_ge(s_copied, 1)
                for l in range(SL):
                    if l >= 4:
                        pe.wait_ge(s_added, l - 3)
                    for h in range(NH):
                        mm = nc.tensor.matmul(o_ps[:, l % 4, 0:BATCH * NSH], ow[:, l, h, :],
                                              turned[:, h].rearrange("p b s -> p (b s)"), start=h == 0, stop=h == NH - 1)
                    mm.then_inc(s_proj, 1)

            @block.vector
            def _(dve):
                nc.vector.scalar_tensor_tensor(x[:], z[:], ob[:], x[:], ALU.add, ALU.add).then_inc(s_pre, 1)
                dve.wait_ge(s_pre, 1)
                xv = x[:].rearrange("p (b s l) -> p b s l", b=BATCH, l=SL)
                for l in range(SL):
                    dve.wait_ge(s_proj, l + 1)
                    nc.vector.tensor_tensor(xv[:, :, :, l], xv[:, :, :, l],
                                            o_ps[:, l % 4, 0:BATCH * NSH].rearrange("p (b s) -> p b s", b=BATCH), ALU.add)\
                        .then_inc(s_added, 1)


def perm_layout(a, w):
    q = lambda k: a["L0_attn_" + k]
    w["l0_ln"] = np.stack([q("ln_w"), q("ln_b")], 1)
    w["l0_w"] = np.concatenate([q("sign_W"), q("gate_W"), q("in_W"), q("perm_W")], 1)
    b = np.concatenate([q("sign_b"), q("gate_b"), q("in_b"), q("perm_b")])
    w["l0_b"] = np.broadcast_to(b, (P, b.size))
    ow = np.zeros((16, 8, 16, 4, P), np.float32)
    for l in range(16):
        ow[l, :, l] = q("out_W").reshape(4, 8, P).transpose(1, 0, 2)
    w["l0_ow"] = ow.reshape(P, 16, 4, P)
    w["l0_ob"] = q("out_b").reshape(P, 1)


def perm_tables():
    return {"c_fall": np.broadcast_to(np.arange(8, 0, -1, dtype=np.float32), (P, 8))}


def more_layout(a, w):
    perm_layout(a, w)
    attn_layout(a, w)
    ffn_layout(a, w)
    mamba_layout(a, w)


def shape_tables():
    return {**selector_tables(), **ffn_tables(), **attn_tables(), **perm_tables()}


STAGE = {"L0_attn": permutation_scan, "L0_ffn": int8_swiglu, "L1_attn": alibi_attention, "L1_ffn": mx_linear,
         "L2_attn": mamba_layer, "L2_ffn": moe, "L3_attn": mamba_stack, "L3_ffn": local_transformer}
ALL_STAGES = tuple(STAGE)


class Tables:
    pass


def transformer_program(nc, w, out, stages=ALL_STAGES):
    with ExitStack() as ctx:
        sb, ps, sem = open_tools(ctx, nc)
        C = Tables()
        C.mean = sb("c_mean", [P, P])
        C.center = sb("c_center", [P, P])
        C.ident = sb("c_ident", [P, P])
        C.eps = sb("c_eps", [P, 1])
        C.one = sb("c_one", [P, 1])
        C.ones = sb("c_ones", [1, G])
        x = sb("x", [P, T])
        z = sb("z", [P, T])
        load_tiles(nc, "start", [(x[:], w["x"]), (C.mean[:], w["c_mean"]), (C.center[:], w["c_center"]), (C.ident[:], w["c_ident"]),
                                 (C.eps[:], w["c_eps"]), (C.one[:], w["c_one"]), (C.ones[:], w["c_ones"])])
        for s in stages:
            STAGE[s](nc, x, z, w, C)
        with ExitStack() as end:
            stored = end.enter_context(semaphore(nc, "stored"))
            block = end.enter_context(nc.Block())

            @block.sync
            def _(sp):
                sp.dma_start(out, x[:]).then_inc(stored, 16)
                sp.wait_ge(stored, 16)


def lay_out(inputs):
    a = {k: np.asarray(v) for k, v in inputs.items()}
    w = {"x": a["L0_attn_x"].reshape(T, P).T}
    for k, v in a.items():
        if k != "L0_attn_x":
            w[k] = v
    for k in ("L0_ffn_w_gate", "L0_ffn_w_up", "L0_ffn_w_down"):
        w[k] = a[k].T
    more_layout(a, w)
    w["c_mean"] = np.full((P, P), 1.0 / P, np.float32)
    w["c_center"] = np.eye(P, dtype=np.float32) - w["c_mean"]
    w["c_ident"] = np.eye(P, dtype=np.float32)
    w["c_eps"] = np.full((P, 1), EPS, np.float32)
    w["c_one"] = np.full((P, 1), 1.0, np.float32)
    w["c_ones"] = np.full((1, G), 1.0, np.float32)
    w.update(shape_tables())
    return {k: np.ascontiguousarray(v) for k, v in w.items()}


def build(nc, w, stages=None):
    args = {k: nc.dram_tensor(f"in_{k}", v.shape, mybir.dt.from_np(v.dtype), kind="ExternalInput").ap()
            for k, v in w.items()}
    out = nc.dram_tensor("out", (P, T), F32, kind="ExternalOutput").ap()
    transformer_program(nc, args, out, stages or ALL_STAGES)
    return {f"in_{k}": v for k, v in w.items()}


def kernel(**inputs):
    import concourse.bacc as bacc
    from concourse.bass_utils import run_bass_kernel_spmd

    nc = bacc.Bacc("TRN2", target_bir_lowering=False, num_devices=1)
    arrays = build(nc, lay_out(inputs))
    r = run_bass_kernel_spmd(nc, [arrays], core_ids=[0])
    return np.ascontiguousarray(r.results[0]["out"].T).reshape(BATCH, SEQ, P)
```
